# Optimizing a Trainium2 kernel written in Bass

```python
import numpy as np
import jax
import jax.numpy as jnp

def _softmax(x, axis=-1):
    return jax.nn.softmax(x, axis=axis)

def _gelu(x):
    return jax.nn.gelu(x, approximate=True)

def _silu(x):
    return jax.nn.silu(x)

def _sigmoid(x):
    return jax.nn.sigmoid(x)

def _layernorm(x, axis=-1, eps=1e-05):
    m = jnp.mean(x, axis=axis, keepdims=True)
    v = jnp.var(x, axis=axis, keepdims=True)
    return (x - m) / jnp.sqrt(v + eps)

def _scatter_add(tgt, idx, src, axis=0):
    return tgt.at[idx].add(src)

def _segment_sum(src, seg, n):
    return jax.ops.segment_sum(src, seg, n)
kernel_name = 'mk_recurrent_d2_jaxref_r8_4338ae'

def setup_inputs(seed: int=0):
    np.random.seed(seed)
    _w = jnp.asarray

    def _L0_attn_setup():
        import jax, jax.numpy as jnp
        import numpy as np
        L, E, H = (4, 128, 16)
        HD = E // H
        EPS_LN = 1e-05

        def _layernorm(x, w, b):
            m = jnp.mean(x, axis=-1, keepdims=True)
            v = jnp.mean((x - m) ** 2, axis=-1, keepdims=True)
            return (x - m) / jnp.sqrt(v + EPS_LN) * w + b

        def _to_quaternion(x):
            p1 = jnp.diff(x, axis=1, prepend=x[:, :1])
            p2 = jnp.roll(x, 1, axis=2)
            p3 = jnp.cos(x)
            return jnp.stack([x, p1, p2, p3], axis=-1)

        def _hamilton(a, b):
            a0, a1, a2, a3 = (a[..., 0], a[..., 1], a[..., 2], a[..., 3])
            b0, b1, b2, b3 = (b[..., 0], b[..., 1], b[..., 2], b[..., 3])
            return jnp.stack([a0 * b0 - a1 * b1 - a2 * b2 - a3 * b3, a0 * b1 + a1 * b0 + a2 * b3 - a3 * b2, a0 * b2 - a1 * b3 + a2 * b0 + a3 * b1, a0 * b3 + a1 * b2 - a2 * b1 + a3 * b0], axis=-1)

        def _spectral_filter(S):
            ks = jnp.fft.fftfreq(S).astype(jnp.float32)[:, None, None]
            kh = jnp.fft.fftfreq(H).astype(jnp.float32)[None, :, None]
            kd = jnp.fft.fftfreq(HD).astype(jnp.float32)[None, None, :]
            km = jnp.sqrt(ks ** 2 + kh ** 2 + kd ** 2 + 1e-10)
            f = jnp.exp(1j * jnp.arctan(jnp.log(km + 1e-10)))
            return f[None, :, :, :, None].astype(jnp.complex64)

        def _modulation(S):
            lam = jnp.arange(S, dtype=jnp.float32) / S
            t = jnp.arange(S, dtype=jnp.float32) * 0.1
            probe = jnp.sin(t + lam)
            phase = t - 2.0 * lam + 0.5 * lam ** 2
            return (probe * jnp.cos(phase))[None, :, None, None]

        def _attention(x, aw, ab, pw, pb):
            B, S, _ = x.shape
            qkv = (x @ aw + ab).reshape(B, S, H, 3 * HD)
            q, k, v = jnp.split(qkv, 3, axis=-1)
            qk = _hamilton(_to_quaternion(q), _to_quaternion(k))
            qkv_p = _hamilton(qk, _to_quaternion(v))
            f = jnp.fft.fftn(qkv_p.astype(jnp.complex64), axes=(-3, -2))
            out = jnp.fft.ifftn(f * _spectral_filter(S), axes=(-3, -2)).real
            a = out[..., 0] * (1.0 + 0.1 * _modulation(S))
            return a.reshape(B, S, E) @ pw + pb

        def _layer(x, p):
            ln1w, ln1b, aw, ab, pw, pb, ln2w, ln2b, fw, fb, mw, mb = p
            x = x + _attention(_layernorm(x, ln1w, ln1b), aw, ab, pw, pb)
            h = _layernorm(x, ln2w, ln2b)
            h = jax.nn.gelu(h @ fw + fb, approximate=False) @ mw + mb
            return x + h
        key = jax.random.key(seed)
        ks = jax.random.split(key, 6)
        s = 0.02
        return {'x': jax.random.normal(ks[0], (2, 256, E), jnp.float32), 'ln1_w': jnp.ones((L, E), jnp.float32), 'ln1_b': jnp.zeros((L, E), jnp.float32), 'attn_w': jax.random.normal(ks[1], (L, E, 3 * E), jnp.float32) * s, 'attn_b': jnp.zeros((L, 3 * E), jnp.float32), 'aproj_w': jax.random.normal(ks[2], (L, E, E), jnp.float32) * s, 'aproj_b': jnp.zeros((L, E), jnp.float32), 'ln2_w': jnp.ones((L, E), jnp.float32), 'ln2_b': jnp.zeros((L, E), jnp.float32), 'fc_w': jax.random.normal(ks[3], (L, E, 4 * E), jnp.float32) * s, 'fc_b': jnp.zeros((L, 4 * E), jnp.float32), 'mproj_w': jax.random.normal(ks[4], (L, 4 * E, E), jnp.float32) * s, 'mproj_b': jnp.zeros((L, E), jnp.float32)}
    _L0_attn_in = _L0_attn_setup()

    def _L0_ffn_setup():
        import jax, jax.numpy as jnp
        import numpy as np
        TOP_K = 2
        key = jax.random.key(seed)
        k0, k1, k2, k3, k4 = jax.random.split(key, 5)
        B, S, D, H, E = (4, 256, 128, 256, 8)
        x = jax.random.normal(k0, (B, S, D), dtype=jnp.float32)
        router_w = jax.random.normal(k1, (E, D), dtype=jnp.float32) * D ** (-0.5)
        w_gate = jax.random.normal(k2, (E, D, H), dtype=jnp.float32) * D ** (-0.5)
        w_up = jax.random.normal(k3, (E, D, H), dtype=jnp.float32) * D ** (-0.5)
        w_down = jax.random.normal(k4, (E, H, D), dtype=jnp.float32) * H ** (-0.5)
        return {'x': x, 'router_w': router_w, 'w_gate': w_gate, 'w_up': w_up, 'w_down': w_down}
    _L0_ffn_in = _L0_ffn_setup()

    def _L1_attn_setup():
        import jax, jax.numpy as jnp
        import numpy as np
        HEADS = 16
        DIM_HEAD = 64
        WINDOW = 128
        LOOK_BACKWARD = 1
        LOOK_FORWARD = 0
        THETA = 10000.0
        PAD_VALUE = -1

        def look_around(x, backward, forward, pad_value, axis):
            w = x.shape[axis]
            size = backward + forward + 1
            pads = [(0, 0)] * x.ndim
            pads[axis] = (backward, forward)
            p = jnp.pad(x, pads, constant_values=pad_value)
            segs = [jax.lax.slice_in_dim(p, s, s + w, axis=axis) for s in range(size)]
            return jnp.concatenate(segs, axis=axis + 1)

        def rotate_half(t):
            t1, t2 = jnp.split(t, 2, axis=-1)
            return jnp.concatenate([-t2, t1], axis=-1)
        key = jax.random.key(seed)
        k1, k2, k3 = jax.random.split(key, 3)
        dim = 128
        x = jax.random.normal(k1, (4, 512, dim), dtype=jnp.float32)
        W_qkv = jax.random.normal(k2, (dim, 3 * HEADS * DIM_HEAD), dtype=jnp.float32) * dim ** (-0.5)
        W_out = jax.random.normal(k3, (HEADS * DIM_HEAD, dim), dtype=jnp.float32) * (HEADS * DIM_HEAD) ** (-0.5)
        return {'x': x, 'W_qkv': W_qkv, 'W_out': W_out}
    _L1_attn_in = _L1_attn_setup()

    def _L1_ffn_setup():
        import jax, jax.numpy as jnp
        import numpy as np
        from jax import lax
        B, S, H = (2, 128, 128)
        I = 64
        E = 32
        TOP_K = 4
        N_GROUP = 4
        TOPK_GROUP = 2
        SCALE = 2.5
        N_SHARED = 2
        SH_I = I * N_SHARED

        def _route(tokens, router_weight, router_bias):
            logits = tokens.astype(jnp.float32) @ router_weight.astype(jnp.float32).T
            scores = jax.nn.sigmoid(logits)
            sfc = scores + router_bias[None, :]
            T = tokens.shape[0]
            grp = sfc.reshape(T, N_GROUP, E // N_GROUP)
            group_scores = lax.top_k(grp, 2)[0].sum(-1)
            _, gidx = lax.top_k(group_scores, TOPK_GROUP)
            gmask = jax.nn.one_hot(gidx, N_GROUP, dtype=sfc.dtype).sum(1)
            smask = jnp.broadcast_to(gmask[:, :, None], (T, N_GROUP, E // N_GROUP)).reshape(T, E)
            tmp = jnp.where(smask > 0, sfc, 0.0)
            _, topk_idx = lax.top_k(tmp, TOP_K)
            topk_w = jnp.take_along_axis(scores, topk_idx, axis=1)
            topk_w = topk_w / (topk_w.sum(-1, keepdims=True) + 1e-20)
            topk_w = topk_w * SCALE
            return (topk_idx, topk_w)
        key = jax.random.key(seed)
        ks = jax.random.split(key, 10)
        std = 0.02
        return {'hidden_states': jax.random.normal(ks[0], (B, S, H), jnp.float32), 'router_weight': jax.random.normal(ks[1], (E, H), jnp.float32) * std, 'router_bias': jnp.zeros((E,), jnp.float32), 'gate_w': jax.random.normal(ks[2], (E, I, H), jnp.float32) * std, 'up_w': jax.random.normal(ks[3], (E, I, H), jnp.float32) * std, 'down_w': jax.random.normal(ks[4], (E, H, I), jnp.float32) * std, 'shared_gate_w': jax.random.normal(ks[5], (SH_I, H), jnp.float32) * std, 'shared_up_w': jax.random.normal(ks[6], (SH_I, H), jnp.float32) * std, 'shared_down_w': jax.random.normal(ks[7], (H, SH_I), jnp.float32) * std}
    _L1_ffn_in = _L1_ffn_setup()
    _d = {'L0_attn_x': _L0_attn_in['x'], 'L0_attn_ln1_w': _L0_attn_in['ln1_w'], 'L0_attn_ln1_b': _L0_attn_in['ln1_b'], 'L0_attn_attn_w': _L0_attn_in['attn_w'], 'L0_attn_attn_b': _L0_attn_in['attn_b'], 'L0_attn_aproj_w': _L0_attn_in['aproj_w'], 'L0_attn_aproj_b': _L0_attn_in['aproj_b'], 'L0_attn_ln2_w': _L0_attn_in['ln2_w'], 'L0_attn_ln2_b': _L0_attn_in['ln2_b'], 'L0_attn_fc_w': _L0_attn_in['fc_w'], 'L0_attn_fc_b': _L0_attn_in['fc_b'], 'L0_attn_mproj_w': _L0_attn_in['mproj_w'], 'L0_attn_mproj_b': _L0_attn_in['mproj_b'], 'L0_ffn_router_w': _L0_ffn_in['router_w'], 'L0_ffn_w_gate': _L0_ffn_in['w_gate'], 'L0_ffn_w_up': _L0_ffn_in['w_up'], 'L0_ffn_w_down': _L0_ffn_in['w_down'], 'L1_attn_W_qkv': _L1_attn_in['W_qkv'], 'L1_attn_W_out': _L1_attn_in['W_out'], 'L1_ffn_router_weight': _L1_ffn_in['router_weight'], 'L1_ffn_router_bias': _L1_ffn_in['router_bias'], 'L1_ffn_gate_w': _L1_ffn_in['gate_w'], 'L1_ffn_up_w': _L1_ffn_in['up_w'], 'L1_ffn_down_w': _L1_ffn_in['down_w'], 'L1_ffn_shared_gate_w': _L1_ffn_in['shared_gate_w'], 'L1_ffn_shared_up_w': _L1_ffn_in['shared_up_w'], 'L1_ffn_shared_down_w': _L1_ffn_in['shared_down_w']}
    _x0 = _d['L0_attn_x']
    _d['L0_attn_x'] = jax.random.normal(jax.random.fold_in(jax.random.key(seed), 1), (16, 512, 128), dtype=_x0.dtype)
    del _x0
    return _d

def reference(L0_attn_x, L0_attn_ln1_w, L0_attn_ln1_b, L0_attn_attn_w, L0_attn_attn_b, L0_attn_aproj_w, L0_attn_aproj_b, L0_attn_ln2_w, L0_attn_ln2_b, L0_attn_fc_w, L0_attn_fc_b, L0_attn_mproj_w, L0_attn_mproj_b, L0_ffn_router_w, L0_ffn_w_gate, L0_ffn_w_up, L0_ffn_w_down, L1_attn_W_qkv, L1_attn_W_out, L1_ffn_router_weight, L1_ffn_router_bias, L1_ffn_gate_w, L1_ffn_up_w, L1_ffn_down_w, L1_ffn_shared_gate_w, L1_ffn_shared_up_w, L1_ffn_shared_down_w):

    def _L0_attn_ref(x, ln1_w, ln1_b, attn_w, attn_b, aproj_w, aproj_b, ln2_w, ln2_b, fc_w, fc_b, mproj_w, mproj_b):
        import jax, jax.numpy as jnp
        import numpy as np
        L, E, H = (4, 128, 16)
        HD = E // H
        EPS_LN = 1e-05

        def _layernorm(x, w, b):
            m = jnp.mean(x, axis=-1, keepdims=True)
            v = jnp.mean((x - m) ** 2, axis=-1, keepdims=True)
            return (x - m) / jnp.sqrt(v + EPS_LN) * w + b

        def _to_quaternion(x):
            p1 = jnp.diff(x, axis=1, prepend=x[:, :1])
            p2 = jnp.roll(x, 1, axis=2)
            p3 = jnp.cos(x)
            return jnp.stack([x, p1, p2, p3], axis=-1)

        def _hamilton(a, b):
            a0, a1, a2, a3 = (a[..., 0], a[..., 1], a[..., 2], a[..., 3])
            b0, b1, b2, b3 = (b[..., 0], b[..., 1], b[..., 2], b[..., 3])
            return jnp.stack([a0 * b0 - a1 * b1 - a2 * b2 - a3 * b3, a0 * b1 + a1 * b0 + a2 * b3 - a3 * b2, a0 * b2 - a1 * b3 + a2 * b0 + a3 * b1, a0 * b3 + a1 * b2 - a2 * b1 + a3 * b0], axis=-1)

        def _spectral_filter(S):
            ks = jnp.fft.fftfreq(S).astype(jnp.float32)[:, None, None]
            kh = jnp.fft.fftfreq(H).astype(jnp.float32)[None, :, None]
            kd = jnp.fft.fftfreq(HD).astype(jnp.float32)[None, None, :]
            km = jnp.sqrt(ks ** 2 + kh ** 2 + kd ** 2 + 1e-10)
            f = jnp.exp(1j * jnp.arctan(jnp.log(km + 1e-10)))
            return f[None, :, :, :, None].astype(jnp.complex64)

        def _modulation(S):
            lam = jnp.arange(S, dtype=jnp.float32) / S
            t = jnp.arange(S, dtype=jnp.float32) * 0.1
            probe = jnp.sin(t + lam)
            phase = t - 2.0 * lam + 0.5 * lam ** 2
            return (probe * jnp.cos(phase))[None, :, None, None]

        def _attention(x, aw, ab, pw, pb):
            B, S, _ = x.shape
            qkv = (x @ aw + ab).reshape(B, S, H, 3 * HD)
            q, k, v = jnp.split(qkv, 3, axis=-1)
            qk = _hamilton(_to_quaternion(q), _to_quaternion(k))
            qkv_p = _hamilton(qk, _to_quaternion(v))
            f = jnp.fft.fftn(qkv_p.astype(jnp.complex64), axes=(-3, -2))
            out = jnp.fft.ifftn(f * _spectral_filter(S), axes=(-3, -2)).real
            a = out[..., 0] * (1.0 + 0.1 * _modulation(S))
            return a.reshape(B, S, E) @ pw + pb

        def _layer(x, p):
            ln1w, ln1b, aw, ab, pw, pb, ln2w, ln2b, fw, fb, mw, mb = p
            x = x + _attention(_layernorm(x, ln1w, ln1b), aw, ab, pw, pb)
            h = _layernorm(x, ln2w, ln2b)
            h = jax.nn.gelu(h @ fw + fb, approximate=False) @ mw + mb
            return x + h
        for i in range(L):
            x = _layer(x, (ln1_w[i], ln1_b[i], attn_w[i], attn_b[i], aproj_w[i], aproj_b[i], ln2_w[i], ln2_b[i], fc_w[i], fc_b[i], mproj_w[i], mproj_b[i]))
        return x

    def _L0_ffn_ref(x, router_w, w_gate, w_up, w_down):
        import jax, jax.numpy as jnp
        import numpy as np
        TOP_K = 2
        B, S, D = x.shape
        E = router_w.shape[0]
        xt = x.reshape(-1, D)
        logits = xt @ router_w.T
        topk_vals, topk_idx = jax.lax.top_k(logits, TOP_K)
        g = jax.nn.sigmoid(topk_vals)
        g = g / (g.sum(axis=-1, keepdims=True) + 1e-10)
        out = jnp.zeros_like(xt)
        for e in range(E):
            ge = jnp.sum(jnp.where(topk_idx == e, g, jnp.zeros_like(g)), axis=-1)
            h = jax.nn.silu(xt @ w_gate[e]) * (xt @ w_up[e])
            out = out + ge[:, None] * (h @ w_down[e])
        return out.reshape(B, S, D)

    def _L1_attn_ref(x, W_qkv, W_out):
        import jax, jax.numpy as jnp
        import numpy as np
        HEADS = 16
        DIM_HEAD = 64
        WINDOW = 128
        LOOK_BACKWARD = 1
        LOOK_FORWARD = 0
        THETA = 10000.0
        PAD_VALUE = -1

        def look_around(x, backward, forward, pad_value, axis):
            w = x.shape[axis]
            size = backward + forward + 1
            pads = [(0, 0)] * x.ndim
            pads[axis] = (backward, forward)
            p = jnp.pad(x, pads, constant_values=pad_value)
            segs = [jax.lax.slice_in_dim(p, s, s + w, axis=axis) for s in range(size)]
            return jnp.concatenate(segs, axis=axis + 1)

        def rotate_half(t):
            t1, t2 = jnp.split(t, 2, axis=-1)
            return jnp.concatenate([-t2, t1], axis=-1)
        b, n, dim = x.shape
        h, dh, ws = (HEADS, DIM_HEAD, WINDOW)
        w = n // ws
        j = ws * (LOOK_BACKWARD + LOOK_FORWARD + 1)
        qkv = x @ W_qkv
        q, k, v = jnp.split(qkv, 3, axis=-1)

        def to_bhwnd(t):
            return t.reshape(b, n, h, dh).transpose(0, 2, 1, 3).reshape(b, h, w, ws, dh)
        bq = to_bhwnd(q) * dh ** (-0.5)
        bk = look_around(to_bhwnd(k), LOOK_BACKWARD, LOOK_FORWARD, float(PAD_VALUE), axis=2)
        bv = look_around(to_bhwnd(v), LOOK_BACKWARD, LOOK_FORWARD, float(PAD_VALUE), axis=2)
        inv_freq = 1.0 / THETA ** (jnp.arange(0, dh, 2, dtype=jnp.float32) / dh)
        t_pos = jnp.arange(j, dtype=jnp.float32)
        freqs = t_pos[:, None] * inv_freq[None, :]
        freqs = jnp.concatenate([freqs, freqs], axis=-1)
        q_freqs = freqs[-ws:]
        bq = bq * jnp.cos(q_freqs) + rotate_half(bq) * jnp.sin(q_freqs)
        bk = bk * jnp.cos(freqs) + rotate_half(bk) * jnp.sin(freqs)
        sim = jnp.einsum('bhwid,bhwjd->bhwij', bq, bk)
        seq = jnp.arange(n).reshape(w, ws)
        bq_t = seq[:, :, None]
        bq_k = look_around(seq[None], LOOK_BACKWARD, LOOK_FORWARD, PAD_VALUE, axis=1)[0]
        bq_k = bq_k[:, None, :]
        pad_mask = bq_k == PAD_VALUE
        causal_mask = (bq_t < bq_k) | (bq_t > bq_k + ws * LOOK_BACKWARD)
        mask = causal_mask | pad_mask
        mask_value = -jnp.finfo(sim.dtype).max
        sim = jnp.where(mask, mask_value, sim)
        attn = jax.nn.softmax(sim, axis=-1)
        out = jnp.einsum('bhwij,bhwjd->bhwid', attn, bv)
        out = out.reshape(b, h, n, dh).transpose(0, 2, 1, 3).reshape(b, n, h * dh)
        return out @ W_out

    def _L1_ffn_ref(hidden_states, router_weight, router_bias, gate_w, up_w, down_w, shared_gate_w, shared_up_w, shared_down_w):
        import jax, jax.numpy as jnp
        import numpy as np
        from jax import lax
        B, S, H = (2, 128, 128)
        I = 64
        E = 32
        TOP_K = 4
        N_GROUP = 4
        TOPK_GROUP = 2
        SCALE = 2.5
        N_SHARED = 2
        SH_I = I * N_SHARED

        def _route(tokens, router_weight, router_bias):
            logits = tokens.astype(jnp.float32) @ router_weight.astype(jnp.float32).T
            scores = jax.nn.sigmoid(logits)
            sfc = scores + router_bias[None, :]
            T = tokens.shape[0]
            grp = sfc.reshape(T, N_GROUP, E // N_GROUP)
            group_scores = lax.top_k(grp, 2)[0].sum(-1)
            _, gidx = lax.top_k(group_scores, TOPK_GROUP)
            gmask = jax.nn.one_hot(gidx, N_GROUP, dtype=sfc.dtype).sum(1)
            smask = jnp.broadcast_to(gmask[:, :, None], (T, N_GROUP, E // N_GROUP)).reshape(T, E)
            tmp = jnp.where(smask > 0, sfc, 0.0)
            _, topk_idx = lax.top_k(tmp, TOP_K)
            topk_w = jnp.take_along_axis(scores, topk_idx, axis=1)
            topk_w = topk_w / (topk_w.sum(-1, keepdims=True) + 1e-20)
            topk_w = topk_w * SCALE
            return (topk_idx, topk_w)
        tokens = hidden_states.reshape(-1, H)
        topk_idx, topk_w = _route(tokens, router_weight, router_bias)
        gate_vals = jax.nn.silu(jnp.einsum('th,eih->tei', tokens, gate_w))
        up_vals = jnp.einsum('th,eih->tei', tokens, up_w)
        hidden_vals = gate_vals * up_vals
        expert_out = jnp.einsum('tei,ehi->teh', hidden_vals, down_w)
        sel = jnp.take_along_axis(expert_out, topk_idx[:, :, None], axis=1)
        mixed = (sel * topk_w[:, :, None].astype(sel.dtype)).sum(1)
        mixed = mixed.reshape(hidden_states.shape)
        sg = jax.nn.silu(jnp.einsum('bsh,ih->bsi', hidden_states, shared_gate_w))
        su = jnp.einsum('bsh,ih->bsi', hidden_states, shared_up_w)
        shared = jnp.einsum('bsi,hi->bsh', sg * su, shared_down_w)
        return mixed + shared
    x = L0_attn_x
    xn = _layernorm(x, axis=-1)
    s = _L0_attn_ref(xn, L0_attn_ln1_w, L0_attn_ln1_b, L0_attn_attn_w, L0_attn_attn_b, L0_attn_aproj_w, L0_attn_aproj_b, L0_attn_ln2_w, L0_attn_ln2_b, L0_attn_fc_w, L0_attn_fc_b, L0_attn_mproj_w, L0_attn_mproj_b)
    g = _silu(_L0_ffn_ref(xn, L0_ffn_router_w, L0_ffn_w_gate, L0_ffn_w_up, L0_ffn_w_down))
    x = x + s * g
    xn = _layernorm(x, axis=-1)
    s = _L1_attn_ref(xn, L1_attn_W_qkv, L1_attn_W_out)
    g = _silu(_L1_ffn_ref(xn, L1_ffn_router_weight, L1_ffn_router_bias, L1_ffn_gate_w, L1_ffn_up_w, L1_ffn_down_w, L1_ffn_shared_gate_w, L1_ffn_shared_up_w, L1_ffn_shared_down_w))
    x = x + s * g
    return x

_drawn_inputs = setup_inputs


def setup_inputs(seed=0):
    import zlib

    import numpy as np

    out = dict(_drawn_inputs(seed))
    spreads = {'L0_attn_ln1_w': (1.0, 0.6),
     'L0_attn_ln1_b': (0.0, 0.8),
     'L0_attn_attn_b': (0.0, 0.524),
     'L0_attn_aproj_b': (0.0, 0.1),
     'L0_attn_ln2_w': (1.0, 0.6),
     'L0_attn_ln2_b': (0.0, 0.8),
     'L0_attn_fc_b': (0.0, 0.778),
     'L0_attn_mproj_b': (0.0, 0.1),
     'L1_ffn_router_bias': (0.0, 0.8)}
    factors = {'L1_attn_W_qkv': 8.0,
     'L1_attn_W_out': 8.0,
     'L1_ffn_router_weight': 8.0,
     'L1_ffn_gate_w': 8.0,
     'L1_ffn_up_w': 8.0,
     'L1_ffn_down_w': 8.0,
     'L1_ffn_shared_gate_w': 8.0,
     'L1_ffn_shared_up_w': 8.0,
     'L1_ffn_shared_down_w': 8.0}
    for name, (base, spread) in spreads.items():
        noise = np.random.default_rng([zlib.crc32(name.encode()), seed]).standard_normal(out[name].shape)
        drawn = base * np.exp(spread * noise) if base else spread * noise
        out[name] = jnp.asarray(drawn.astype(out[name].dtype))
    for name, factor in factors.items():
        out[name] = (out[name] * factor).astype(out[name].dtype)
    return out
```

```python
import math
from contextlib import ExitStack

import numpy as np
import concourse.bass as bass
from concourse import mybir

NB, S, D = 16, 512, 128
P = 128
NT = S // P
L, H = 4, 16
HD = D // H
FC = 4
E0, H0, K0 = 8, 256, 2
HALF0 = H0 // P
E1, I1 = 32, 64
PAIR1 = E1 * I1 // P
GROUPS, TOPG, TOPK1, SCALE1 = 4, 2, 4, 2.5
EG = E1 // GROUPS
AH, DH, WIN = 16, 64, 128
HP = AH // 2
NW = S // WIN
INNER = AH * DH
PARTS = 3
EPS = 1e-5
ROUND = 1.5 * 2.0 ** 23
TWO_PI = 2.0 * math.pi
MASKED = -1e30

SLOTS = 23
HAM0 = 4
STEP_A = {0: "ln1_T", 1: "q", 2: "k", 3: "v", 13: "hart", 14: "proj", 15: "proj_T", 16: "ln2_T",
          17: "fc0", 18: "fc1", 19: "fc2", 20: "fc3", 21: "mproj", 22: "mproj_T"}
PREP = {5: "prep_T", 7: "route0", 10: "gates0_T"}
UNIT_SLOTS = (0, 3, 4, 5, 6, 8, 9, 14, 21)
UNITS0, UNITS1 = E0 * HALF0, PAIR1 + 1
UNITS = UNITS0 + UNITS1


def fills_of_a():
    out = []
    for l in range(L):
        for s in range(SLOTS):
            if s in STEP_A:
                out.append((STEP_A[s], l))
            if l == L - 1 and s in PREP:
                out.append((PREP[s], 0))
    return out + [("gate_T", 0)]


FILL = {name: n for n, name in enumerate(fills_of_a())}
PREP_FILL = {("prep_T", 0): 0, ("route0", 0): 1, ("gates0_T", 0): 2}
NFILL, NPREP = len(FILL), len(PREP_FILL)
LN_ORDER = [(k, l) for l in range(L) for k in (("ln1", "prep", "ln2") if l == L - 1 else ("ln1", "ln2"))]
LN_AT = {name: n for n, name in enumerate(LN_ORDER)}


def steps_in(l, s):
    p0, p1, p2 = 2 * l, 2 * l + 1, 2 * l + 2
    last = p2 >= HP
    table = {1: [("S", p0, 0)], 2: [("S", p0, 1)], 3: [("PT", p0, 0)], 4: [("q", p1)], 5: [("O", p0, 0)],
             6: [("PT", p0, 1)], 7: [("k", p1)], 8: [("O", p0, 1)], 9: [("OT", p0), ("V", p1)],
             10: [("S", p1, 0)], 11: [("S", p1, 1)], 12: [("PT", p1, 0)],
             13: [] if last else [("q", p2)], 14: [("O", p1, 0)], 15: [("PT", p1, 1)],
             16: [] if last else [("k", p2)], 17: [("O", p1, 1)],
             18: [("OT", p1)] + ([] if last else [("V", p2)]), 20: [("out", l)]}
    if l == 0:
        table[22] = [("gates1_T",)]
    return table.get(s, [])


FIRST_STEPS = [("xn1_T",), ("route1",), ("q", 0), ("k", 0), ("V", 0)]
STEPS = FIRST_STEPS + [t for l in range(L) for s in range(SLOTS) for t in steps_in(l, s)] + [("final_T",)]
STEP_AT = {t: n for n, t in enumerate(STEPS)}
STEPS_OF = [len(STEPS[0::2]), len(STEPS[1::2])]
ROPE_ORDER = [t for t in STEPS if t[0] in "qk"]
HAM_OPS = 20
R0_STEPS, R0_TOP, R1_STEPS = 14, 1, 27
PREP_BANKS = 2 + 3 * (PAIR1 // 4) + 3


def program(nc, x, ln1_w, ln1_b, attn_w, attn_b, aproj_w, aproj_b, ln2_w, ln2_b, fc_w, fc_b, mproj_w, mproj_b,
            router_w, w_gate, w_up, w_down, w_qkv, w_out, route_w1, route_b1, gate_w1, up_w1, down_w1,
            sh_gate, sh_up, sh_down, c_ident, c_identb, c_hart, c_cmod, c_cos, c_sin, c_mask, c_sel0, c_sel1,
            c_iota, c_ltri, out):
    fp32, bf16, u32 = mybir.dt.float32, mybir.dt.bfloat16, mybir.dt.uint32
    ALU, ACT, AX = mybir.AluOpType, mybir.ActivationFunctionType, mybir.AxisListType
    ctx = ExitStack()
    with ctx:
        def sb(name, shape, dt=fp32):
            return ctx.enter_context(nc.sbuf_tensor(name, shape, dt))

        def sem(name):
            return ctx.enter_context(nc.semaphore(name))

        w_att = sb("w_att", [P, L, 3, D])
        w_hp = sb("w_hp", [P, L, D])
        w_fc = sb("w_fc", [P, L, FC * D])
        w_mp = sb("w_mp", [P, L, FC, D])
        NCOL = 4 + 3 + FC + 2
        LN1W, LN1B, LN2W, LN2B, AB, FB, PB, MB = 0, 1, 2, 3, 4, 7, 7 + FC, 8 + FC
        cols = sb("cols", [P, NCOL, L])
        w_g0 = sb("w_g0", [P, E0, H0])
        w_u0 = sb("w_u0", [P, E0, H0])
        w_d0 = sb("w_d0", [P, E0, HALF0, D])
        w_r = sb("w_r", [P, E0 + E1])
        w_r0, w_r1 = w_r[:, 0:E0], w_r[:, E0:E0 + E1]
        w_a1 = sb("w_a1", [P, 3 * INNER])
        w_rot = sb("w_rot", [P, 2 * INNER])
        w_o1 = sb("w_o1", [P, HP, D])
        w_g1 = sb("w_g1", [P, PAIR1 + 1, P])
        w_u1 = sb("w_u1", [P, PAIR1 + 1, P])
        w_d1 = sb("w_d1", [P, PAIR1 + 1, D])
        rbias = sb("rbias", [P, E1])
        ident = sb("ident", [P, P])
        identb = sb("identb", [P, P], bf16)
        cmod = sb("cmod", [P, S])
        cosT = sb("cosT", [P, S])
        sinT = sb("sinT", [P, S])
        maskb = sb("maskb", [P, 6 * WIN], bf16)
        sel0 = sb("sel0", [PARTS * E0, E0, P], bf16)
        sel1 = sb("sel1", [PARTS * E1, PAIR1, P], bf16)
        iota = sb("iota", [P, E1])
        ltri = sb("ltri", [P, GROUPS, GROUPS])
        nhalf = sb("nhalf", [P, NT])
        epsT = sb("epsT", [P, NT])
        scratch = sb("scratch", [P, 1])
        hpi = sb("hpi", [P, 1])
        x_ld = sb("x_ld", [P, NT, D])
        xn = sb("xn", [P, NT, D])
        xr = sb("xr", [P, NT, D])
        xn_f = sb("xn_f", [P, S])
        gates0 = sb("gates0", [PARTS * E0, S], bf16)
        comps = sb("comps", [P, 3, 4, S])
        acc = sb("acc", [P, 4, S])
        tmp = sb("tmp", [P, 2, S])
        gate_f = sb("gate_f", [P, S])
        z, zc, pfm, xf = acc[:, 0, :], acc[:, 1, :], acc[:, 2, :], acc[:, 3, :]
        turns = acc[:, 0:3, :]
        hid = acc
        ln_hat = tmp[:, 0, :].rearrange("p (t d) -> p t d", t=NT)
        xmul = tmp[:, 1, :].rearrange("p (t d) -> p t d", t=NT)
        stA, mvA = sb("stA", [P, NT, 6]), sb("mvA", [P, NT, 2])
        veA, rsA = sb("veA", [P, NT]), sb("rsA", [P, NT])
        r0_lg = sb("r0_lg", [P, NT, E0])
        r0_top = sb("r0_top", [P, NT, 8])
        r0_idx = sb("r0_idx", [P, NT, 8], u32)
        r0_idf = sb("r0_idf", [P, NT, 8])
        r0_sg = sb("r0_sg", [P, NT, K0])
        r0_sum = sb("r0_sum", [P, NT])
        r0_hit = sb("r0_hit", [P, NT, K0, E0])
        r0_g = sb("r0_g", [P, NT, E0])
        r0_parts = sb("r0_parts", [P, NT, PARTS, E0], bf16)
        x1 = sb("x1", [P, NT, D])
        x1n_f = sb("x1n_f", [P, S])
        Q = sb("Q", [P, S])
        Kk = sb("Kk", [P, WIN + S])
        rot = sb("rot", [P, S])
        V = sb("V", [P, 1 + NW, P])
        probs = sb("probs", [P, 2, NW, 2 * WIN])
        probsT = sb("probsT", [P, 2, 4 * WIN])
        O = sb("O", [P, NW, P])
        OT = sb("OT", [P, 2, S])
        y = sb("y", [P, S])
        nmax = sb("nmax", [P, 2, NW])
        rsum = sb("rsum", [P, NW, 2])
        rinv = sb("rinv", [P, NW, 2])
        s_h = sb("s_h", [P, S])
        ge = sb("ge", [P, S])
        hu = sb("hu", [P, S])
        gate1_f = sb("gate1_f", [P, S])
        gates1 = sb("gates1", [PARTS * E1, S], bf16)
        x1n = rot[:, :].rearrange("p (t d) -> p t d", t=NT)
        y_out = O
        stB, mvB = sb("stB", [P, NT, 6]), sb("mvB", [P, NT, 2])
        veB, rsB = sb("veB", [P, NT]), sb("rsB", [P, NT])
        r1_s = sb("r1_s", [P, NT, E1])
        r1_c = sb("r1_c", [P, NT, E1])
        r1_m8 = sb("r1_m8", [P, NT, GROUPS, 8])
        r1_gs = sb("r1_gs", [P, NT, GROUPS])
        r1_gt = sb("r1_gt", [P, NT, GROUPS, GROUPS])
        r1_eq = sb("r1_eq", [P, NT, GROUPS, GROUPS])
        r1_top = sb("r1_top", [P, NT, 8])
        r1_idx = sb("r1_idx", [P, NT, 8], u32)
        r1_idf = sb("r1_idf", [P, NT, 8])
        r1_hit = y[:, :].rearrange("p (t k e) -> p t k e", t=NT, k=TOPK1)
        r1_sum = sb("r1_sum", [P, NT])
        r1_parts = sb("r1_parts", [P, NT, PARTS, E1], bf16)

        bA = ctx.enter_context(nc.psum_tensor("bA", [P, S], fp32))
        bT = [[ctx.enter_context(nc.psum_tensor(f"bT{i}{j}", [P, S], fp32)) for j in range(2)] for i in range(2)]
        bG = ctx.enter_context(nc.psum_tensor("bG", [P, S], fp32))
        bU = ctx.enter_context(nc.psum_tensor("bU", [P, S], fp32))
        bC = ctx.enter_context(nc.psum_tensor("bC", [P, S], fp32))
        banks = [bA, bT[0][0], bT[0][1], bT[1][0], bT[1][1], bG, bU]

        st_att = comps[:, 0, 0:3, :].rearrange("p a n -> p (a n)").rearrange("p (l n) -> p l n", l=L)
        st_par = comps[0:L, 0, 3, :]
        st_par2 = comps[0:L, 1, 0:3, :].rearrange("p a n -> p (a n)")
        st_g = probs[:, :, :, :].rearrange("p a b n -> p (a b n)").rearrange("p (j n) -> p j n", n=P)
        st_u = acc[:, :, :].rearrange("p a n -> p (a n)").rearrange("p (j n) -> p j n", n=P)
        st_d = comps[:, 2, :, :].rearrange("p a n -> p (a n)")
        st_sh = comps[:, 1, 3, :].rearrange("p (a n) -> p a n", n=P)
        st_r0, st_r1 = tmp[0:E0, 0, 0:P], tmp[0:E1, 0, P:2 * P]
        st_pw = tmp[:, 1, :].rearrange("p (l n) -> p l n", l=L)
        hart_w = sb("hart_w", [P, D])

        loaded = {n: sem("loaded_" + n) for n in ("small", "consts", "attn", "gates", "experts0", "wqkv")}
        set_up = sem("set_up")
        prep_T = sem("prep_T")
        prep_c = sem("prep_c")
        w_perm = sem("w_perm")
        bias_mm = sem("bias_mm")
        folded = sem("folded")
        hp_mm = sem("hp_mm")
        hp_c = sem("hp_c")
        a_full = sem("a_full")
        a_done = sem("a_done")
        lnA_bn, lnA_mv, lnA_rs, lnA_out = sem("lnA_bn"), sem("lnA_mv"), sem("lnA_rs"), sem("lnA_out")
        lnA_ve, lnB_ve = sem("lnA_ve"), sem("lnB_ve")
        lnB_bn, lnB_mv, lnB_rs, lnB_out = sem("lnB_bn"), sem("lnB_mv"), sem("lnB_rs"), sem("lnB_out")
        ham = sem("ham")
        rolled = sem("rolled")
        diffed = sem("diffed")
        folded_ang = sem("folded_ang")
        cosined = sem("cosined")
        r0_step, r0_sig, r0_done = sem("r0_step"), sem("r0_sig"), sem("r0_done")
        r1_step, r1_done = sem("r1_step"), sem("r1_done")
        x_in = sem("x_in")
        comb = sem("comb")
        x1_ready = sem("x1_ready")
        t_full = sem("t_full")
        t_done = [sem("t_done0"), sem("t_done1")]
        roped = sem("roped")
        smax = sem("smax")
        rinved = sem("rinved")
        y_step = sem("y_step")
        y_gated = sem("y_gated")
        stored = sem("stored")
        g_full, e_full, u_full = sem("g_full"), sem("e_full"), sem("u_full")
        silu = sem("silu")
        ge_sb = sem("ge_sb")
        weighed = sem("weighed")
        h_ready = sem("h_ready")
        c_full = sem("c_full")
        c_done = sem("c_done")

        block = ctx.enter_context(nc.Block())

        class Round:

            def __init__(self, a, b, unit, gel, wei, mix):
                self.a, self.b, self.unit, self.gel, self.wei, self.mix = a, b, unit, gel, wei, mix

        GEL0, GEL1 = E0, PAIR1
        WEI = UNITS0 + PAIR1
        first = Round(0, None, 0, 0, 0, 0)
        last = Round(None, NB - 1, (NB - 1) * UNITS, (NB - 1) * (GEL0 + GEL1), (NB - 1) * WEI, (NB - 1) * 2)

        def middle(i):
            return Round(i, i - 1, i * UNITS - UNITS1, i * (GEL0 + GEL1) - GEL1, i * WEI - PAIR1, i * 2 - 1)

        def fill_no(r, name):
            return r.a * NFILL + (NPREP + FILL[name])

        def a_ready(eng, r, name):
            eng.wait_ge(a_full, fill_no(r, name) + 1)

        def a_ended(eng, r, name):
            eng.wait_ge(a_done, fill_no(r, name) + 1)

        def t_set(t):
            return bT[STEP_AT[t] % 2]

        def t_ready(eng, r, t):
            eng.wait_ge(t_full, r.b * len(STEPS) + (STEP_AT[t] + 1))

        def t_sem(t):
            return t_done[STEP_AT[t] % 2]

        def t_ended(eng, r, t):
            n = STEP_AT[t]
            eng.wait_ge(t_done[n % 2], r.b * STEPS_OF[n % 2] + (n // 2 + 2))

        def t_begin(eng, r, t, *earlier):
            n = STEP_AT[t]
            eng.wait_ge(t_done[n % 2], r.b * STEPS_OF[n % 2] + (n // 2 + 1))
            other = [STEP_AT[e] for e in earlier if STEP_AT[e] % 2 != n % 2]
            if other:
                t_ended(eng, r, STEPS[max(other)])

        def ham_no(r, l, n):
            return r.a * (L * HAM_OPS) + (l * HAM_OPS + n)

        def ln_no(r, name):
            return r.a * len(LN_ORDER) + (1 + LN_AT[name])

        def unit_kind(u):
            if u < UNITS0:
                e, half = u // HALF0, u % HALF0
                c = slice(half * P, half * P + P)
                return w_g0[:, e, c], w_u0[:, e, c], w_d0[:, e, half, :], (sel0[:, e, :] if half == 0 else None), e
            j = u - UNITS0
            return w_g1[:, j, :], w_u1[:, j, :], w_d1[:, j, :], (sel1[:, j, :] if j < PAIR1 else None), GEL0 + j

        def has_weight(u):
            return u < UNITS - 1

        def units_of(r):
            return range(0 if r.a is not None else UNITS0, UNITS if r.b is not None else UNITS0)

        def rounds(eng, one):
            one(first)
            with eng.Fori(1, NB) as i:
                one(middle(i))
            one(last)

        def each_slot(r, a_part, t_part, u_part):
            turn = 0
            units = units_of(r)
            for l in range(L):
                for s in range(SLOTS):
                    if r.a is not None:
                        a_part(l, s)
                    if r.b is not None:
                        for t in steps_in(l, s):
                            t_part(t)
                    if s in UNIT_SLOTS:
                        u = turn
                        if u in units or u - 1 in units:
                            u_part(u if u in units else None, u - 1 if u - 1 in units else None)
                        turn += 1

        def gates0_no(r):
            return NPREP if r is first else r.a * NFILL + (NPREP - NFILL + FILL[("gates0_T", 0)] + 1)

        def prep_sources():
            rows = [st_par[:, n * D:(n + 1) * D] for n in range(4)] + \
                   [st_par2[:, n * D:(n + 1) * D] for n in range(NCOL - 4)]
            out = [rows, [st_r0, st_r1]]
            for st in (st_g, st_u):
                out += [[st[:, 4 * g + k, :] for k in range(4)] for g in range(PAIR1 // 4)]
            out += [[st_d[:, (4 * g + k) * P:(4 * g + k + 1) * P] for k in range(4)] for g in range(PAIR1 // 4)]
            return out + [[st_sh[:, n, :]] for n in range(3)]

        def prep_targets():
            out = [(cols[:, :, :], NCOL * L, NCOL), (w_r[:, :], E0 + E1, None)]
            for w in (w_g1, w_u1, w_d1):
                out += [(w[:, 4 * g:4 * g + 4, :], 4 * P, 4) for g in range(PAIR1 // 4)]
            return out + [(w[:, PAIR1, :], P, None) for w in (w_g1, w_u1, w_d1)]

        @block.sync
        def _(sp):
            def load(dst, src, s, n=1):
                sp.dma_start(dst, src).then_inc(s, 16)

            load(x_ld[:, :, :], x[0].rearrange("(t p) d -> p t d", p=P), x_in)
            sm = loaded["small"]
            for n, src in enumerate((ln1_w, ln1_b, ln2_w, ln2_b)):
                load(st_par[:, n * D:(n + 1) * D], src, sm)
            for n in range(3):
                load(st_par2[:, n * D:(n + 1) * D].rearrange("l (h d) -> l h d", h=H),
                     attn_b.rearrange("l (h t d) -> l h t d", h=H, t=3)[:, :, n, :], sm)
            load(st_par2[:, 3 * D:3 * D + FC * D], fc_b, sm)
            load(st_par2[:, 7 * D:8 * D], aproj_b, sm)
            load(st_par2[:, 8 * D:9 * D], mproj_b, sm)
            load(ident[:, :], c_ident, sm)
            load(st_r0, router_w, sm)
            load(st_r1, route_w1, sm)
            load(hart_w[:, :], c_hart, sm)
            load(st_pw, aproj_w.rearrange("l k n -> k l n"), sm)
            load(st_att, attn_w.rearrange("l k n -> k l n"), loaded["attn"])
            load(w_fc[:, :, :], fc_w.rearrange("l k n -> k l n"), loaded["attn"])
            load(st_g, gate_w1.rearrange("(j e) i h -> (e i) j h", j=PAIR1), loaded["gates"])
            load(st_u, up_w1.rearrange("(j e) i h -> (e i) j h", j=PAIR1), loaded["gates"])
            load(st_d.rearrange("p (e i) -> p e i", e=E1), down_w1.rearrange("e h i -> h e i"), loaded["gates"])
            for n, src in enumerate((sh_gate, sh_up, sh_down)):
                load(st_sh[:, n, :], src, loaded["gates"])
            load(w_g0[:, :, :], w_gate.rearrange("e k n -> k e n"), loaded["experts0"])
            load(w_u0[:, :, :], w_up.rearrange("e k n -> k e n"), loaded["experts0"])
            load(w_d0[:, :, :, :], w_down.rearrange("e (a p) n -> p e a n", p=P), loaded["experts0"])
            load(w_a1[:, :], w_qkv, loaded["wqkv"])
            cs = loaded["consts"]
            load(identb[:, :], c_identb, cs)
            load(cmod[:, :], c_cmod, cs)
            load(cosT[:, :], c_cos, cs)
            load(sinT[:, :], c_sin, cs)
            load(maskb[:, :], c_mask, cs)
            load(sel0[:, :, :], c_sel0, cs)
            load(sel1[:, :, :], c_sel1, cs)
            load(iota[:, :], c_iota, cs)
            load(ltri[:, :, :], c_ltri, cs)
            load(rbias[:, :], route_b1.unsqueeze(0).to_broadcast([P, E1]), cs)
            load(w_mp[:, :, :, :], mproj_w.rearrange("l (a p) n -> p l a n", p=P), cs)
            load(w_o1[:, :, :], w_out.rearrange("(a p) n -> p a n", p=P), cs)

            def one(r):
                if r.a is not None:
                    if r is first:
                        sp.wait_ge(lnA_out, 1)
                    else:
                        sp.wait_ge(x1_ready, r.a)
                    nxt = (r.a + 1) % NB
                    sp.dma_start(x_ld[:, :, :], x[nxt].rearrange("(t p) d -> p t d", p=P)).then_inc(x_in, 16)
                    for l in range(L):
                        a_ended(sp, r, ("v", l))
                        sp.dma_start(comps[HD:P, :, 2, :], comps[0:P - HD, :, 0, :]).then_inc(rolled, 16)
                        sp.dma_start(comps[0:HD, :, 2, :], comps[P - HD:P, :, 0, :]).then_inc(rolled, 16)
                    sp.wait_ge(lnA_out, ln_no(r, ("prep", L - 1)) + 1)
                    sp.dma_start(x_ld[:, :, :], x[r.a].rearrange("(t p) d -> p t d", p=P)).then_inc(x_in, 16)
                if r.b is not None:
                    t_ended(sp, r, ("final_T",))
                    sp.dma_start(out[r.b].rearrange("(t p) d -> p t d", p=P), y_out[:, :, :]).then_inc(stored, 16)

            rounds(sp, one)
            sp.wait_ge(stored, (NB + 1) * 16)

        @block.gpsimd
        def _(pool):
            nc.gpsimd.memset(nhalf[:, :], -0.5).then_inc(t_done[0], 1)
            nc.gpsimd.memset(epsT[:, :], EPS).then_inc(t_done[1], 1)
            nc.gpsimd.memset(hpi[:, :], math.pi / 2).then_inc(roped, 1)
            nc.gpsimd.memset(Kk[:, 0:WIN], 0.0).then_inc(stored, 16)
            nc.gpsimd.memset(V[:, 0, :], 0.0).then_inc(set_up, 1)
            pool.wait_ge(prep_T, PREP_BANKS)
            pool.wait_ge(w_perm, 1)
            nc.gpsimd.memset(comps[:, :, 1, 0:1], 0.0).then_inc(set_up, 1)
            pool.wait_ge(set_up, 2)

            def rstd(mv, ve, rs, mv_sem, ve_sem, rs_sem, n):
                pool.wait_ge(mv_sem, n + 1)
                nc.gpsimd.tensor_tensor(ve[:, :], mv[:, :, 1], epsT[:, :], ALU.add).then_inc(ve_sem, 1)
                pool.wait_ge(ve_sem, n + 1)
                nc.gpsimd.tensor_tensor(rs[:, :], ve[:, :], nhalf[:, :], ALU.pow).then_inc(rs_sem, 1)

            rstd(mvA, veA, rsA, lnA_mv, lnA_ve, lnA_rs, 0)

            def one(r):
                def a_part(l, s):
                    if s == 0:
                        rstd(mvA, veA, rsA, lnA_mv, lnA_ve, lnA_rs, ln_no(r, ("ln1", l)))
                    if l == L - 1 and s == min(PREP):
                        rstd(mvA, veA, rsA, lnA_mv, lnA_ve, lnA_rs, ln_no(r, ("prep", l)))
                    if s == 16:
                        rstd(mvA, veA, rsA, lnA_mv, lnA_ve, lnA_rs, ln_no(r, ("ln2", l)))
                    if s == 3:
                        a_ended(pool, r, ("v", l))
                        c0 = comps[:, :, 0, :]
                        nc.gpsimd.tensor_tensor(comps[:, :, 1, 1:S], c0[:, :, 1:S], c0[:, :, 0:S - 1],
                                                ALU.subtract).then_inc(diffed, 1)

                def t_part(t):
                    if t[0] in "qk":
                        dst = Q[:, :] if t[0] == "q" else Kk[:, WIN:]
                        t_ended(pool, r, t)
                        nc.gpsimd.tensor_tensor(dst, dst, rot[:, :], ALU.add).then_inc(roped, 1)

                def u_part(u, before):
                    if u is not None and has_weight(u):
                        pool.wait_ge(silu, r.unit + (u + 1))
                        pool.wait_ge(ge_sb, r.gel + (unit_kind(u)[4] + 1))
                        nc.gpsimd.tensor_tensor(s_h[:, :], s_h[:, :], ge[:, :], ALU.mult).then_inc(weighed, 1)

                if r.b is not None:
                    rstd(mvB, veB, rsB, lnB_mv, lnB_ve, lnB_rs, r.b)
                    for t in FIRST_STEPS:
                        t_part(t)
                each_slot(r, a_part, t_part, u_part)

            rounds(pool, one)

        @block.scalar
        def _(act):
            def copy(dst, src):
                return nc.scalar.activation(dst, src, ACT.Copy)

            for n, (dst, width, shape) in enumerate(prep_targets()):
                act.wait_ge(prep_T, n + 1)
                copy(dst, banks[n % len(banks)][:, 0:width] if shape is None else
                     banks[n % len(banks)][:, 0:width].rearrange("p (a n) -> p a n", a=shape)).then_inc(prep_c, 1)
            act.wait_ge(hp_mm, 1)
            copy(w_hp[:, :, :], bC[:, :].rearrange("p (l n) -> p l n", l=L)).then_inc(hp_c, 1)

            def prep_copy(ready):
                ready(act, ("prep_T", 0))
                copy(xn_f[:, :], bA[:, :]).then_inc(a_done, 1)

            def prep_sig(n):
                act.wait_ge(r0_step, n)
                nc.scalar.activation(r0_sg[:, :, :], r0_top[:, :, 0:K0], ACT.Sigmoid).then_inc(r0_sig, 1)

            def prep_gates(ready):
                ready(act, ("gates0_T", 0))
                copy(gates0[:, :], bA[:, :].bitcast(bf16)[0:PARTS * E0, 0:S]).then_inc(a_done, 1)

            prep_copy(lambda e, n: e.wait_ge(a_full, PREP_FILL[n] + 1))
            prep_sig(R0_TOP)
            prep_gates(lambda e, n: e.wait_ge(a_full, PREP_FILL[n] + 1))

            def one(r):
                def ready(e, name):
                    a_ready(e, r, name)

                def a_part(l, s):
                    name = STEP_A.get(s)
                    if name in ("ln1_T", "ln2_T"):
                        a_ready(act, r, (name, l))
                        copy(xf, bA[:, :]).then_inc(a_done, 1)
                    if name in ("q", "k", "v"):
                        n = "qkv".index(name)
                        a_ready(act, r, (name, l))
                        nc.scalar.activation(comps[:, n, 0, :], bA[:, :], ACT.Identity,
                                             bias=cols[:, AB + n, l:l + 1]).then_inc(a_done, 1)
                    if s == HAM0 + 1:
                        act.wait_ge(ham, ham_no(r, l, 3))
                        nc.scalar.activation(comps[:, :, 3, :], comps[:, :, 3, :], ACT.Abs).then_inc(folded_ang, 1)
                        act.wait_ge(folded_ang, r.a * L + (l + 1))
                        nc.scalar.activation(comps[:, :, 3, :], comps[:, :, 3, :], ACT.Sin, bias=hpi[:, 0:1],
                                             scale=-1.0).then_inc(cosined, 1)
                    if name in ("proj", "mproj"):
                        a_ready(act, r, (name, l))
                        n = PB if name == "proj" else MB
                        nc.scalar.activation(pfm, bA[:, :], ACT.Identity,
                                             bias=cols[:, n, l:l + 1]).then_inc(a_done, 1)
                    if name in ("fc0", "fc1", "fc2", "fc3"):
                        j = int(name[2])
                        a_ready(act, r, (name, l))
                        nc.scalar.activation(hid[:, j, :], bA[:, :], ACT.Gelu,
                                             bias=cols[:, FB + j, l:l + 1]).then_inc(a_done, 1)
                    if l == L - 1 and s in PREP:
                        if PREP[s] == "prep_T":
                            prep_copy(ready)
                        if PREP[s] == "route0":
                            prep_sig((r.a + 1) * R0_STEPS + R0_TOP)
                        if PREP[s] == "gates0_T":
                            prep_gates(ready)

                def t_part(t):
                    b = t_set(t)
                    if t[0] == "xn1_T":
                        t_ready(act, r, t)
                        copy(x1n_f[:, :], b[0][:, :]).then_inc(t_sem(t), 1)
                    if t[0] == "route1":
                        t_ready(act, r, t)
                        nc.scalar.activation(r1_s[:, :, :], b[0][:, 0:NT * E1].rearrange("p (t e) -> p t e", t=NT),
                                             ACT.Sigmoid).then_inc(t_sem(t), 1)
                    if t[0] == "V":
                        t_ready(act, r, t)
                        copy(V[:, 1:, :], b[0][:, :].rearrange("p (w n) -> p w n", w=NW)).then_inc(t_sem(t), 1)
                    if t[0] == "S":
                        n = 2 * t[1] + t[2] + 1
                        act.wait_ge(smax, r.b * (2 * HP) + n)
                        for h in range(2):
                            for w in range(2):
                                ww = 2 * t[2] + w
                                ins = nc.scalar.activation(probs[:, h, ww, :], b[h][:, w * 2 * WIN:(w + 1) * 2 * WIN],
                                                           ACT.Exp, bias=nmax[:, h, ww:ww + 1],
                                                           accum_out=rsum[:, ww, h:h + 1])
                        ins.then_inc(t_sem(t), 1)
                    if t[0] == "PT":
                        t_ready(act, r, t)
                        copy(probsT[:, 0, :], b[0][:, :])
                        copy(probsT[:, 1, :], b[1][:, :]).then_inc(t_sem(t), 1)
                    if t[0] == "OT":
                        t_ready(act, r, t)
                        copy(OT[:, t[1] % 2, :], b[0][:, :]).then_inc(t_sem(t), 1)
                    if t[0] == "gates1_T":
                        t_ready(act, r, t)
                        copy(gates1[:, :], b[0][:, :].bitcast(bf16)[0:PARTS * E1, 0:S]).then_inc(t_sem(t), 1)

                def mixture(n, dst):
                    act.wait_ge(c_full, r.mix + (n + 1))
                    nc.scalar.activation(dst, bC[:, :], ACT.Silu).then_inc(c_done, 1)

                def u_part(u, before):
                    if before == UNITS0 - 1:
                        mixture(0, gate_f[:, :])
                    if before == UNITS - 1:
                        mixture(1, gate1_f[:, :])
                    if u is None:
                        return
                    sel, g = unit_kind(u)[3:]
                    if sel is not None:
                        act.wait_ge(e_full, r.gel + (g + 1))
                        copy(ge[:, :], bU[:, :]).then_inc(ge_sb, 1)
                    act.wait_ge(g_full, r.unit + (u + 1))
                    nc.scalar.activation(s_h[:, :], bG[:, :], ACT.Silu).then_inc(silu, 1)

                if r.b is not None:
                    for t in FIRST_STEPS:
                        t_part(t)
                each_slot(r, a_part, t_part, u_part)

            rounds(act, one)

        @block.vector
        def _(dve):
            V_ = nc.vector

            def settled():
                V_.memset(scratch[:, :], 0.0)

            def layernorm(src, dst, st, mv, rs, bn_s, mv_s, rs_s, out_s, n):
                for t in range(NT):
                    ins = V_.bn_stats(st[:, t, :], src[:, t, :])
                ins.then_inc(bn_s, 1)
                dve.wait_ge(bn_s, n + 1)
                settled()
                for t in range(NT):
                    ins = V_.bn_aggr(mv[:, t, :], st[:, t, :])
                ins.then_inc(mv_s, 1)
                dve.wait_ge(mv_s, n + 1)
                dve.wait_ge(rs_s, n + 1)
                for t in range(NT):
                    ins = V_.tensor_scalar(dst[:, t, :], src[:, t, :], mv[:, t, 0:1], rs[:, t:t + 1],
                                           ALU.subtract, ALU.mult)
                ins.then_inc(out_s, 1)

            def layernorm_a(src, dst, n):
                layernorm(src, dst, stA, mvA, rsA, lnA_bn, lnA_mv, lnA_rs, lnA_out, n)

            def linker(s, base):
                n = [0]

                def link(ins, alone=False):
                    n[0] += 1
                    ins.then_inc(s, 1)
                    dve.wait_ge(s, base + n[0])
                    if alone:
                        settled()
                return link

            def split(link, g, parts, done):
                for k in range(PARTS):
                    ins = V_.tensor_copy(parts[:, :, k, :], g)
                    if k == PARTS - 1:
                        ins.then_inc(done, 1)
                    else:
                        link(ins)
                        link(V_.tensor_tensor(g, g, parts[:, :, k, :], ALU.subtract))

            def route0(base, sig_n, ready):
                link = linker(r0_step, base)
                ready(dve, ("route0", 0))
                ins = V_.tensor_copy(r0_lg[:, :, :], bA[:, 0:NT * E0].rearrange("p (t e) -> p t e", t=NT))
                ins.then_inc(a_done, 1)
                return link

            def route0_rest(link, sig_n, copied):
                dve.wait_ge(a_done, copied)
                settled()
                for t in range(NT):
                    ins = V_.max(r0_top[:, t, :], r0_lg[:, t, :])
                link(ins, True)
                for t in range(NT):
                    ins = V_.max_index(r0_idx[:, t, :], r0_top[:, t, :], r0_lg[:, t, :])
                link(ins)
                link(V_.tensor_copy(r0_idf[:, :, :], r0_idx[:, :, :]))
                link(V_.tensor_tensor(r0_hit[:, :, :, :], iota[:, 0:E0].unsqueeze(1).unsqueeze(1).to_broadcast([P, NT, K0, E0]),
                                      r0_idf[:, :, 0:K0].unsqueeze(3).to_broadcast([P, NT, K0, E0]), ALU.is_equal))
                dve.wait_ge(r0_sig, sig_n)
                link(V_.tensor_reduce(r0_sum[:, :], r0_sg[:, :, :], AX.X, ALU.add))
                link(V_.tensor_scalar(r0_sum[:, :], r0_sum[:, :], 1e-10, None, ALU.add))
                link(V_.reciprocal(r0_sum[:, :], r0_sum[:, :]))
                link(V_.tensor_tensor(r0_sg[:, :, :], r0_sg[:, :, :], r0_sum[:, :].unsqueeze(2).to_broadcast([P, NT, K0]), ALU.mult))
                link(V_.tensor_tensor(r0_hit[:, :, :, :], r0_hit[:, :, :, :],
                                      r0_sg[:, :, :].unsqueeze(3).to_broadcast([P, NT, K0, E0]), ALU.mult))
                link(V_.tensor_tensor(r0_g[:, :, :], r0_hit[:, :, 0, :], r0_hit[:, :, 1, :], ALU.add))
                split(link, r0_g[:, :, :], r0_parts, r0_done)

            dve.wait_ge(loaded["attn"], 32)
            for l in range(L):
                ins = V_.tensor_copy(w_att[:, l, :, :].rearrange("p t (h d) -> p t h d", h=H),
                                     st_att[:, l, :].rearrange("p (h t d) -> p t h d", h=H, t=3))
            ins.then_inc(w_perm, 1)
            dve.wait_ge(loaded["wqkv"], 16)
            V_.tensor_scalar(w_a1[:, 0:INNER], w_a1[:, 0:INNER], DH ** -0.5, None, ALU.mult).then_inc(folded, 1)
            dve.wait_ge(folded, 1)
            V_.tensor_copy(w_rot[:, :].rearrange("p (h a d) -> p h a d", a=2, d=DH // 2),
                           w_a1[:, 0:2 * INNER].rearrange("p (h a d) -> p h a d", a=2, d=DH // 2)[:, :, ::-1, :])
            dve.wait_ge(prep_c, PREP_BANKS)
            dve.wait_ge(bias_mm, 1)
            nb = L * (3 + FC)
            V_.tensor_tensor(cols[:, AB:AB + 3 + FC, :], cols[:, AB:AB + 3 + FC, :],
                             bC[:, 0:nb].rearrange("p (n l) -> p n l", l=L), ALU.add)
            for l in range(L):
                V_.tensor_scalar(w_att[:, l, :, :], w_att[:, l, :, :], cols[:, LN1W, l:l + 1], None, ALU.mult)
                ins = V_.tensor_scalar(w_fc[:, l, :], w_fc[:, l, :], cols[:, LN2W, l:l + 1], None, ALU.mult)
            ins.then_inc(folded, 1)
            dve.wait_ge(loaded["consts"], 16 * 12)
            dve.wait_ge(x_in, 16)
            layernorm_a(x_ld, xn, 0)

            def prep_ready(e, name):
                e.wait_ge(a_full, PREP_FILL[name] + 1)

            link0 = route0(0, 1, prep_ready)
            route0_rest(link0, 1, PREP_FILL[("route0", 0)] + 1)

            def quaternions(r, l, part):
                a, b, c = comps[:, 0], comps[:, 1], comps[:, 2]
                no = lambda n: ham_no(r, l, n)

                def many(q, k, n):
                    return q[:, k:k + 1, :].to_broadcast([P, n, S])

                def tt(dst, i0, i1, op, n):
                    dve.wait_ge(ham, no(n - 1))
                    V_.tensor_tensor(dst, i0, i1, op).then_inc(ham, 1)

                if part == 0:
                    a_ended(dve, r, ("v", l))
                    c0 = comps[:, :, 0, :]
                    V_.tensor_scalar(turns, c0, 1.0 / TWO_PI, None, ALU.mult).then_inc(ham, 1)
                    dve.wait_ge(ham, no(1))
                    V_.tensor_scalar(turns, turns, ROUND, ROUND, ALU.add, ALU.subtract).then_inc(ham, 1)
                    dve.wait_ge(ham, no(2))
                    V_.scalar_tensor_tensor(comps[:, :, 3, :].rearrange("p a n -> p a n"), turns, -TWO_PI, c0,
                                            ALU.mult, ALU.add).then_inc(ham, 1)
                if part == 1:
                    dve.wait_ge(cosined, r.a * L + (l + 1))
                    dve.wait_ge(diffed, r.a * L + (l + 1))
                    dve.wait_ge(rolled, r.a * (L * 32) + (l + 1) * 32)
                    tt(acc[:, :, :], many(b, 0, 4), c, ALU.mult, 4)
                if part == 2:
                    tt(tmp[:, :, :], many(b, 1, 2), c[:, 1::2, :], ALU.mult, 5)
                    tt(acc[:, 0::2, :], acc[:, 0::2, :], tmp[:, :, :], ALU.subtract, 6)
                    tt(tmp[:, :, :], many(b, 1, 2), c[:, 0::2, :], ALU.mult, 7)
                if part == 3:
                    tt(acc[:, 1::2, :], acc[:, 1::2, :], tmp[:, :, :], ALU.add, 8)
                    tt(tmp[:, :, :], many(b, 2, 2), c[:, 2:0:-1, :], ALU.mult, 9)
                    tt(acc[:, 0::3, :], acc[:, 0::3, :], tmp[:, :, :], ALU.subtract, 10)
                if part == 4:
                    tt(tmp[:, :, :], many(b, 2, 2), c[:, 3::-3, :], ALU.mult, 11)
                    tt(acc[:, 1:3, :], acc[:, 1:3, :], tmp[:, :, :], ALU.add, 12)
                if part == 5:
                    tt(tmp[:, :, :], many(b, 3, 2), c[:, 3:1:-1, :], ALU.mult, 13)
                    tt(acc[:, 0:2, :], acc[:, 0:2, :], tmp[:, :, :], ALU.subtract, 14)
                    tt(tmp[:, :, :], many(b, 3, 2), c[:, 1::-1, :], ALU.mult, 15)
                if part == 6:
                    tt(acc[:, 2:4, :], acc[:, 2:4, :], tmp[:, :, :], ALU.add, 16)
                    tt(acc[:, :, :], a, acc[:, :, :], ALU.mult, 17)
                if part == 7:
                    tt(tmp[:, 0, :], acc[:, 0, :], acc[:, 1, :], ALU.subtract, 18)
                    tt(tmp[:, 1, :], acc[:, 2, :], acc[:, 3, :], ALU.add, 19)
                if part == 8:
                    tt(z, tmp[:, 0, :], tmp[:, 1, :], ALU.subtract, 20)

            def route1(r):
                link = linker(r1_step, r.b * R1_STEPS)
                t_ended(dve, r, ("route1",))
                link(V_.tensor_tensor(r1_c[:, :, :], r1_s[:, :, :], rbias[:, :].unsqueeze(1).to_broadcast([P, NT, E1]), ALU.add), True)
                for t in range(NT):
                    for g in range(GROUPS):
                        ins = V_.max(r1_m8[:, t, g, :], r1_c[:, t, g * EG:(g + 1) * EG])
                link(ins)
                link(V_.tensor_tensor(r1_gs[:, :, :], r1_m8[:, :, :, 0], r1_m8[:, :, :, 1], ALU.add))
                other = r1_gs[:, :, :].unsqueeze(2).to_broadcast([P, NT, GROUPS, GROUPS])
                mine = r1_gs[:, :, :].unsqueeze(3).to_broadcast([P, NT, GROUPS, GROUPS])
                link(V_.tensor_tensor(r1_gt[:, :, :, :], other, mine, ALU.is_gt))
                link(V_.tensor_tensor(r1_eq[:, :, :, :], other, mine, ALU.is_equal))
                link(V_.tensor_tensor(r1_eq[:, :, :, :], r1_eq[:, :, :, :],
                                      ltri[:, :, :].unsqueeze(1).to_broadcast([P, NT, GROUPS, GROUPS]), ALU.mult))
                link(V_.tensor_tensor(r1_gt[:, :, :, :], r1_gt[:, :, :, :], r1_eq[:, :, :, :], ALU.add))
                link(V_.tensor_reduce(r1_gs[:, :, :], r1_gt[:, :, :, :], AX.X, ALU.add))
                link(V_.tensor_scalar(r1_gs[:, :, :], r1_gs[:, :, :], float(TOPG), None, ALU.is_lt))
                by_group = r1_c[:, :, :].rearrange("p t (g e) -> p t g e", g=GROUPS)
                link(V_.tensor_tensor(by_group, by_group, r1_gs[:, :, :].unsqueeze(3).to_broadcast([P, NT, GROUPS, EG]), ALU.mult))
                link(V_.tensor_scalar(r1_c[:, :, :], r1_c[:, :, :], 0.0, None, ALU.add), True)
                for t in range(NT):
                    ins = V_.max(r1_top[:, t, :], r1_c[:, t, :])
                link(ins, True)
                for t in range(NT):
                    ins = V_.max_index(r1_idx[:, t, :], r1_top[:, t, :], r1_c[:, t, :])
                link(ins)
                link(V_.tensor_copy(r1_idf[:, :, :], r1_idx[:, :, :]))
                link(V_.tensor_tensor(r1_hit, iota[:, :].unsqueeze(1).unsqueeze(1).to_broadcast([P, NT, TOPK1, E1]),
                                      r1_idf[:, :, 0:TOPK1].unsqueeze(3).to_broadcast([P, NT, TOPK1, E1]), ALU.is_equal))
                link(V_.tensor_tensor(r1_hit[:, :, 0:2, :], r1_hit[:, :, 0:2, :], r1_hit[:, :, 2:4, :], ALU.add))
                link(V_.tensor_tensor(r1_c[:, :, :], r1_hit[:, :, 0, :], r1_hit[:, :, 1, :], ALU.add))
                link(V_.tensor_tensor(r1_s[:, :, :], r1_s[:, :, :], r1_c[:, :, :], ALU.mult))
                link(V_.tensor_reduce(r1_sum[:, :], r1_s[:, :, :], AX.X, ALU.add))
                link(V_.tensor_scalar(r1_sum[:, :], r1_sum[:, :], 1e-20, None, ALU.add))
                link(V_.reciprocal(r1_sum[:, :], r1_sum[:, :]))
                link(V_.tensor_scalar(r1_sum[:, :], r1_sum[:, :], SCALE1, None, ALU.mult))
                link(V_.tensor_tensor(r1_s[:, :, :], r1_s[:, :, :], r1_sum[:, :].unsqueeze(2).to_broadcast([P, NT, E1]), ALU.mult))
                split(link, r1_s[:, :, :], r1_parts, r1_done)

            def one(r):
                def a_part(l, s):
                    name = STEP_A.get(s)
                    src = xn if l == 0 else xr
                    if s == 0:
                        layernorm_a(src, ln_hat, ln_no(r, ("ln1", l)))
                    if HAM0 <= s < HAM0 + 9:
                        quaternions(r, l, s - HAM0)
                    if name == "hart":
                        a_ready(dve, r, (name, l))
                        V_.tensor_tensor(zc, bA[:, :], cmod[:, :], ALU.mult).then_inc(a_done, 1)
                    if name in ("proj_T", "mproj_T"):
                        if name == "mproj_T" or l:
                            src = xr
                        a_ready(dve, r, (name, l))
                        V_.tensor_tensor(xr[:, :, :], bA[:, :].rearrange("p (t d) -> p t d", t=NT), src[:, :, :],
                                         ALU.add).then_inc(a_done, 1)
                        a_ended(dve, r, (name, l))
                    if name == "ln2_T":
                        layernorm_a(xr, ln_hat, ln_no(r, ("ln2", l)))
                    if l == L - 1 and s in PREP:
                        if PREP[s] == "prep_T":
                            dve.wait_ge(x_in, r.a * 32 + 32)
                            layernorm_a(x_ld, xn, ln_no(r, ("prep", l)))
                        if PREP[s] == "route0":
                            link = route0((r.a + 1) * R0_STEPS, r.a + 2, lambda e, n: a_ready(e, r, n))
                            route0_rest(link, r.a + 2, fill_no(r, ("route0", 0)) + 1)

                def t_part(t):
                    b = t_set(t)
                    if t[0] in "qk":
                        n = ROPE_ORDER.index(t)
                        dst = Q[:, :] if t[0] == "q" else Kk[:, WIN:]
                        t_ready(dve, r, t)
                        V_.tensor_tensor(dst, b[0][:, :], cosT[:, :], ALU.mult)
                        dve.wait_ge(roped, r.b * len(ROPE_ORDER) + (n + 1))
                        V_.tensor_tensor(rot[:, :], b[1][:, :], sinT[:, :], ALU.mult).then_inc(t_sem(t), 1)
                    if t[0] == "S":
                        t_ready(dve, r, t)
                        for h in range(2):
                            ins = V_.tensor_reduce(nmax[:, h, 2 * t[2]:2 * t[2] + 2],
                                                   b[h][:, :].rearrange("p (w n) -> p w n", w=2), AX.X, ALU.max,
                                                   negate=True)
                        ins.then_inc(smax, 1)
                    if t[0] == "O":
                        n = 2 * t[1] + t[2] + 1
                        w = slice(2 * t[2], 2 * t[2] + 2)
                        t_ended(dve, r, ("S", t[1], t[2]))
                        if (t[1], t[2]) == (0, 0):
                            dve.wait_ge(stored, r.b * 16 + 16)
                        V_.reciprocal(rinv[:, w, :], rsum[:, w, :]).then_inc(rinved, 1)
                        dve.wait_ge(rinved, r.b * (2 * HP) + n)
                        t_ready(dve, r, t)
                        V_.tensor_tensor(O[:, w, :].rearrange("p w (h d) -> p w h d", h=2),
                                         b[0][:, 0:2 * P].rearrange("p (w h d) -> p w h d", w=2, h=2),
                                         rinv[:, w, :].unsqueeze(3).to_broadcast([P, 2, 2, DH]),
                                         ALU.mult).then_inc(t_sem(t), 1)
                    if t[0] == "out":
                        l = t[1]
                        t_ready(dve, r, t)
                        if l == 0:
                            V_.tensor_copy(y[:, :], b[0][:, :]).then_inc(t_sem(t), 1)
                        else:
                            t_ended(dve, r, ("out", l - 1))
                            V_.tensor_tensor(y[:, :], b[0][:, :], y[:, :], ALU.add).then_inc(t_sem(t), 1)

                def u_part(u, before):
                    if u is None:
                        return
                    dve.wait_ge(u_full, r.unit + (u + 1))
                    if has_weight(u):
                        dve.wait_ge(weighed, r.wei + (u + 1))
                    else:
                        dve.wait_ge(silu, r.unit + (u + 1))
                    V_.tensor_tensor(hu[:, :], bU[:, :], s_h[:, :], ALU.mult).then_inc(h_ready, 1)

                if r.b is not None:
                    dve.wait_ge(x1_ready, r.b + 1)
                    layernorm(x1, x1n, stB, mvB, rsB, lnB_bn, lnB_mv, lnB_rs, lnB_out, r.b)
                    for t in FIRST_STEPS:
                        t_part(t)
                        if t[0] == "V":
                            route1(r)
                each_slot(r, a_part, t_part, u_part)
                if r.b is not None:
                    dve.wait_ge(c_done, r.mix + 2)
                    t_ended(dve, r, ("out", L - 1))
                    V_.tensor_tensor(y[:, :], y[:, :], gate1_f[:, :], ALU.mult).then_inc(y_gated, 1)
                    t_ready(dve, r, ("final_T",))
                    V_.tensor_tensor(y_out[:, :, :], t_set(("final_T",))[0][:, :].rearrange("p (t d) -> p t d", t=NT),
                                     x1[:, :, :], ALU.add).then_inc(t_sem(("final_T",)), 1)
                if r.a is not None:
                    a_ready(dve, r, ("gate_T", 0))
                    V_.tensor_tensor(xmul, bA[:, :].rearrange("p (t d) -> p t d", t=NT), xr[:, :, :],
                                     ALU.mult).then_inc(a_done, 1)
                    a_ended(dve, r, ("gate_T", 0))
                    dve.wait_ge(x_in, r.a * 32 + 48)
                    V_.tensor_tensor(x1[:, :, :], xmul, x_ld[:, :, :], ALU.add).then_inc(x1_ready, 1)

            rounds(dve, one)

        @block.tensor
        def _(pe):
            mm = nc.tensor.matmul

            def transpose(dst, src):
                k = src.shape[0]
                return nc.tensor.transpose(dst, src, ident[0:k, 0:k])

            def transpose_b(dst, src):
                return nc.tensor.transpose(dst, src, identb[:, :])

            def transposes(bank, tiles):
                for n, src in enumerate(tiles):
                    ins = transpose(bank[:, n * P:(n + 1) * P], src)
                return ins

            for n, tiles in enumerate(prep_sources()):
                if n == 0:
                    pe.wait_ge(loaded["small"], 15 * 16)
                if n == 2:
                    pe.wait_ge(loaded["gates"], 6 * 16)
                if n >= len(banks):
                    pe.wait_ge(prep_c, n - len(banks) + 1)
                at = 0
                for src in tiles:
                    k = src.shape[0]
                    ins = transpose(banks[n % len(banks)][:, at:at + k], src)
                    at += k
                ins.then_inc(prep_T, 1)
            pe.wait_ge(w_perm, 1)
            pe.wait_ge(prep_c, 1)
            for n in range(3 + FC):
                for l in range(L):
                    w = w_att[:, l, n, :] if n < 3 else w_fc[:, l, (n - 3) * D:(n - 2) * D]
                    b = LN1B if n < 3 else LN2B
                    ins = mm(bC[:, n * L + l:n * L + l + 1], w, cols[:, b, l:l + 1], start=True, stop=True)
            ins.then_inc(bias_mm, 1)
            pe.wait_ge(folded, 2)
            for l in range(L):
                ins = mm(bC[:, l * D:(l + 1) * D], hart_w[:, :], st_pw[:, l, :], start=True, stop=True)
            ins.then_inc(hp_mm, 1)
            pe.wait_ge(hp_c, 1)
            pe.wait_ge(prep_c, PREP_BANKS)
            pe.wait_ge(loaded["experts0"], 3 * 16)
            pe.wait_ge(loaded["consts"], 12 * 16)

            def prep_step(name, before, out_n, done_n):
                pe.wait_ge(a_done, before)
                if name == "prep_T":
                    pe.wait_ge(lnA_out, out_n)
                    return transposes(bA, [xn[:, t, :] for t in range(NT)])
                if name == "route0":
                    for t in range(NT):
                        ins = mm(bA[:, t * E0:(t + 1) * E0], xn_f[:, t * P:(t + 1) * P], w_r0, start=True, stop=True)
                    return ins
                pe.wait_ge(r0_done, done_n)
                bank = bA[:, :].bitcast(bf16)
                for t in range(NT):
                    ins = transpose_b(bank[0:PARTS * E0, t * P:(t + 1) * P],
                                      r0_parts[:, t, :, :].rearrange("p k e -> p (k e)"))
                return ins

            for n, name in enumerate(PREP.values()):
                prep_step(name, n, 1, 1).then_inc(a_full, 1)

            def one(r):
                def fill(name, l):
                    pe.wait_ge(a_done, fill_no(r, (name, l)))

                def a_part(l, s):
                    name = STEP_A.get(s)
                    if name is not None:
                        if name == "hart":
                            pe.wait_ge(ham, ham_no(r, l, HAM_OPS))
                        if name in ("ln1_T", "ln2_T"):
                            pe.wait_ge(lnA_out, ln_no(r, (name[0:3], l)) + 1)
                        fill(name, l)
                        if name in ("ln1_T", "ln2_T"):
                            ins = transposes(bA, [ln_hat[:, t, :] for t in range(NT)])
                        if name in ("q", "k", "v"):
                            ins = mm(bA[:, :], w_att[:, l, "qkv".index(name), :], xf, start=True, stop=True)
                        if name == "hart":
                            ins = mm(bA[:, :], hart_w[:, :], z, start=True, stop=True)
                        if name == "proj":
                            ins = mm(bA[:, :], w_hp[:, l, :], zc, start=True, stop=True)
                        if name in ("proj_T", "mproj_T"):
                            ins = transposes(bA, [pfm[:, t * P:(t + 1) * P] for t in range(NT)])
                        if name in ("fc0", "fc1", "fc2", "fc3"):
                            j = int(name[2])
                            ins = mm(bA[:, :], w_fc[:, l, j * D:(j + 1) * D], xf, start=True, stop=True)
                        if name == "mproj":
                            for j in range(FC):
                                ins = mm(bA[:, :], w_mp[:, l, j, :], hid[:, j, :], start=j == 0, stop=j == FC - 1)
                        ins.then_inc(a_full, 1)
                    if l == L - 1 and s in PREP:
                        prep_step(PREP[s], fill_no(r, (PREP[s], 0)), ln_no(r, ("prep", l)) + 1, r.a + 2).then_inc(a_full, 1)

                def t_part(t):
                    b = t_set(t)
                    builds_on = {"route1": [("xn1_T",)], "PT": [("S",) + t[1:]], "O": [("PT",) + t[1:], ("V",) + t[1:2]],
                                 "OT": [("O",) + t[1:] + (k,) for k in range(2)],
                                 "out": [("OT", 2 * t[-1] + k) for k in range(2)] if t[0] == "out" else []}
                    if t == ("q", 0):
                        builds_on["q"] = [("xn1_T",)]
                    t_begin(pe, r, t, *builds_on.get(t[0], []))
                    if t[0] == "xn1_T":
                        pe.wait_ge(lnB_out, r.b + 1)
                        ins = transposes(b[0], [x1n[:, k, :] for k in range(NT)])
                    if t[0] == "route1":
                        for k in range(NT):
                            ins = mm(b[0][:, k * E1:(k + 1) * E1], x1n_f[:, k * P:(k + 1) * P], w_r1, start=True, stop=True)
                    if t[0] in "qk":
                        c = t[1] * P + (0 if t[0] == "q" else INNER)
                        mm(b[0][:, :], w_a1[:, c:c + P], x1n_f[:, :], start=True, stop=True)
                        ins = mm(b[1][:, :], w_rot[:, c:c + P], x1n_f[:, :], start=True, stop=True)
                    if t[0] == "V":
                        c = t[1] * P + 2 * INNER
                        for w in range(NW):
                            ins = mm(b[0][:, w * P:(w + 1) * P], x1n_f[:, w * WIN:(w + 1) * WIN], w_a1[:, c:c + P],
                                     start=True, stop=True)
                    if t[0] == "S":
                        if t[2] == 0:
                            pe.wait_ge(roped, r.b * len(ROPE_ORDER) + (ROPE_ORDER.index(("k", t[1])) + 2))
                        for h in range(2):
                            mm(b[h][:, :], identb[:, :], maskb[:, t[2] * 2 * WIN:t[2] * 2 * WIN + S], start=True, stop=False)
                        for w in range(2):
                            ww = 2 * t[2] + w
                            for h in range(2):
                                f = slice(h * DH, (h + 1) * DH)
                                ins = mm(b[h][:, w * 2 * WIN:(w + 1) * 2 * WIN], Q[f, ww * WIN:(ww + 1) * WIN],
                                         Kk[f, ww * WIN:(ww + 2) * WIN], start=False, stop=w == 1)
                    if t[0] == "PT":
                        for h in range(2):
                            ins = transposes(b[h], [probs[:, h, 2 * t[2] + w, k * P:(k + 1) * P]
                                                    for w in range(2) for k in range(2)])
                    if t[0] == "O":
                        for w in range(2):
                            for h in range(2):
                                for k in range(2):
                                    ins = mm(b[0][:, (2 * w + h) * DH:(2 * w + h + 1) * DH],
                                             probsT[:, h, (2 * w + k) * P:(2 * w + k + 1) * P],
                                             V[:, 2 * t[2] + w + k, h * DH:(h + 1) * DH], start=k == 0, stop=k == 1)
                    if t[0] == "OT":
                        ins = transposes(b[0], [O[:, w, :] for w in range(NW)])
                    if t[0] == "gates1_T":
                        pe.wait_ge(r1_done, r.b + 1)
                        bank = b[0][:, :].bitcast(bf16)
                        for k in range(NT):
                            ins = transpose_b(bank[0:PARTS * E1, k * P:(k + 1) * P],
                                              r1_parts[:, k, :, :].rearrange("p k e -> p (k e)"))
                    if t[0] == "out":
                        for k in range(2):
                            ins = mm(b[0][:, :], w_o1[:, 2 * t[1] + k, :], OT[:, k, :], start=k == 0, stop=k == 1)
                    if t[0] == "final_T":
                        pe.wait_ge(y_gated, r.b + 1)
                        ins = transposes(b[0], [y[:, k * P:(k + 1) * P] for k in range(NT)])
                    ins.then_inc(t_full, 1)

                def u_part(u, before):
                    if before is not None:
                        first_of = before in (0, UNITS0)
                        last_of = before in (UNITS0 - 1, UNITS - 1)
                        if first_of:
                            pe.wait_ge(c_done, r.mix + (1 if before else 0))
                        pe.wait_ge(h_ready, r.unit + (before + 1))
                        ins = mm(bC[:, :], unit_kind(before)[2], hu[:, :], start=first_of, stop=last_of)
                        if last_of:
                            ins.then_inc(c_full, 1)
                    if u is not None:
                        g, up, _, sel, e = unit_kind(u)
                        src, gates = (xn_f, gates0) if u < UNITS0 else (x1n_f, gates1)
                        if sel is not None:
                            if u == UNITS0:
                                t_ended(pe, r, ("gates1_T",))
                            if u == 0:
                                pe.wait_ge(a_done, gates0_no(r))
                            mm(bU[:, :], sel, gates[:, :], start=True, stop=True).then_inc(e_full, 1)
                        mm(bG[:, :], g, src[:, :], start=True, stop=True).then_inc(g_full, 1)
                        if sel is not None:
                            pe.wait_ge(ge_sb, r.gel + (e + 1))
                        mm(bU[:, :], up, src[:, :], start=True, stop=True).then_inc(u_full, 1)

                if r.b is not None:
                    for t in FIRST_STEPS:
                        t_part(t)
                each_slot(r, a_part, t_part, u_part)
                if r.b is not None:
                    t_part(("final_T",))
                if r.a is not None:
                    fill("gate_T", 0)
                    pe.wait_ge(c_done, r.mix + 1)
                    transposes(bA, [gate_f[:, k * P:(k + 1) * P] for k in range(NT)]).then_inc(a_full, 1)

            rounds(pe, one)


def hartley():
    h, d = np.divmod(np.arange(D), HD)
    turns = (np.outer(h, h) % H) / H + (np.outer(d, d) % HD) / HD
    return ((np.cos(2 * np.pi * turns) + np.sin(2 * np.pi * turns)) / np.sqrt(D)).astype(np.float32)


def filter_modulation():
    h, d = np.divmod(np.arange(D), HD)
    ks, kh, kd = np.fft.fftfreq(S)[None, :], np.fft.fftfreq(H)[h][:, None], np.fft.fftfreq(HD)[d][:, None]
    km = np.sqrt(ks ** 2 + kh ** 2 + kd ** 2 + 1e-10)
    real = np.cos(np.arctan(np.log(km + 1e-10)))
    lam, t = np.arange(S) / S, np.arange(S) * 0.1
    mod = np.sin(t + lam) * np.cos(t - 2.0 * lam + 0.5 * lam ** 2)
    return (real * (1.0 + 0.1 * mod)[None, :]).astype(np.float32)


def rotary():
    d = np.arange(P) % DH
    ang = (10000.0 ** -(2.0 * (d % (DH // 2)) / DH))[:, None] * np.arange(S)[None, :]
    return np.cos(ang).astype(np.float32), (np.sin(ang) * np.where(d < DH // 2, -1, 1)[:, None]).astype(np.float32)


def masks(dtype):
    i, j = np.arange(WIN)[:, None], np.arange(WIN)[None, :]
    here, before = np.where(j <= i, 0.0, MASKED), np.where(j >= i, 0.0, MASKED)
    return np.concatenate([np.full((WIN, WIN), MASKED), here, before, here, before, here], 1).astype(dtype)


def selectors(dtype):
    e0 = np.arange(PARTS * E0) % E0
    s0 = np.broadcast_to((e0[:, None] == np.arange(E0)[None, :])[:, :, None], (PARTS * E0, E0, P))
    e1 = np.arange(PARTS * E1) % E1
    s1 = e1[:, None, None] == (2 * np.arange(PAIR1)[:, None] + np.arange(P)[None, :] // I1)[None, :, :]
    return s0.astype(dtype), s1.astype(dtype)


_INS = ["L0_attn_x", "L0_attn_ln1_w", "L0_attn_ln1_b", "L0_attn_attn_w", "L0_attn_attn_b", "L0_attn_aproj_w",
        "L0_attn_aproj_b", "L0_attn_ln2_w", "L0_attn_ln2_b", "L0_attn_fc_w", "L0_attn_fc_b", "L0_attn_mproj_w",
        "L0_attn_mproj_b", "L0_ffn_router_w", "L0_ffn_w_gate", "L0_ffn_w_up", "L0_ffn_w_down", "L1_attn_W_qkv",
        "L1_attn_W_out", "L1_ffn_router_weight", "L1_ffn_router_bias", "L1_ffn_gate_w", "L1_ffn_up_w",
        "L1_ffn_down_w", "L1_ffn_shared_gate_w", "L1_ffn_shared_up_w", "L1_ffn_shared_down_w"]


def kernel(**inputs):
    import concourse.bacc as bacc
    from concourse.bass_utils import run_bass_kernel_spmd

    bf = mybir.dt.np(mybir.dt.bfloat16)
    nc = bacc.Bacc("TRN2", target_bir_lowering=False, num_devices=1)
    arrays = {name: np.ascontiguousarray(inputs[name]) for name in _INS}
    cos, sin = rotary()
    sel0, sel1 = selectors(bf)
    consts = {
        "c_ident": np.eye(P, dtype=np.float32), "c_identb": np.eye(P).astype(bf), "c_hart": hartley(),
        "c_cmod": filter_modulation(), "c_cos": cos, "c_sin": sin, "c_mask": masks(bf), "c_sel0": sel0, "c_sel1": sel1,
        "c_iota": np.broadcast_to(np.arange(E1, dtype=np.float32), (P, E1)),
        "c_ltri": np.broadcast_to(np.tril(np.ones((GROUPS, GROUPS), np.float32), -1), (P, GROUPS, GROUPS)),
    }
    arrays.update({n: np.ascontiguousarray(a) for n, a in consts.items()})
    args = [nc.dram_tensor("in_" + n, a.shape, mybir.dt.from_np(a.dtype), kind="ExternalInput").ap()
            for n, a in arrays.items()]
    out = nc.dram_tensor("out", (NB, S, D), mybir.dt.float32, kind="ExternalOutput").ap()
    program(nc, *args, out)
    r = run_bass_kernel_spmd(nc, [{"in_" + n: a for n, a in arrays.items()}], core_ids=[0])
    return r.results[0]["out"]
```

```python
import math
from contextlib import ExitStack

import numpy as np
import concourse.bass as bass
from concourse import mybir

NB, S, D = 16, 512, 128
P = 128
NT = S // P
L, H = 4, 16
HD = D // H
FC = 4
E0, H0, K0 = 8, 256, 2
HALF0 = H0 // P
E1, I1 = 32, 64
PAIR1 = E1 * I1 // P
GROUPS, TOPG, TOPK1, SCALE1 = 4, 2, 4, 2.5
EG = E1 // GROUPS
AH, DH, WIN = 16, 64, 128
HP = AH // 2
NW = S // WIN
INNER = AH * DH
PARTS = 3
EPS = 1e-5
ROUND = 1.5 * 2.0 ** 23
TWO_PI = 2.0 * math.pi
MASKED = -1e30

UNITS0, UNITS1 = E0 * HALF0, PAIR1 + 1
UNITS = UNITS0 + UNITS1
HAMS = 15
R0_CHUNKS, R1_CHUNKS = 4, 6


def stream_a():
    out = []
    for l in range(L):
        names = ["stats1", "norm1", "ln1_T", "k", "turn_k", "v", "turn_v", "ang_k", "abs_k", "q", "ang_v", "abs_v", "cos_k",
                 "cos_v", "turn_q", "ham0", "ang_q", "abs_q", "cos_q", "ham1"]
        if l == L - 1:
            names += ["prep_stats", "ham2", "prep_norm", "prep_T", "ham3", "ham4", "route0"]
        names += [f"ham{n}" for n in range(5 if l == L - 1 else 2, HAMS)]
        names += ["hart", "proj", "proj_T", "stats2"]
        names += {L - 2: ["gate_T"], L - 1: ["gates0_T"]}.get(l, [])
        names += ["norm2", "ln2_T", "fc0", "fc1", "fc2", "fc3", "mproj", "mproj_T"]
        out += [(name, l) for name in names]
    return out + [("join", L - 1)]


def stream_t():
    out = [("statsB",), ("normB",), ("xn1_T",), ("route1",), ("q", 0), ("k", 0), ("V", 0)]
    for p in range(HP):
        more = p + 1 < HP
        out += [("S", p, 0), ("S", p, 1), ("PT", p, 0)] + [("q", p + 1)] * more + [("O", p, 0), ("PT", p, 1)]
        out += [("k", p + 1)] * more + [("O", p, 1), ("OT", p)] + [("V", p + 1)] * more
        if p == 1:
            out += [("gates1_T",)]
        if p % 2:
            out += [("out", p // 2)]
    return out + [("gated",), ("final_T",)]


def stream_u():
    out = []
    for u in range(UNITS):
        out += [("gate", u), ("weight", u)] + ([("down", u - 1)] if u else []) + [("up", u), ("hidden", u)]
    return out + [("down", UNITS - 1)]


STREAMS = {"a": stream_a(), "t": stream_t(), "u": stream_u(),
           "r": [("r1", n) for n in range(R1_CHUNKS)] + [("r0", n) for n in range(R0_CHUNKS)]}
HAM_NAMES = {f"ham{n}" for n in range(HAMS)}
DOES = {
    "pe": {"a": {"ln1_T", "k", "v", "q", "prep_T", "route0", "hart", "proj", "proj_T", "gate_T", "gates0_T", "ln2_T",
                 "fc0", "fc1", "fc2", "fc3", "mproj", "mproj_T"},
           "t": {"xn1_T", "route1", "q", "k", "V", "S", "PT", "O", "OT", "gates1_T", "out", "final_T"},
           "u": {"gate", "weight", "down", "up"}, "r": set()},
    "act": {"a": {"ln1_T", "k", "turn_k", "v", "turn_v", "q", "turn_q", "abs_k", "abs_v", "abs_q", "cos_k", "cos_v", "cos_q",
                  "prep_T", "proj", "gate_T", "gates0_T", "ln2_T", "fc0", "fc1", "fc2", "fc3", "mproj"},
            "t": {"xn1_T", "route1", "V", "S", "PT", "OT", "gates1_T"},
            "u": {"gate", "weight", "down"}, "r": {"r0"}},
    "dve": {"a": {"stats1", "norm1", "ang_k", "ang_v", "ang_q", "prep_stats", "prep_norm", "route0", "hart", "proj_T",
                  "stats2", "norm2", "mproj_T", "join"} | HAM_NAMES,
            "t": {"statsB", "normB", "q", "k", "S", "O", "out", "gated", "final_T"},
            "u": {"hidden"}, "r": {"r0", "r1"}},
    "pool": {"a": {"stats1", "k", "v", "q", "prep_stats", "stats2"}, "t": {"statsB", "q", "k"}, "u": {"weight"}, "r": set()},
}


def has_work(engine, stream, step):
    if step[0] not in DOES[engine][stream]:
        return False
    if step[0] == "weight":
        u = step[1]
        if engine == "pool":
            return u < UNITS - 1
        return u < UNITS - 1 and (u >= UNITS0 or u % HALF0 == 0)
    if engine == "act":
        return step not in [("down", u) for u in range(UNITS) if u not in (UNITS0 - 1, UNITS - 1)] and \
            (step[0] != "r0" or step[1] == 1)
    return True


STEPS_FOR = {e: {k: [t for t in steps if has_work(e, k, t)] for k, steps in STREAMS.items()} for e in DOES}
ORDER = {
    "pe": "uuuautauttatautuuuttuuuututtuuuutuuuttuuuuttatatauututtauuattautauuatutuatuuatutuautautautauuttt"
          "uutuuutttuutuutuututtuuuuautautaututtuuauuatuatauutuauutatuatututuuatuatuautautuuutuuuuttututtuu"
          "uutttututauuauutatattuautauutauuatuutatauutauutuutttuutauuautauautaaaaaaaaaaaaa",
    "act": "uuatuaataaaaaaaatuuaatuttuutuuututatttuauataauattuautuatataataauaaaaautaauttuutttutuuuuuatutuaua"
           "uatatatuuatuuatuaautaaaaaaaatuauattuutuuttuutattuautauauauatutatauutttuutauaaaaaauaaaaaaaraaaaaa"
           "aa",
    "dve": "atatuatrautraaatauatarauaratauatauaratataurattaauattttuuaatuattuatataaauatatauaataatauaaatauatua"
           "ttaauatuttuttuaatatuaatuaaataauaaatatauatatauaatattauaattauttututatautauatuattaaaaaaaaaarararara"
           "aaaaaaaaaaa",
    "pool": "atuuaatatuuutuutuatutuuauaatauutuutuutauutuautauaauututuatutuuuauaaaaa",
}


def take_turns(engine, parts):
    at = dict.fromkeys(parts, 0)
    for k in ORDER[engine]:
        step = STEPS_FOR[engine][k][at[k]]
        at[k] += 1
        if parts[k] is not None:
            parts[k](*step)


A_FILLS = ("ln1_T", "k", "v", "q", "prep_T", "route0", "hart", "proj", "proj_T", "gate_T", "gates0_T", "ln2_T",
           "fc0", "fc1", "fc2", "fc3", "mproj", "mproj_T")
FILL = {step: n for n, step in enumerate(t for t in STREAMS["a"] if t[0] in A_FILLS)}
PREP = ("prep_T", "route0", "gates0_T")
PREP_FILL = {name: n for n, name in enumerate(PREP)}
NFILL, NPREP = len(FILL), len(PREP_FILL)
LN_AT = {step: n for n, step in enumerate(t for t in STREAMS["a"] if t[0] in ("stats1", "stats2", "prep_stats"))}
LNS = len(LN_AT)
STEPS = [t for t in STREAMS["t"] if t[0] not in ("statsB", "normB", "gated")]
STEP_AT = {t: n for n, t in enumerate(STEPS)}
STEPS_OF = [len(STEPS[0::2]), len(STEPS[1::2])]
ROPE_ORDER = [t for t in STEPS if t[0] in "qk"]
ANGLE_ORDER = "kvq"
HAM_OPS = 17
R0_STEPS, R0_TOP, R1_STEPS = 14, 1, 27
PREP_BANKS = 2 + 3 * (PAIR1 // 4) + 3


def program(nc, x, ln1_w, ln1_b, attn_w, attn_b, aproj_w, aproj_b, ln2_w, ln2_b, fc_w, fc_b, mproj_w, mproj_b,
            router_w, w_gate, w_up, w_down, w_qkv, w_out, route_w1, route_b1, gate_w1, up_w1, down_w1,
            sh_gate, sh_up, sh_down, c_ident, c_identb, c_hart, c_cmod, c_cos, c_sin, c_mask, c_sel0, c_sel1,
            c_iota, c_ltri, out):
    fp32, bf16, u32 = mybir.dt.float32, mybir.dt.bfloat16, mybir.dt.uint32
    ALU, ACT, AX = mybir.AluOpType, mybir.ActivationFunctionType, mybir.AxisListType
    ctx = ExitStack()
    with ctx:
        def sb(name, shape, dt=fp32):
            return ctx.enter_context(nc.sbuf_tensor(name, shape, dt))

        def sem(name):
            return ctx.enter_context(nc.semaphore(name))

        w_att = sb("w_att", [P, L, 3, D])
        w_hp = sb("w_hp", [P, L, D])
        w_fc = sb("w_fc", [P, L, FC * D])
        w_mp = sb("w_mp", [P, L, FC, D])
        NCOL = 4 + 3 + FC + 2
        LN1W, LN1B, LN2W, LN2B, AB, FB, PB, MB = 0, 1, 2, 3, 4, 7, 7 + FC, 8 + FC
        cols = sb("cols", [P, NCOL, L])
        w_g0 = sb("w_g0", [P, E0, H0])
        w_u0 = sb("w_u0", [P, E0, H0])
        w_d0 = sb("w_d0", [P, E0, HALF0, D])
        w_r = sb("w_r", [P, E0 + E1])
        w_r0, w_r1 = w_r[:, 0:E0], w_r[:, E0:E0 + E1]
        w_a1 = sb("w_a1", [P, 3 * INNER])
        w_rot = sb("w_rot", [P, 2 * INNER])
        w_o1 = sb("w_o1", [P, HP, D])
        w_g1 = sb("w_g1", [P, PAIR1 + 1, P])
        w_u1 = sb("w_u1", [P, PAIR1 + 1, P])
        w_d1 = sb("w_d1", [P, PAIR1 + 1, D])
        rbias = sb("rbias", [P, E1])
        ident = sb("ident", [P, P])
        identb = sb("identb", [P, P], bf16)
        cmod = sb("cmod", [P, S])
        cosT = sb("cosT", [P, S])
        sinT = sb("sinT", [P, S])
        maskb = sb("maskb", [P, 6 * WIN], bf16)
        sel0 = sb("sel0", [PARTS * E0, E0, P], bf16)
        sel1 = sb("sel1", [PARTS * E1, PAIR1, P], bf16)
        iota = sb("iota", [P, E1])
        ltri = sb("ltri", [P, GROUPS, GROUPS])
        nhalf = sb("nhalf", [P, NT])
        epsT = sb("epsT", [P, NT])
        roundT = sb("roundT", [P, 1])
        scratch = sb("scratch", [P, 1])
        hpi = sb("hpi", [P, 1])
        x_ld = sb("x_ld", [P, NT, D])
        xn = sb("xn", [P, NT, D])
        xr = sb("xr", [P, NT, D])
        xn_f = sb("xn_f", [P, S])
        gates0 = sb("gates0", [PARTS * E0, S], bf16)
        comps = sb("comps", [P, 3, 4, S])
        acc = sb("acc", [P, 4, S])
        tmp = sb("tmp", [P, 2, S])
        gate_f = sb("gate_f", [P, S])
        z, zc, pfm, xf = acc[:, 0, :], acc[:, 1, :], acc[:, 2, :], acc[:, 3, :]
        hid = acc
        ln_hat = tmp[:, 0, :].rearrange("p (t d) -> p t d", t=NT)
        xmul = tmp[:, 1, :].rearrange("p (t d) -> p t d", t=NT)
        stA, mvA = sb("stA", [P, NT, 6]), sb("mvA", [P, NT, 2])
        veA, rsA = sb("veA", [P, NT]), sb("rsA", [P, NT])
        r0_lg = sb("r0_lg", [P, NT, E0])
        r0_top = sb("r0_top", [P, NT, 8])
        r0_idx = sb("r0_idx", [P, NT, 8], u32)
        r0_idf = sb("r0_idf", [P, NT, 8])
        r0_sg = sb("r0_sg", [P, NT, K0])
        r0_sum = sb("r0_sum", [P, NT])
        r0_hit = sb("r0_hit", [P, NT, K0, E0])
        r0_g = sb("r0_g", [P, NT, E0])
        r0_parts = sb("r0_parts", [P, NT, PARTS, E0], bf16)
        x1 = sb("x1", [P, NT, D])
        x1n_f = sb("x1n_f", [P, S])
        Q = sb("Q", [P, S])
        Kk = sb("Kk", [P, WIN + S])
        rot = sb("rot", [P, S])
        V = sb("V", [P, 1 + NW, P])
        probs = sb("probs", [P, 2, NW, 2 * WIN])
        probsT = sb("probsT", [P, 2, 4 * WIN])
        O = sb("O", [P, NW, P])
        OT = sb("OT", [P, 2, S])
        y = sb("y", [P, S])
        nmax = sb("nmax", [P, 2, NW])
        rsum = sb("rsum", [P, NW, 2])
        rinv = sb("rinv", [P, NW, 2])
        s_h = sb("s_h", [P, S])
        ge = sb("ge", [P, S])
        hu = sb("hu", [P, S])
        gate1_f = sb("gate1_f", [P, S])
        gates1 = sb("gates1", [PARTS * E1, S], bf16)
        x1n = rot[:, :].rearrange("p (t d) -> p t d", t=NT)
        y_out = O
        stB, mvB = sb("stB", [P, NT, 6]), sb("mvB", [P, NT, 2])
        veB, rsB = sb("veB", [P, NT]), sb("rsB", [P, NT])
        r1_s = sb("r1_s", [P, NT, E1])
        r1_c = sb("r1_c", [P, NT, E1])
        r1_m8 = sb("r1_m8", [P, NT, GROUPS, 8])
        r1_gs = sb("r1_gs", [P, NT, GROUPS])
        r1_gt = sb("r1_gt", [P, NT, GROUPS, GROUPS])
        r1_eq = sb("r1_eq", [P, NT, GROUPS, GROUPS])
        r1_top = sb("r1_top", [P, NT, 8])
        r1_idx = sb("r1_idx", [P, NT, 8], u32)
        r1_idf = sb("r1_idf", [P, NT, 8])
        r1_hit = y[:, :].rearrange("p (t k e) -> p t k e", t=NT, k=TOPK1)
        r1_sum = sb("r1_sum", [P, NT])
        r1_parts = sb("r1_parts", [P, NT, PARTS, E1], bf16)

        bA = ctx.enter_context(nc.psum_tensor("bA", [P, S], fp32))
        bT = [[ctx.enter_context(nc.psum_tensor(f"bT{i}{j}", [P, S], fp32)) for j in range(2)] for i in range(2)]
        bG = ctx.enter_context(nc.psum_tensor("bG", [P, S], fp32))
        bU = ctx.enter_context(nc.psum_tensor("bU", [P, S], fp32))
        bC = ctx.enter_context(nc.psum_tensor("bC", [P, S], fp32))
        banks = [bA, bT[0][0], bT[0][1], bT[1][0], bT[1][1], bG, bU]

        st_att = comps[:, 0, 0:3, :].rearrange("p a n -> p (a n)").rearrange("p (l n) -> p l n", l=L)
        st_par = comps[0:L, 0, 3, :]
        st_par2 = comps[0:L, 1, 0:3, :].rearrange("p a n -> p (a n)")
        st_g = probs[:, :, :, :].rearrange("p a b n -> p (a b n)").rearrange("p (j n) -> p j n", n=P)
        st_u = acc[:, :, :].rearrange("p a n -> p (a n)").rearrange("p (j n) -> p j n", n=P)
        st_d = comps[:, 2, :, :].rearrange("p a n -> p (a n)")
        st_sh = comps[:, 1, 3, :].rearrange("p (a n) -> p a n", n=P)
        st_r0, st_r1 = tmp[0:E0, 0, 0:P], tmp[0:E1, 0, P:2 * P]
        st_pw = tmp[:, 1, :].rearrange("p (l n) -> p l n", l=L)
        hart_w = sb("hart_w", [P, D])

        loaded = {n: sem("loaded_" + n) for n in ("small", "consts", "attn", "gates", "experts0", "wqkv")}
        set_up = sem("set_up")
        prep_T = sem("prep_T")
        prep_c = sem("prep_c")
        w_perm = sem("w_perm")
        bias_mm = sem("bias_mm")
        folded = sem("folded")
        hp_mm = sem("hp_mm")
        hp_c = sem("hp_c")
        a_full = sem("a_full")
        a_done = sem("a_done")
        lnA_bn, lnA_mv, lnA_rs, lnA_out = sem("lnA_bn"), sem("lnA_mv"), sem("lnA_rs"), sem("lnA_out")
        lnA_ve, lnB_ve = sem("lnA_ve"), sem("lnB_ve")
        lnB_bn, lnB_mv, lnB_rs, lnB_out = sem("lnB_bn"), sem("lnB_mv"), sem("lnB_rs"), sem("lnB_out")
        angled = sem("angled")
        ham = sem("ham")
        rolled_kv, rolled_q = sem("rolled_kv"), sem("rolled_q")
        diffed = sem("diffed")
        turned = sem("turned")
        folded_ang = sem("folded_ang")
        cosined = sem("cosined")
        r0_step, r0_sig, r0_done = sem("r0_step"), sem("r0_sig"), sem("r0_done")
        r1_step, r1_done = sem("r1_step"), sem("r1_done")
        x_in = sem("x_in")
        joined = sem("joined")
        x1_ready = sem("x1_ready")
        t_full = sem("t_full")
        t_done = [sem("t_done0"), sem("t_done1")]
        roped = sem("roped")
        smax = sem("smax")
        rinved = sem("rinved")
        y_gated = sem("y_gated")
        stored = sem("stored")
        g_full, e_full, u_full = sem("g_full"), sem("e_full"), sem("u_full")
        silu = sem("silu")
        ge_sb = sem("ge_sb")
        weighed = sem("weighed")
        h_ready = sem("h_ready")
        c_full = sem("c_full")
        c_done = sem("c_done")

        block = ctx.enter_context(nc.Block())

        class Round:

            def __init__(self, a, b, unit, gel, wei, mix):
                self.a, self.b, self.unit, self.gel, self.wei, self.mix = a, b, unit, gel, wei, mix

        GEL0, GEL1 = E0, PAIR1
        WEI = UNITS0 + PAIR1
        first = Round(0, None, 0, 0, 0, 0)
        last = Round(None, NB - 1, (NB - 1) * UNITS, (NB - 1) * (GEL0 + GEL1), (NB - 1) * WEI, (NB - 1) * 2)

        def middle(i):
            return Round(i, i - 1, i * UNITS - UNITS1, i * (GEL0 + GEL1) - GEL1, i * WEI - PAIR1, i * 2 - 1)

        def fill_no(r, name):
            return r.a * NFILL + (NPREP + FILL[name])

        def a_ready(eng, r, name):
            eng.wait_ge(a_full, fill_no(r, name) + 1)

        def a_ended(eng, r, name):
            eng.wait_ge(a_done, fill_no(r, name) + 1)

        def t_set(t):
            return bT[STEP_AT[t] % 2]

        def t_ready(eng, r, t):
            eng.wait_ge(t_full, r.b * len(STEPS) + (STEP_AT[t] + 1))

        def t_sem(t):
            return t_done[STEP_AT[t] % 2]

        def t_ended(eng, r, t):
            n = STEP_AT[t]
            eng.wait_ge(t_done[n % 2], r.b * STEPS_OF[n % 2] + (n // 2 + 2))

        def t_begin(eng, r, t, *earlier):
            n = STEP_AT[t]
            eng.wait_ge(t_done[n % 2], r.b * STEPS_OF[n % 2] + (n // 2 + 1))
            other = [STEP_AT[e] for e in earlier if STEP_AT[e] % 2 != n % 2]
            if other:
                t_ended(eng, r, STEPS[max(other)])

        def ham_no(r, l, n):
            return r.a * (L * HAM_OPS) + (l * HAM_OPS + n)

        def angle_no(r, l, n):
            return r.a * (L * 3) + (l * 3 + n)

        def ln_no(r, name):
            return r.a * LNS + (1 + LN_AT[name])

        def unit_kind(u):
            if u < UNITS0:
                e, half = u // HALF0, u % HALF0
                c = slice(half * P, half * P + P)
                return w_g0[:, e, c], w_u0[:, e, c], w_d0[:, e, half, :], (sel0[:, e, :] if half == 0 else None), e
            j = u - UNITS0
            return w_g1[:, j, :], w_u1[:, j, :], w_d1[:, j, :], (sel1[:, j, :] if j < PAIR1 else None), GEL0 + j

        def has_weight(u):
            return u < UNITS - 1

        def units_of(r):
            return range(0 if r.a is not None else UNITS0, UNITS if r.b is not None else UNITS0)

        def rounds(eng, one):
            one(first)
            with eng.Fori(1, NB) as i:
                one(middle(i))
            one(last)

        def streams(r, a=None, t=None, u=None, rt=None):
            units = units_of(r)

            def u_part(name, n):
                if n in units:
                    u(name, n)

            def r_part(name, n):
                if (r.a if name == "r0" else r.b) is not None:
                    rt(name, n)

            return {"a": a if r.a is not None else None, "t": t if r.b is not None else None, "u": u_part, "r": r_part}

        def gates0_no(r):
            return NPREP if r is first else r.a * NFILL + (NPREP - NFILL + FILL[("gates0_T", L - 1)] + 1)

        def prep_sources():
            rows = [st_par[:, n * D:(n + 1) * D] for n in range(4)] + \
                   [st_par2[:, n * D:(n + 1) * D] for n in range(NCOL - 4)]
            out = [rows, [st_r0, st_r1]]
            for st in (st_g, st_u):
                out += [[st[:, 4 * g + k, :] for k in range(4)] for g in range(PAIR1 // 4)]
            out += [[st_d[:, (4 * g + k) * P:(4 * g + k + 1) * P] for k in range(4)] for g in range(PAIR1 // 4)]
            return out + [[st_sh[:, n, :]] for n in range(3)]

        def prep_targets():
            out = [(cols[:, :, :], NCOL * L, NCOL), (w_r[:, :], E0 + E1, None)]
            for w in (w_g1, w_u1, w_d1):
                out += [(w[:, 4 * g:4 * g + 4, :], 4 * P, 4) for g in range(PAIR1 // 4)]
            return out + [(w[:, PAIR1, :], P, None) for w in (w_g1, w_u1, w_d1)]

        @block.sync
        def _(sp):
            def load(dst, src, s, n=1):
                sp.dma_start(dst, src).then_inc(s, 16)

            load(x_ld[:, :, :], x[0].rearrange("(t p) d -> p t d", p=P), x_in)
            sm = loaded["small"]
            for n, src in enumerate((ln1_w, ln1_b, ln2_w, ln2_b)):
                load(st_par[:, n * D:(n + 1) * D], src, sm)
            for n in range(3):
                load(st_par2[:, n * D:(n + 1) * D].rearrange("l (h d) -> l h d", h=H),
                     attn_b.rearrange("l (h t d) -> l h t d", h=H, t=3)[:, :, n, :], sm)
            load(st_par2[:, 3 * D:3 * D + FC * D], fc_b, sm)
            load(st_par2[:, 7 * D:8 * D], aproj_b, sm)
            load(st_par2[:, 8 * D:9 * D], mproj_b, sm)
            load(ident[:, :], c_ident, sm)
            load(st_r0, router_w, sm)
            load(st_r1, route_w1, sm)
            load(hart_w[:, :], c_hart, sm)
            load(st_pw, aproj_w.rearrange("l k n -> k l n"), sm)
            load(st_att, attn_w.rearrange("l k n -> k l n"), loaded["attn"])
            load(w_fc[:, :, :], fc_w.rearrange("l k n -> k l n"), loaded["attn"])
            load(st_g, gate_w1.rearrange("(j e) i h -> (e i) j h", j=PAIR1), loaded["gates"])
            load(st_u, up_w1.rearrange("(j e) i h -> (e i) j h", j=PAIR1), loaded["gates"])
            load(st_d.rearrange("p (e i) -> p e i", e=E1), down_w1.rearrange("e h i -> h e i"), loaded["gates"])
            for n, src in enumerate((sh_gate, sh_up, sh_down)):
                load(st_sh[:, n, :], src, loaded["gates"])
            load(w_g0[:, :, :], w_gate.rearrange("e k n -> k e n"), loaded["experts0"])
            load(w_u0[:, :, :], w_up.rearrange("e k n -> k e n"), loaded["experts0"])
            load(w_d0[:, :, :, :], w_down.rearrange("e (a p) n -> p e a n", p=P), loaded["experts0"])
            load(w_a1[:, :], w_qkv, loaded["wqkv"])
            cs = loaded["consts"]
            load(identb[:, :], c_identb, cs)
            load(cmod[:, :], c_cmod, cs)
            load(cosT[:, :], c_cos, cs)
            load(sinT[:, :], c_sin, cs)
            load(maskb[:, :], c_mask, cs)
            load(sel0[:, :, :], c_sel0, cs)
            load(sel1[:, :, :], c_sel1, cs)
            load(iota[:, :], c_iota, cs)
            load(ltri[:, :, :], c_ltri, cs)
            load(rbias[:, :], route_b1.unsqueeze(0).to_broadcast([P, E1]), cs)
            load(w_mp[:, :, :, :], mproj_w.rearrange("l (a p) n -> p l a n", p=P), cs)
            load(w_o1[:, :, :], w_out.rearrange("(a p) n -> p a n", p=P), cs)

            def one(r):
                if r.a is not None:
                    if r is first:
                        sp.wait_ge(lnA_out, 1)
                    else:
                        sp.wait_ge(x1_ready, r.a)
                    nxt = (r.a + 1) % NB
                    sp.dma_start(x_ld[:, :, :], x[nxt].rearrange("(t p) d -> p t d", p=P)).then_inc(x_in, 16)
                    for l in range(L):
                        for name in ANGLE_ORDER:
                            n, done = "qkv".index(name), rolled_q if name == "q" else rolled_kv
                            a_ended(sp, r, (name, l))
                            sp.dma_start(comps[HD:P, n, 2, :], comps[0:P - HD, n, 0, :]).then_inc(done, 16)
                            sp.dma_start(comps[0:HD, n, 2, :], comps[P - HD:P, n, 0, :]).then_inc(done, 16)
                    sp.wait_ge(lnA_out, ln_no(r, ("prep_stats", L - 1)) + 1)
                    sp.dma_start(x_ld[:, :, :], x[r.a].rearrange("(t p) d -> p t d", p=P)).then_inc(x_in, 16)
                if r.b is not None:
                    t_ended(sp, r, ("final_T",))
                    sp.dma_start(out[r.b].rearrange("(t p) d -> p t d", p=P), y_out[:, :, :]).then_inc(stored, 16)

            rounds(sp, one)
            sp.wait_ge(stored, (NB + 1) * 16)

        @block.gpsimd
        def _(pool):
            nc.gpsimd.memset(nhalf[:, :], -0.5).then_inc(t_done[0], 1)
            nc.gpsimd.memset(epsT[:, :], EPS).then_inc(t_done[1], 1)
            nc.gpsimd.memset(hpi[:, :], math.pi / 2).then_inc(roped, 1)
            nc.gpsimd.memset(roundT[:, :], ROUND).then_inc(h_ready, 1)
            nc.gpsimd.memset(Kk[:, 0:WIN], 0.0).then_inc(stored, 16)
            nc.gpsimd.memset(V[:, 0, :], 0.0).then_inc(set_up, 1)
            pool.wait_ge(prep_T, PREP_BANKS)
            pool.wait_ge(w_perm, 1)
            nc.gpsimd.memset(comps[:, :, 1, 0:1], 0.0).then_inc(set_up, 1)
            pool.wait_ge(set_up, 2)

            def rstd(mv, ve, rs, mv_sem, ve_sem, rs_sem, n):
                pool.wait_ge(mv_sem, n + 1)
                nc.gpsimd.tensor_tensor(ve[:, :], mv[:, :, 1], epsT[:, :], ALU.add).then_inc(ve_sem, 1)
                pool.wait_ge(ve_sem, n + 1)
                nc.gpsimd.tensor_tensor(rs[:, :], ve[:, :], nhalf[:, :], ALU.pow).then_inc(rs_sem, 1)

            rstd(mvA, veA, rsA, lnA_mv, lnA_ve, lnA_rs, 0)

            def one(r):
                def a_part(name, l):
                    if name in ("stats1", "stats2", "prep_stats"):
                        rstd(mvA, veA, rsA, lnA_mv, lnA_ve, lnA_rs, ln_no(r, (name, l)))
                    if name in ("q", "k", "v"):
                        a_ended(pool, r, (name, l))
                        c = comps[:, "qkv".index(name), :, :]
                        nc.gpsimd.tensor_tensor(c[:, 1, 1:S], c[:, 0, 1:S], c[:, 0, 0:S - 1],
                                                ALU.subtract).then_inc(diffed, 1)

                def t_part(*t):
                    if t[0] == "statsB":
                        rstd(mvB, veB, rsB, lnB_mv, lnB_ve, lnB_rs, r.b)
                    if t[0] in "qk":
                        dst = Q[:, :] if t[0] == "q" else Kk[:, WIN:]
                        t_ended(pool, r, t)
                        nc.gpsimd.tensor_tensor(dst, dst, rot[:, :], ALU.add).then_inc(roped, 1)

                def u_part(name, u):
                    pool.wait_ge(silu, r.unit + (u + 1))
                    pool.wait_ge(ge_sb, r.gel + (unit_kind(u)[4] + 1))
                    nc.gpsimd.tensor_tensor(s_h[:, :], s_h[:, :], ge[:, :], ALU.mult).then_inc(weighed, 1)

                take_turns("pool", streams(r, a_part, t_part, u_part))

            rounds(pool, one)

        @block.scalar
        def _(act):
            def copy(dst, src):
                return nc.scalar.activation(dst, src, ACT.Copy)

            for n, (dst, width, shape) in enumerate(prep_targets()):
                act.wait_ge(prep_T, n + 1)
                copy(dst, banks[n % len(banks)][:, 0:width] if shape is None else
                     banks[n % len(banks)][:, 0:width].rearrange("p (a n) -> p a n", a=shape)).then_inc(prep_c, 1)
            act.wait_ge(hp_mm, 1)
            copy(w_hp[:, :, :], bC[:, :].rearrange("p (l n) -> p l n", l=L)).then_inc(hp_c, 1)

            def prep_copy(ready):
                ready(act, "prep_T")
                copy(xn_f[:, :], bA[:, :]).then_inc(a_done, 1)

            def prep_sig(n):
                act.wait_ge(r0_step, n)
                nc.scalar.activation(r0_sg[:, :, :], r0_top[:, :, 0:K0], ACT.Sigmoid).then_inc(r0_sig, 1)

            def prep_gates(ready):
                ready(act, "gates0_T")
                copy(gates0[:, :], bA[:, :].bitcast(bf16)[0:PARTS * E0, 0:S]).then_inc(a_done, 1)

            def prep_ready(e, name):
                e.wait_ge(a_full, PREP_FILL[name] + 1)

            prep_copy(prep_ready)
            prep_sig(R0_TOP)
            prep_gates(prep_ready)

            def one(r):
                def ready(e, name):
                    a_ready(e, r, (name, L - 1))

                def a_part(name, l):
                    n = "qkv".find(name[-1])
                    if name in ("ln1_T", "ln2_T"):
                        a_ready(act, r, (name, l))
                        copy(xf, bA[:, :]).then_inc(a_done, 1)
                    if name in ("q", "k", "v"):
                        a_ready(act, r, (name, l))
                        nc.scalar.activation(comps[:, n, 0, :], bA[:, :], ACT.Identity,
                                             bias=cols[:, AB + n, l:l + 1]).then_inc(a_done, 1)
                    if name in ("turn_q", "turn_k", "turn_v"):
                        a_ended(act, r, (name[-1], l))
                        nc.scalar.activation(comps[:, n, 3, :], comps[:, n, 0, :], ACT.Identity, bias=roundT[:, 0:1],
                                             scale=1.0 / TWO_PI).then_inc(turned, 1)
                    if name in ("abs_q", "abs_k", "abs_v"):
                        act.wait_ge(angled, 2 * angle_no(r, l, ANGLE_ORDER.index(name[-1]) + 1))
                        nc.scalar.activation(comps[:, n, 3, :], comps[:, n, 3, :], ACT.Abs).then_inc(folded_ang, 1)
                    if name in ("cos_q", "cos_k", "cos_v"):
                        act.wait_ge(folded_ang, angle_no(r, l, ANGLE_ORDER.index(name[-1]) + 1))
                        nc.scalar.activation(comps[:, n, 3, :], comps[:, n, 3, :], ACT.Sin, bias=hpi[:, 0:1],
                                             scale=-1.0).then_inc(cosined, 1)
                    if name in ("proj", "mproj"):
                        a_ready(act, r, (name, l))
                        b = PB if name == "proj" else MB
                        nc.scalar.activation(pfm, bA[:, :], ACT.Identity,
                                             bias=cols[:, b, l:l + 1]).then_inc(a_done, 1)
                    if name in ("fc0", "fc1", "fc2", "fc3"):
                        j = int(name[2])
                        a_ready(act, r, (name, l))
                        nc.scalar.activation(hid[:, j, :], bA[:, :], ACT.Gelu,
                                             bias=cols[:, FB + j, l:l + 1]).then_inc(a_done, 1)
                    if name == "gate_T":
                        a_ready(act, r, (name, l))
                        copy(gate_f[:, :], bA[:, :]).then_inc(a_done, 1)
                    if name == "prep_T":
                        prep_copy(ready)
                    if name == "gates0_T":
                        prep_gates(ready)

                def r_part(name, n):
                    prep_sig((r.a + 1) * R0_STEPS + R0_TOP)

                def t_part(*t):
                    b = t_set(t)
                    if t[0] == "xn1_T":
                        t_ready(act, r, t)
                        copy(x1n_f[:, :], b[0][:, :]).then_inc(t_sem(t), 1)
                    if t[0] == "route1":
                        t_ready(act, r, t)
                        nc.scalar.activation(r1_s[:, :, :], b[0][:, 0:NT * E1].rearrange("p (t e) -> p t e", t=NT),
                                             ACT.Sigmoid).then_inc(t_sem(t), 1)
                    if t[0] == "V":
                        t_ready(act, r, t)
                        copy(V[:, 1:, :], b[0][:, :].rearrange("p (w n) -> p w n", w=NW)).then_inc(t_sem(t), 1)
                    if t[0] == "S":
                        n = 2 * t[1] + t[2] + 1
                        act.wait_ge(smax, r.b * (2 * HP) + n)
                        for h in range(2):
                            for w in range(2):
                                ww = 2 * t[2] + w
                                ins = nc.scalar.activation(probs[:, h, ww, :], b[h][:, w * 2 * WIN:(w + 1) * 2 * WIN],
                                                           ACT.Exp, bias=nmax[:, h, ww:ww + 1],
                                                           accum_out=rsum[:, ww, h:h + 1])
                        ins.then_inc(t_sem(t), 1)
                    if t[0] == "PT":
                        t_ready(act, r, t)
                        copy(probsT[:, 0, :], b[0][:, :])
                        copy(probsT[:, 1, :], b[1][:, :]).then_inc(t_sem(t), 1)
                    if t[0] == "OT":
                        t_ready(act, r, t)
                        copy(OT[:, t[1] % 2, :], b[0][:, :]).then_inc(t_sem(t), 1)
                    if t[0] == "gates1_T":
                        t_ready(act, r, t)
                        copy(gates1[:, :], b[0][:, :].bitcast(bf16)[0:PARTS * E1, 0:S]).then_inc(t_sem(t), 1)

                def mixture(n, dst):
                    act.wait_ge(c_full, r.mix + (n + 1))
                    nc.scalar.activation(dst, bC[:, :], ACT.Silu).then_inc(c_done, 1)

                def u_part(name, u):
                    g = unit_kind(u)[4]
                    if name == "gate":
                        act.wait_ge(g_full, r.unit + (u + 1))
                        act.wait_ge(h_ready, r.unit + (u + 1))
                        nc.scalar.activation(s_h[:, :], bG[:, :], ACT.Silu).then_inc(silu, 1)
                    if name == "weight":
                        act.wait_ge(e_full, r.gel + (g + 1))
                        copy(ge[:, :], bU[:, :]).then_inc(ge_sb, 1)
                    if name == "down":
                        if u == UNITS0 - 1:
                            mixture(0, gate_f[:, :])
                        else:
                            mixture(1, gate1_f[:, :])

                take_turns("act", streams(r, a_part, t_part, u_part, r_part))

            rounds(act, one)

        @block.vector
        def _(dve):
            V_ = nc.vector

            def settled():
                V_.memset(scratch[:, :], 0.0)

            def stats(src, st, mv, bn_s, mv_s, n):
                for t in range(NT):
                    ins = V_.bn_stats(st[:, t, :], src[:, t, :])
                ins.then_inc(bn_s, 1)
                dve.wait_ge(bn_s, n + 1)
                settled()
                for t in range(NT):
                    ins = V_.bn_aggr(mv[:, t, :], st[:, t, :])
                ins.then_inc(mv_s, 1)

            def normalise(src, dst, mv, rs, mv_s, rs_s, out_s, n):
                dve.wait_ge(mv_s, n + 1)
                dve.wait_ge(rs_s, n + 1)
                for t in range(NT):
                    ins = V_.tensor_scalar(dst[:, t, :], src[:, t, :], mv[:, t, 0:1], rs[:, t:t + 1],
                                           ALU.subtract, ALU.mult)
                ins.then_inc(out_s, 1)

            def stats_a(src, n):
                stats(src, stA, mvA, lnA_bn, lnA_mv, n)

            def normalise_a(src, dst, n):
                normalise(src, dst, mvA, rsA, lnA_mv, lnA_rs, lnA_out, n)

            def linker(s, base, start):
                n = [start]

                def link(ins, alone=False, end=False):
                    n[0] += 1
                    ins.then_inc(s, 1)
                    if not end:
                        dve.wait_ge(s, base + n[0])
                        if alone:
                            settled()
                return link

            def split(link, g, parts, done):
                for k in range(PARTS):
                    ins = V_.tensor_copy(parts[:, :, k, :], g)
                    if k == PARTS - 1:
                        ins.then_inc(done, 1)
                    else:
                        link(ins)
                        link(V_.tensor_tensor(g, g, parts[:, :, k, :], ALU.subtract))

            def route0(ready):
                ready(dve, "route0")
                V_.tensor_copy(r0_lg[:, :, :], bA[:, 0:NT * E0].rearrange("p (t e) -> p t e", t=NT)).then_inc(a_done, 1)

            def route0_chunk(k, base, sig_n, copied):
                start = (0, 1, 4, 9)[k]
                link = linker(r0_step, base, start)
                if k == 0:
                    dve.wait_ge(a_done, copied)
                    settled()
                    for t in range(NT):
                        ins = V_.max(r0_top[:, t, :], r0_lg[:, t, :])
                    link(ins, end=True)
                    return
                dve.wait_ge(r0_step, base + start)
                if k == 1:
                    settled()
                    for t in range(NT):
                        ins = V_.max_index(r0_idx[:, t, :], r0_top[:, t, :], r0_lg[:, t, :])
                    link(ins)
                    link(V_.tensor_copy(r0_idf[:, :, :], r0_idx[:, :, :]))
                    link(V_.tensor_tensor(r0_hit[:, :, :, :], iota[:, 0:E0].unsqueeze(1).unsqueeze(1).to_broadcast([P, NT, K0, E0]),
                                          r0_idf[:, :, 0:K0].unsqueeze(3).to_broadcast([P, NT, K0, E0]), ALU.is_equal), end=True)
                if k == 2:
                    dve.wait_ge(r0_sig, sig_n)
                    link(V_.tensor_reduce(r0_sum[:, :], r0_sg[:, :, :], AX.X, ALU.add))
                    link(V_.tensor_scalar(r0_sum[:, :], r0_sum[:, :], 1e-10, None, ALU.add))
                    link(V_.reciprocal(r0_sum[:, :], r0_sum[:, :]))
                    link(V_.tensor_tensor(r0_sg[:, :, :], r0_sg[:, :, :], r0_sum[:, :].unsqueeze(2).to_broadcast([P, NT, K0]), ALU.mult))
                    link(V_.tensor_tensor(r0_hit[:, :, :, :], r0_hit[:, :, :, :],
                                          r0_sg[:, :, :].unsqueeze(3).to_broadcast([P, NT, K0, E0]), ALU.mult), end=True)
                if k == 3:
                    link(V_.tensor_tensor(r0_g[:, :, :], r0_hit[:, :, 0, :], r0_hit[:, :, 1, :], ALU.add))
                    split(link, r0_g[:, :, :], r0_parts, r0_done)

            dve.wait_ge(loaded["attn"], 32)
            for l in range(L):
                ins = V_.tensor_copy(w_att[:, l, :, :].rearrange("p t (h d) -> p t h d", h=H),
                                     st_att[:, l, :].rearrange("p (h t d) -> p t h d", h=H, t=3))
            ins.then_inc(w_perm, 1)
            dve.wait_ge(loaded["wqkv"], 16)
            V_.tensor_scalar(w_a1[:, 0:INNER], w_a1[:, 0:INNER], DH ** -0.5, None, ALU.mult).then_inc(folded, 1)
            dve.wait_ge(folded, 1)
            V_.tensor_copy(w_rot[:, :].rearrange("p (h a d) -> p h a d", a=2, d=DH // 2),
                           w_a1[:, 0:2 * INNER].rearrange("p (h a d) -> p h a d", a=2, d=DH // 2)[:, :, ::-1, :])
            dve.wait_ge(prep_c, PREP_BANKS)
            dve.wait_ge(bias_mm, 1)
            nb = L * (3 + FC)
            V_.tensor_tensor(cols[:, AB:AB + 3 + FC, :], cols[:, AB:AB + 3 + FC, :],
                             bC[:, 0:nb].rearrange("p (n l) -> p n l", l=L), ALU.add)
            for l in range(L):
                V_.tensor_scalar(w_att[:, l, :, :], w_att[:, l, :, :], cols[:, LN1W, l:l + 1], None, ALU.mult)
                ins = V_.tensor_scalar(w_fc[:, l, :], w_fc[:, l, :], cols[:, LN2W, l:l + 1], None, ALU.mult)
            ins.then_inc(folded, 1)
            dve.wait_ge(loaded["consts"], 16 * 12)
            dve.wait_ge(x_in, 16)
            stats_a(x_ld, 0)
            normalise_a(x_ld, xn, 0)

            def prep_ready(e, name):
                e.wait_ge(a_full, PREP_FILL[name] + 1)

            route0(prep_ready)
            for k in range(R0_CHUNKS):
                route0_chunk(k, 0, 1, PREP_FILL["route0"] + 1)

            def angle(r, l, name):
                n, no = "qkv".index(name), angle_no(r, l, ANGLE_ORDER.index(name))
                dve.wait_ge(turned, no + 1)
                V_.tensor_scalar(comps[:, n, 3, :], comps[:, n, 3, :], ROUND, TWO_PI, ALU.subtract, ALU.mult).then_inc(angled, 1)
                dve.wait_ge(angled, 2 * no + 1)
                V_.tensor_tensor(comps[:, n, 3, :], comps[:, n, 0, :], comps[:, n, 3, :], ALU.subtract).then_inc(angled, 1)

            def quaternions(r, l, k):
                a, b, c = comps[:, 0], comps[:, 1], comps[:, 2]

                def many(k, n):
                    return b[:, k:k + 1, :].to_broadcast([P, n, S])

                def tt(n, dst, i0, i1, op):
                    if n > 1:
                        dve.wait_ge(ham, ham_no(r, l, n - 1))
                    V_.tensor_tensor(dst, i0, i1, op).then_inc(ham, 1)

                if k == 0:
                    dve.wait_ge(cosined, angle_no(r, l, 2))
                    dve.wait_ge(diffed, angle_no(r, l, 2))
                    dve.wait_ge(rolled_kv, 32 * (r.a * (2 * L) + (2 * l + 2)))
                    tt(1, acc[:, :, :], many(0, 4), c, ALU.mult)
                if k == 1:
                    tt(2, tmp[:, :, :], many(1, 2), c[:, 1::2, :], ALU.mult)
                if k == 2:
                    tt(3, acc[:, 0::2, :], acc[:, 0::2, :], tmp[:, :, :], ALU.subtract)
                if k == 3:
                    tt(4, tmp[:, :, :], many(1, 2), c[:, 0::2, :], ALU.mult)
                if k == 4:
                    tt(5, acc[:, 1::2, :], acc[:, 1::2, :], tmp[:, :, :], ALU.add)
                if k == 5:
                    tt(6, tmp[:, :, :], many(2, 2), c[:, 2:0:-1, :], ALU.mult)
                if k == 6:
                    tt(7, acc[:, 0::3, :], acc[:, 0::3, :], tmp[:, :, :], ALU.subtract)
                if k == 7:
                    tt(8, tmp[:, :, :], many(2, 2), c[:, 3::-3, :], ALU.mult)
                if k == 8:
                    tt(9, acc[:, 1:3, :], acc[:, 1:3, :], tmp[:, :, :], ALU.add)
                if k == 9:
                    tt(10, tmp[:, :, :], many(3, 2), c[:, 3:1:-1, :], ALU.mult)
                if k == 10:
                    tt(11, acc[:, 0:2, :], acc[:, 0:2, :], tmp[:, :, :], ALU.subtract)
                if k == 11:
                    tt(12, tmp[:, :, :], many(3, 2), c[:, 1::-1, :], ALU.mult)
                if k == 12:
                    tt(13, acc[:, 2:4, :], acc[:, 2:4, :], tmp[:, :, :], ALU.add)
                if k == 13:
                    dve.wait_ge(cosined, angle_no(r, l, 3))
                    dve.wait_ge(diffed, angle_no(r, l, 3))
                    dve.wait_ge(rolled_q, 32 * (r.a * L + (l + 1)))
                    tt(14, acc[:, :, :], a, acc[:, :, :], ALU.mult)
                if k == 14:
                    tt(15, tmp[:, 0, :], acc[:, 0, :], acc[:, 1, :], ALU.subtract)
                    tt(16, tmp[:, 1, :], acc[:, 2, :], acc[:, 3, :], ALU.add)
                    tt(17, z, tmp[:, 0, :], tmp[:, 1, :], ALU.subtract)

            def route1_chunk(k, r):
                start = (0, 2, 9, 12, 17, 23)[k]
                link = linker(r1_step, r.b * R1_STEPS, start)
                if k == 0:
                    t_ended(dve, r, ("route1",))
                    link(V_.tensor_tensor(r1_c[:, :, :], r1_s[:, :, :], rbias[:, :].unsqueeze(1).to_broadcast([P, NT, E1]), ALU.add), True)
                    for t in range(NT):
                        for g in range(GROUPS):
                            ins = V_.max(r1_m8[:, t, g, :], r1_c[:, t, g * EG:(g + 1) * EG])
                    link(ins, end=True)
                    return
                dve.wait_ge(r1_step, r.b * R1_STEPS + start)
                if k == 1:
                    link(V_.tensor_tensor(r1_gs[:, :, :], r1_m8[:, :, :, 0], r1_m8[:, :, :, 1], ALU.add))
                    other = r1_gs[:, :, :].unsqueeze(2).to_broadcast([P, NT, GROUPS, GROUPS])
                    mine = r1_gs[:, :, :].unsqueeze(3).to_broadcast([P, NT, GROUPS, GROUPS])
                    link(V_.tensor_tensor(r1_gt[:, :, :, :], other, mine, ALU.is_gt))
                    link(V_.tensor_tensor(r1_eq[:, :, :, :], other, mine, ALU.is_equal))
                    link(V_.tensor_tensor(r1_eq[:, :, :, :], r1_eq[:, :, :, :],
                                          ltri[:, :, :].unsqueeze(1).to_broadcast([P, NT, GROUPS, GROUPS]), ALU.mult))
                    link(V_.tensor_tensor(r1_gt[:, :, :, :], r1_gt[:, :, :, :], r1_eq[:, :, :, :], ALU.add))
                    link(V_.tensor_reduce(r1_gs[:, :, :], r1_gt[:, :, :, :], AX.X, ALU.add))
                    link(V_.tensor_scalar(r1_gs[:, :, :], r1_gs[:, :, :], float(TOPG), None, ALU.is_lt), end=True)
                if k == 2:
                    by_group = r1_c[:, :, :].rearrange("p t (g e) -> p t g e", g=GROUPS)
                    link(V_.tensor_tensor(by_group, by_group, r1_gs[:, :, :].unsqueeze(3).to_broadcast([P, NT, GROUPS, EG]), ALU.mult))
                    link(V_.tensor_scalar(r1_c[:, :, :], r1_c[:, :, :], 0.0, None, ALU.add), True)
                    for t in range(NT):
                        ins = V_.max(r1_top[:, t, :], r1_c[:, t, :])
                    link(ins, end=True)
                if k == 3:
                    settled()
                    for t in range(NT):
                        ins = V_.max_index(r1_idx[:, t, :], r1_top[:, t, :], r1_c[:, t, :])
                    link(ins)
                    link(V_.tensor_copy(r1_idf[:, :, :], r1_idx[:, :, :]))
                    link(V_.tensor_tensor(r1_hit, iota[:, :].unsqueeze(1).unsqueeze(1).to_broadcast([P, NT, TOPK1, E1]),
                                          r1_idf[:, :, 0:TOPK1].unsqueeze(3).to_broadcast([P, NT, TOPK1, E1]), ALU.is_equal))
                    link(V_.tensor_tensor(r1_hit[:, :, 0:2, :], r1_hit[:, :, 0:2, :], r1_hit[:, :, 2:4, :], ALU.add))
                    link(V_.tensor_tensor(r1_c[:, :, :], r1_hit[:, :, 0, :], r1_hit[:, :, 1, :], ALU.add), end=True)
                if k == 4:
                    link(V_.tensor_tensor(r1_s[:, :, :], r1_s[:, :, :], r1_c[:, :, :], ALU.mult))
                    link(V_.tensor_reduce(r1_sum[:, :], r1_s[:, :, :], AX.X, ALU.add))
                    link(V_.tensor_scalar(r1_sum[:, :], r1_sum[:, :], 1e-20, None, ALU.add))
                    link(V_.reciprocal(r1_sum[:, :], r1_sum[:, :]))
                    link(V_.tensor_scalar(r1_sum[:, :], r1_sum[:, :], SCALE1, None, ALU.mult))
                    link(V_.tensor_tensor(r1_s[:, :, :], r1_s[:, :, :], r1_sum[:, :].unsqueeze(2).to_broadcast([P, NT, E1]), ALU.mult), end=True)
                if k == 5:
                    split(link, r1_s[:, :, :], r1_parts, r1_done)

            def one(r):
                def a_part(name, l):
                    if name in ("stats1", "stats2", "prep_stats"):
                        if name == "prep_stats":
                            dve.wait_ge(x_in, r.a * 32 + 32)
                        src = x_ld if name == "prep_stats" else xn if name == "stats1" and l == 0 else xr
                        if src is xr:
                            a_ended(dve, r, ("proj_T", l) if name == "stats2" else ("mproj_T", l - 1))
                        stats_a(src, ln_no(r, (name, l)))
                    if name in ("norm1", "norm2"):
                        normalise_a(xn if name == "norm1" and l == 0 else xr, ln_hat, ln_no(r, ("stats" + name[-1], l)))
                    if name == "prep_norm":
                        normalise_a(x_ld, xn, ln_no(r, ("prep_stats", l)))
                    if name == "route0":
                        route0(lambda e, n: a_ready(e, r, (n, L - 1)))
                    if name in ("ang_k", "ang_v", "ang_q"):
                        angle(r, l, name[-1])
                    if name in HAM_NAMES:
                        quaternions(r, l, int(name[3:]))
                    if name == "hart":
                        a_ready(dve, r, (name, l))
                        V_.tensor_tensor(zc, bA[:, :], cmod[:, :], ALU.mult).then_inc(a_done, 1)
                    if name in ("proj_T", "mproj_T"):
                        a_ready(dve, r, (name, l))
                        src = xn if name == "proj_T" and l == 0 else xr
                        V_.tensor_tensor(xr[:, :, :], bA[:, :].rearrange("p (t d) -> p t d", t=NT), src[:, :, :],
                                         ALU.add).then_inc(a_done, 1)
                    if name == "join":
                        a_ended(dve, r, ("gate_T", L - 2))
                        a_ended(dve, r, ("mproj_T", L - 1))
                        V_.tensor_tensor(xmul, gate_f[:, :].rearrange("p (t d) -> p t d", t=NT), xr[:, :, :],
                                         ALU.mult).then_inc(joined, 1)
                        dve.wait_ge(joined, r.a + 1)
                        dve.wait_ge(x_in, r.a * 32 + 48)
                        V_.tensor_tensor(x1[:, :, :], xmul, x_ld[:, :, :], ALU.add).then_inc(x1_ready, 1)

                def t_part(*t):
                    if t[0] == "statsB":
                        dve.wait_ge(x1_ready, r.b + 1)
                        stats(x1, stB, mvB, lnB_bn, lnB_mv, r.b)
                    if t[0] == "normB":
                        normalise(x1, x1n, mvB, rsB, lnB_mv, lnB_rs, lnB_out, r.b)
                    b = t_set(t) if t in STEP_AT else None
                    if t[0] in "qk":
                        n = ROPE_ORDER.index(t)
                        dst = Q[:, :] if t[0] == "q" else Kk[:, WIN:]
                        t_ready(dve, r, t)
                        V_.tensor_tensor(dst, b[0][:, :], cosT[:, :], ALU.mult)
                        dve.wait_ge(roped, r.b * len(ROPE_ORDER) + (n + 1))
                        V_.tensor_tensor(rot[:, :], b[1][:, :], sinT[:, :], ALU.mult).then_inc(t_sem(t), 1)
                    if t[0] == "S":
                        t_ready(dve, r, t)
                        for h in range(2):
                            ins = V_.tensor_reduce(nmax[:, h, 2 * t[2]:2 * t[2] + 2],
                                                   b[h][:, :].rearrange("p (w n) -> p w n", w=2), AX.X, ALU.max,
                                                   negate=True)
                        ins.then_inc(smax, 1)
                    if t[0] == "O":
                        n = 2 * t[1] + t[2] + 1
                        w = slice(2 * t[2], 2 * t[2] + 2)
                        t_ended(dve, r, ("S", t[1], t[2]))
                        if (t[1], t[2]) == (0, 0):
                            dve.wait_ge(stored, r.b * 16 + 16)
                        V_.reciprocal(rinv[:, w, :], rsum[:, w, :]).then_inc(rinved, 1)
                        dve.wait_ge(rinved, r.b * (2 * HP) + n)
                        t_ready(dve, r, t)
                        V_.tensor_tensor(O[:, w, :].rearrange("p w (h d) -> p w h d", h=2),
                                         b[0][:, 0:2 * P].rearrange("p (w h d) -> p w h d", w=2, h=2),
                                         rinv[:, w, :].unsqueeze(3).to_broadcast([P, 2, 2, DH]),
                                         ALU.mult).then_inc(t_sem(t), 1)
                    if t[0] == "out":
                        l = t[1]
                        t_ready(dve, r, t)
                        if l == 0:
                            V_.tensor_copy(y[:, :], b[0][:, :]).then_inc(t_sem(t), 1)
                        else:
                            t_ended(dve, r, ("out", l - 1))
                            V_.tensor_tensor(y[:, :], b[0][:, :], y[:, :], ALU.add).then_inc(t_sem(t), 1)

                    if t[0] == "gated":
                        dve.wait_ge(c_done, r.mix + 2)
                        t_ended(dve, r, ("out", L - 1))
                        V_.tensor_tensor(y[:, :], y[:, :], gate1_f[:, :], ALU.mult).then_inc(y_gated, 1)
                    if t[0] == "final_T":
                        t_ready(dve, r, t)
                        V_.tensor_tensor(y_out[:, :, :], b[0][:, :].rearrange("p (t d) -> p t d", t=NT),
                                         x1[:, :, :], ALU.add).then_inc(t_sem(t), 1)

                def u_part(name, u):
                    dve.wait_ge(u_full, r.unit + (u + 1))
                    if has_weight(u):
                        dve.wait_ge(weighed, r.wei + (u + 1))
                    else:
                        dve.wait_ge(silu, r.unit + (u + 1))
                    V_.tensor_tensor(hu[:, :], bU[:, :], s_h[:, :], ALU.mult).then_inc(h_ready, 1)

                def r_part(name, k):
                    if name == "r1":
                        route1_chunk(k, r)
                    else:
                        route0_chunk(k, (r.a + 1) * R0_STEPS, r.a + 2, fill_no(r, ("route0", L - 1)) + 1)

                take_turns("dve", streams(r, a_part, t_part, u_part, r_part))

            rounds(dve, one)

        @block.tensor
        def _(pe):
            mm = nc.tensor.matmul

            def transpose(dst, src):
                k = src.shape[0]
                return nc.tensor.transpose(dst, src, ident[0:k, 0:k])

            def transpose_b(dst, src):
                return nc.tensor.transpose(dst, src, identb[:, :])

            def transposes(bank, tiles):
                for n, src in enumerate(tiles):
                    ins = transpose(bank[:, n * P:(n + 1) * P], src)
                return ins

            for n, tiles in enumerate(prep_sources()):
                if n == 0:
                    pe.wait_ge(loaded["small"], 15 * 16)
                if n == 2:
                    pe.wait_ge(loaded["gates"], 6 * 16)
                if n >= len(banks):
                    pe.wait_ge(prep_c, n - len(banks) + 1)
                at = 0
                for src in tiles:
                    k = src.shape[0]
                    ins = transpose(banks[n % len(banks)][:, at:at + k], src)
                    at += k
                ins.then_inc(prep_T, 1)
            pe.wait_ge(w_perm, 1)
            pe.wait_ge(prep_c, 1)
            for n in range(3 + FC):
                for l in range(L):
                    w = w_att[:, l, n, :] if n < 3 else w_fc[:, l, (n - 3) * D:(n - 2) * D]
                    b = LN1B if n < 3 else LN2B
                    ins = mm(bC[:, n * L + l:n * L + l + 1], w, cols[:, b, l:l + 1], start=True, stop=True)
            ins.then_inc(bias_mm, 1)
            pe.wait_ge(folded, 2)
            for l in range(L):
                ins = mm(bC[:, l * D:(l + 1) * D], hart_w[:, :], st_pw[:, l, :], start=True, stop=True)
            ins.then_inc(hp_mm, 1)
            pe.wait_ge(hp_c, 1)
            pe.wait_ge(prep_c, PREP_BANKS)
            pe.wait_ge(loaded["experts0"], 3 * 16)
            pe.wait_ge(loaded["consts"], 12 * 16)

            def prep_step(name, before, out_n, done_n):
                pe.wait_ge(a_done, before)
                if name == "prep_T":
                    pe.wait_ge(lnA_out, out_n)
                    return transposes(bA, [xn[:, t, :] for t in range(NT)])
                if name == "route0":
                    for t in range(NT):
                        ins = mm(bA[:, t * E0:(t + 1) * E0], xn_f[:, t * P:(t + 1) * P], w_r0, start=True, stop=True)
                    return ins
                pe.wait_ge(r0_done, done_n)
                bank = bA[:, :].bitcast(bf16)
                for t in range(NT):
                    ins = transpose_b(bank[0:PARTS * E0, t * P:(t + 1) * P],
                                      r0_parts[:, t, :, :].rearrange("p k e -> p (k e)"))
                return ins

            for n, name in enumerate(PREP):
                prep_step(name, n, 1, 1).then_inc(a_full, 1)

            def one(r):
                def fill(name, l):
                    pe.wait_ge(a_done, fill_no(r, (name, l)))

                def a_part(name, l):
                    if name == "prep_T":
                        pe.wait_ge(h_ready, r.unit + (UNITS0 + 1))
                    if name in PREP:
                        ins = prep_step(name, fill_no(r, (name, l)), ln_no(r, ("prep_stats", l)) + 1, r.a + 2)
                    else:
                        if name == "hart":
                            pe.wait_ge(ham, ham_no(r, l, HAM_OPS))
                        if name in ("ln1_T", "ln2_T"):
                            pe.wait_ge(lnA_out, ln_no(r, ("stats" + name[2], l)) + 1)
                        if name == "gate_T":
                            pe.wait_ge(c_done, r.mix + 1)
                        fill(name, l)
                    if name in ("ln1_T", "ln2_T"):
                        ins = transposes(bA, [ln_hat[:, t, :] for t in range(NT)])
                    if name in ("q", "k", "v"):
                        ins = mm(bA[:, :], w_att[:, l, "qkv".index(name), :], xf, start=True, stop=True)
                    if name == "hart":
                        ins = mm(bA[:, :], hart_w[:, :], z, start=True, stop=True)
                    if name == "proj":
                        ins = mm(bA[:, :], w_hp[:, l, :], zc, start=True, stop=True)
                    if name in ("proj_T", "mproj_T", "gate_T"):
                        src = gate_f if name == "gate_T" else pfm
                        ins = transposes(bA, [src[:, t * P:(t + 1) * P] for t in range(NT)])
                    if name in ("fc0", "fc1", "fc2", "fc3"):
                        j = int(name[2])
                        ins = mm(bA[:, :], w_fc[:, l, j * D:(j + 1) * D], xf, start=True, stop=True)
                    if name == "mproj":
                        for j in range(FC):
                            ins = mm(bA[:, :], w_mp[:, l, j, :], hid[:, j, :], start=j == 0, stop=j == FC - 1)
                    ins.then_inc(a_full, 1)

                def t_part(*t):
                    b = t_set(t)
                    builds_on = {"route1": [("xn1_T",)], "PT": [("S",) + t[1:]], "O": [("PT",) + t[1:], ("V",) + t[1:2]],
                                 "OT": [("O",) + t[1:] + (k,) for k in range(2)],
                                 "out": [("OT", 2 * t[-1] + k) for k in range(2)] if t[0] == "out" else []}
                    if t == ("q", 0):
                        builds_on["q"] = [("xn1_T",)]
                    t_begin(pe, r, t, *builds_on.get(t[0], []))
                    if t[0] == "xn1_T":
                        pe.wait_ge(lnB_out, r.b + 1)
                        ins = transposes(b[0], [x1n[:, k, :] for k in range(NT)])
                    if t[0] == "route1":
                        for k in range(NT):
                            ins = mm(b[0][:, k * E1:(k + 1) * E1], x1n_f[:, k * P:(k + 1) * P], w_r1, start=True, stop=True)
                    if t[0] in "qk":
                        c = t[1] * P + (0 if t[0] == "q" else INNER)
                        mm(b[0][:, :], w_a1[:, c:c + P], x1n_f[:, :], start=True, stop=True)
                        ins = mm(b[1][:, :], w_rot[:, c:c + P], x1n_f[:, :], start=True, stop=True)
                    if t[0] == "V":
                        c = t[1] * P + 2 * INNER
                        for w in range(NW):
                            ins = mm(b[0][:, w * P:(w + 1) * P], x1n_f[:, w * WIN:(w + 1) * WIN], w_a1[:, c:c + P],
                                     start=True, stop=True)
                    if t[0] == "S":
                        if t[2] == 0:
                            pe.wait_ge(roped, r.b * len(ROPE_ORDER) + (ROPE_ORDER.index(("k", t[1])) + 2))
                        for h in range(2):
                            mm(b[h][:, :], identb[:, :], maskb[:, t[2] * 2 * WIN:t[2] * 2 * WIN + S], start=True, stop=False)
                        for w in range(2):
                            ww = 2 * t[2] + w
                            for h in range(2):
                                f = slice(h * DH, (h + 1) * DH)
                                ins = mm(b[h][:, w * 2 * WIN:(w + 1) * 2 * WIN], Q[f, ww * WIN:(ww + 1) * WIN],
                                         Kk[f, ww * WIN:(ww + 2) * WIN], start=False, stop=w == 1)
                    if t[0] == "PT":
                        for h in range(2):
                            ins = transposes(b[h], [probs[:, h, 2 * t[2] + w, k * P:(k + 1) * P]
                                                    for w in range(2) for k in range(2)])
                    if t[0] == "O":
                        for w in range(2):
                            for h in range(2):
                                for k in range(2):
                                    ins = mm(b[0][:, (2 * w + h) * DH:(2 * w + h + 1) * DH],
                                             probsT[:, h, (2 * w + k) * P:(2 * w + k + 1) * P],
                                             V[:, 2 * t[2] + w + k, h * DH:(h + 1) * DH], start=k == 0, stop=k == 1)
                    if t[0] == "OT":
                        ins = transposes(b[0], [O[:, w, :] for w in range(NW)])
                    if t[0] == "gates1_T":
                        pe.wait_ge(r1_done, r.b + 1)
                        bank = b[0][:, :].bitcast(bf16)
                        for k in range(NT):
                            ins = transpose_b(bank[0:PARTS * E1, k * P:(k + 1) * P],
                                              r1_parts[:, k, :, :].rearrange("p k e -> p (k e)"))
                    if t[0] == "out":
                        for k in range(2):
                            ins = mm(b[0][:, :], w_o1[:, 2 * t[1] + k, :], OT[:, k, :], start=k == 0, stop=k == 1)
                    if t[0] == "final_T":
                        pe.wait_ge(y_gated, r.b + 1)
                        ins = transposes(b[0], [y[:, k * P:(k + 1) * P] for k in range(NT)])
                    ins.then_inc(t_full, 1)

                def u_part(name, u):
                    g, up, down, sel, e = unit_kind(u)
                    src, gates = (xn_f, gates0) if u < UNITS0 else (x1n_f, gates1)
                    begins = u == units_of(r)[0]
                    if name == "gate":
                        if u == 0:
                            pe.wait_ge(a_done, gates0_no(r))
                        if u == UNITS0:
                            t_ended(pe, r, ("gates1_T",))
                        if not begins:
                            pe.wait_ge(silu, r.unit + u)
                        mm(bG[:, :], g, src[:, :], start=True, stop=True).then_inc(g_full, 1)
                    if name == "weight":
                        pe.wait_ge(h_ready, r.unit + (u + 1))
                        mm(bU[:, :], sel, gates[:, :], start=True, stop=True).then_inc(e_full, 1)
                    if name == "up":
                        if sel is not None:
                            pe.wait_ge(ge_sb, r.gel + (e + 1))
                        mm(bU[:, :], up, src[:, :], start=True, stop=True).then_inc(u_full, 1)
                    if name == "down":
                        if u == UNITS0:
                            pe.wait_ge(c_done, r.mix + 1)
                        if u == 0 and r is not first:
                            pe.wait_ge(c_done, r.mix)
                        pe.wait_ge(h_ready, r.unit + (u + 2))
                        ins = mm(bC[:, :], down, hu[:, :], start=u in (0, UNITS0), stop=u in (UNITS0 - 1, UNITS - 1))
                        if u in (UNITS0 - 1, UNITS - 1):
                            ins.then_inc(c_full, 1)

                take_turns("pe", streams(r, a_part, t_part, u_part))

            rounds(pe, one)


def hartley():
    h, d = np.divmod(np.arange(D), HD)
    turns = (np.outer(h, h) % H) / H + (np.outer(d, d) % HD) / HD
    return ((np.cos(2 * np.pi * turns) + np.sin(2 * np.pi * turns)) / np.sqrt(D)).astype(np.float32)


def filter_modulation():
    h, d = np.divmod(np.arange(D), HD)
    ks, kh, kd = np.fft.fftfreq(S)[None, :], np.fft.fftfreq(H)[h][:, None], np.fft.fftfreq(HD)[d][:, None]
    km = np.sqrt(ks ** 2 + kh ** 2 + kd ** 2 + 1e-10)
    real = np.cos(np.arctan(np.log(km + 1e-10)))
    lam, t = np.arange(S) / S, np.arange(S) * 0.1
    mod = np.sin(t + lam) * np.cos(t - 2.0 * lam + 0.5 * lam ** 2)
    return (real * (1.0 + 0.1 * mod)[None, :]).astype(np.float32)


def rotary():
    d = np.arange(P) % DH
    ang = (10000.0 ** -(2.0 * (d % (DH // 2)) / DH))[:, None] * np.arange(S)[None, :]
    return np.cos(ang).astype(np.float32), (np.sin(ang) * np.where(d < DH // 2, -1, 1)[:, None]).astype(np.float32)


def masks(dtype):
    i, j = np.arange(WIN)[:, None], np.arange(WIN)[None, :]
    here, before = np.where(j <= i, 0.0, MASKED), np.where(j >= i, 0.0, MASKED)
    return np.concatenate([np.full((WIN, WIN), MASKED), here, before, here, before, here], 1).astype(dtype)


def selectors(dtype):
    e0 = np.arange(PARTS * E0) % E0
    s0 = np.broadcast_to((e0[:, None] == np.arange(E0)[None, :])[:, :, None], (PARTS * E0, E0, P))
    e1 = np.arange(PARTS * E1) % E1
    s1 = e1[:, None, None] == (2 * np.arange(PAIR1)[:, None] + np.arange(P)[None, :] // I1)[None, :, :]
    return s0.astype(dtype), s1.astype(dtype)


_INS = ["L0_attn_x", "L0_attn_ln1_w", "L0_attn_ln1_b", "L0_attn_attn_w", "L0_attn_attn_b", "L0_attn_aproj_w",
        "L0_attn_aproj_b", "L0_attn_ln2_w", "L0_attn_ln2_b", "L0_attn_fc_w", "L0_attn_fc_b", "L0_attn_mproj_w",
        "L0_attn_mproj_b", "L0_ffn_router_w", "L0_ffn_w_gate", "L0_ffn_w_up", "L0_ffn_w_down", "L1_attn_W_qkv",
        "L1_attn_W_out", "L1_ffn_router_weight", "L1_ffn_router_bias", "L1_ffn_gate_w", "L1_ffn_up_w",
        "L1_ffn_down_w", "L1_ffn_shared_gate_w", "L1_ffn_shared_up_w", "L1_ffn_shared_down_w"]


def kernel(**inputs):
    import concourse.bacc as bacc
    from concourse.bass_utils import run_bass_kernel_spmd

    bf = mybir.dt.np(mybir.dt.bfloat16)
    nc = bacc.Bacc("TRN2", target_bir_lowering=False, num_devices=1)
    arrays = {name: np.ascontiguousarray(inputs[name]) for name in _INS}
    cos, sin = rotary()
    sel0, sel1 = selectors(bf)
    consts = {
        "c_ident": np.eye(P, dtype=np.float32), "c_identb": np.eye(P).astype(bf), "c_hart": hartley(),
        "c_cmod": filter_modulation(), "c_cos": cos, "c_sin": sin, "c_mask": masks(bf), "c_sel0": sel0, "c_sel1": sel1,
        "c_iota": np.broadcast_to(np.arange(E1, dtype=np.float32), (P, E1)),
        "c_ltri": np.broadcast_to(np.tril(np.ones((GROUPS, GROUPS), np.float32), -1), (P, GROUPS, GROUPS)),
    }
    arrays.update({n: np.ascontiguousarray(a) for n, a in consts.items()})
    args = [nc.dram_tensor("in_" + n, a.shape, mybir.dt.from_np(a.dtype), kind="ExternalInput").ap()
            for n, a in arrays.items()]
    out = nc.dram_tensor("out", (NB, S, D), mybir.dt.float32, kind="ExternalOutput").ap()
    program(nc, *args, out)
    r = run_bass_kernel_spmd(nc, [{"in_" + n: a for n, a in arrays.items()}], core_ids=[0])
    return r.results[0]["out"]
```

```python
import math
from contextlib import ExitStack

import numpy as np
import concourse.bass as bass
from concourse import mybir

NB, S, D = 16, 512, 128
P = 128
NT = S // P
HT = S // 2
L, H = 4, 16
HD = D // H
FC = 4
E0, H0, K0 = 8, 256, 2
HALF0 = H0 // P
E1, I1 = 32, 64
PAIR1 = E1 * I1 // P
GROUPS, TOPG, TOPK1, SCALE1 = 4, 2, 4, 2.5
EG = E1 // GROUPS
AH, DH, WIN = 16, 64, 128
HP = AH // 2
NW = S // WIN
INNER = AH * DH
PARTS = 3
GROUP = 32
EPS = 1e-5
ROUND = 1.5 * 2.0 ** 23
TWO_PI = 2.0 * math.pi
MASKED = -1e30

UNITS0, UNITS1 = E0 * HALF0, PAIR1 + 1
UNITS = UNITS0 + UNITS1
TB = 3
HAMS = 15
R0_CHUNKS, R1_CHUNKS = 4, 6


def stream_a():
    out = []
    for l in range(L):
        names = ["stats1", "norm1", "ln1_T", "k", "turn_k", "v", "turn_v", "ang_k", "abs_k", "q", "ang_v", "abs_v", "cos_k",
                 "cos_v", "turn_q", "ham0", "ang_q", "abs_q", "cos_q", "ham1"]
        if l == L - 1:
            names += ["prep_stats", "ham2", "prep_norm", "prep_T", "ham3", "ham4", "route0"]
        names += [f"ham{n}" for n in range(5 if l == L - 1 else 2, HAMS)]
        names += ["hart", "proj", "stats2"]
        names += {L - 2: ["gate_T"], L - 1: ["gates0_T"]}.get(l, [])
        names += ["norm2", "ln2_T", "fc0", "fc1", "fc2", "fc3", "mproj"]
        out += [(name, l) for name in names]
    return out + [("join", L - 1)]


def stream_t():
    out = [("statsB",), ("normB",), ("xn1_T",), ("route1",), ("q", 0), ("k", 0), ("rope", 0), ("V", 0)]
    for p in range(HP):
        more = p + 1 < HP
        out += [("q", p + 1), ("k", p + 1)] * more + [("S", p, n) for n in range(4)] + [("rope", p + 1)] * more
        out += [("PT", p, 0), ("PT", p, 1), ("O", p, 0), ("PT", p, 2), ("PT", p, 3), ("O", p, 1), ("OT", p)]
        out += [("V", p + 1)] * more
        if p == 1:
            out += [("gates1_T",)]
        if p % 2:
            out += [("out", p // 2)]
    return out + [("gated",), ("final_T",)]


def stream_u():
    out = []
    for u in range(UNITS):
        out += [("gate", u), ("weight", u)] + ([("down", u - 1)] if u else []) + [("up", u), ("hidden", u)]
    return out + [("down", UNITS - 1)]


STREAMS = {"a": stream_a(), "b": stream_a(), "t": stream_t(), "u": stream_u(),
           "r": [("r1", n) for n in range(R1_CHUNKS)] + [("r0", n) for n in range(R0_CHUNKS)]}
HAM_NAMES = {f"ham{n}" for n in range(HAMS)}
DOES = {
    "pe": {"a": {"ln1_T", "k", "v", "q", "prep_T", "route0", "hart", "proj", "gate_T", "gates0_T", "ln2_T",
                 "fc0", "fc1", "fc2", "fc3", "mproj"},
           "t": {"xn1_T", "route1", "q", "k", "V", "S", "PT", "O", "OT", "gates1_T", "out", "final_T"},
           "u": {"gate", "weight", "down", "up"}, "r": set()},
    "act": {"a": {"ln1_T", "k", "turn_k", "v", "turn_v", "q", "turn_q", "abs_k", "abs_v", "abs_q", "cos_k", "cos_v", "cos_q",
                  "prep_T", "gate_T", "gates0_T", "ln2_T", "fc0", "fc1", "fc2", "fc3"},
            "t": {"xn1_T", "route1", "q", "k", "V", "S", "PT", "OT", "gates1_T"},
            "u": {"gate", "weight", "down"}, "r": {"r0"}},
    "dve": {"a": {"stats1", "norm1", "ang_k", "ang_v", "ang_q", "prep_stats", "prep_norm", "route0", "hart", "proj",
                  "stats2", "norm2", "mproj", "join"} | HAM_NAMES,
            "t": {"statsB", "normB", "rope", "S", "O", "out", "gated", "final_T"},
            "u": {"hidden"}, "r": {"r0", "r1"}},
    "pool": {"a": {"stats1", "k", "v", "q", "prep_stats", "stats2"}, "t": {"statsB", "q", "k", "rope"},
             "u": {"weight"}, "r": set()},
    "sp": {"a": {"k", "v", "q", "prep_norm"}, "t": {"q", "k", "final_T"}, "u": set(), "r": set()},
}


def has_work(engine, stream, step):
    if step[0] not in DOES[engine]["a" if stream == "b" else stream]:
        return False
    if step[0] == "weight":
        u = step[1]
        if engine == "pool":
            return u < UNITS - 1
        return u < UNITS - 1 and (u >= UNITS0 or u % HALF0 == 0)
    if engine == "act":
        return step not in [("down", u) for u in range(UNITS) if u not in (UNITS0 - 1, UNITS - 1)] and \
            (step[0] != "r0" or step[1] == 1)
    return True


STEPS_FOR = {e: {k: [t for t in steps if has_work(e, k, t)] for k, steps in STREAMS.items()} for e in DOES}
ORDER = {
    "pe": "uuuaauabbauubtuubutuuutuutuuutuuuuttuuuuttataututtutatuauutauauauatbuuuabauattauubtbutubtbtubtbu"
          "utuuubuttbuubtttauautbutatatttatatattatututuutttuautuabubatuatuububtttbububutbuuttubttbuubtattbu"
          "autuautttuauattutauauatatttbutuubtbttuatabubuattttbtbtbtbtauttuttbtubuubtbuutttatttattubututtuub"
          "ttuutuutuuutuuuutuuuaututatbuuttbtuutattabuabtbuababtabtbta",
    "act": "uuaaaubaababaaaabtaubbuabbbbbuttauutubuuttbtuttttttuatuataaauuuaaaaataaaaatbuatbtbabbuuttauttbtb"
           "tububtbtubbbbbbattabtaattattttttuubuttauaauaaataaaaaubtbutbtabbuuatttbttbtbubutbbbtbbbbutubtbaau"
           "atautaattttttuuttababubtuatabtbtabtttaaatttaaatbtbubbubbabbbbtbutabbatttbutttttuuttuuuuuutrtuutt"
           "ttttuatabtbabababtabu",
    "dve": "abatubatabuaaabauababauababauabatauababautabtatabtbuabrbtbubtbrbaautbarbbuaabraaauataratatababau"
           "abatauataabatuaabtarbbbtbbbbtbtbtbbatbuabbtatbubtbabbaubaaaaaaauaatatabbauatbtaaatbatbauatbbbabb"
           "ubtbbbbbbbtbtbbttuabatbbatubttaattbbtbtutaaaaabbtaaubbtbbatbabttbabtautbbrabtaubababatubabaubaru"
           "batbtratbutabrbatbutttbtbaa",
    "pool": "aubtuababuuaututtuuattubtuauabaauubtubtuabtbuauttauabtuubtatubbtabuuaubtttuaatbatabubbtbuuttutuu"
            "uab",
    "sp": "aababtttbtaattabbtbtaatatbbbttttaabbattabbt",
}


def take_turns(engine, parts):
    at = dict.fromkeys(parts, 0)
    for k in ORDER[engine]:
        step = STEPS_FOR[engine][k][at[k]]
        at[k] += 1
        if parts[k] is not None:
            parts[k](*step)


A_FILLS = ("ln1_T", "k", "v", "q", "prep_T", "route0", "hart", "proj", "gate_T", "gates0_T", "ln2_T",
           "fc0", "fc1", "fc2", "fc3", "mproj")
FILL = {step: n for n, step in enumerate(t for t in STREAMS["a"] if t[0] in A_FILLS)}
PREP = ("prep_T", "route0", "gates0_T")
PREP_FILL = {name: n for n, name in enumerate(PREP)}
NFILL, NPREP = len(FILL), len(PREP_FILL)
LN_AT = {step: n for n, step in enumerate(t for t in STREAMS["a"] if t[0] in ("stats1", "stats2", "prep_stats"))}
LNS = len(LN_AT)
STEPS = [t for t in STREAMS["t"] if t[0] not in ("statsB", "normB", "rope", "gated")]
STEP_AT = {t: n for n, t in enumerate(STEPS)}
STEPS_OF = [len(STEPS[i::TB]) for i in range(TB)]
ROPE_ORDER = [t for t in STEPS if t[0] in ("q", "k")]
ANGLE_ORDER = "kvq"
HAM_OPS = 17
R0_STEPS, R0_TOP, R1_STEPS = 14, 1, 27
PREP_BANKS = 2 + 3 * (PAIR1 // 4) + 3


def program(nc, x, ln1_w, ln1_b, attn_w, attn_b, aproj_w, aproj_b, ln2_w, ln2_b, fc_w, fc_b, mproj_w, mproj_b,
            router_w, w_gate, w_up, w_down, w_qkv, w_out, route_w1, route_b1, gate_w1, up_w1, down_w1,
            sh_gate, sh_up, sh_down, c_ident, c_identb, c_hart, c_cmod, c_cos, c_sin, c_mask, c_sel0, c_sel1,
            c_iota, c_ltri, out):
    fp32, bf16, u32 = mybir.dt.float32, mybir.dt.bfloat16, mybir.dt.uint32
    ALU, ACT, AX = mybir.AluOpType, mybir.ActivationFunctionType, mybir.AxisListType
    ctx = ExitStack()
    with ctx:
        def sb(name, shape, dt=fp32):
            return ctx.enter_context(nc.sbuf_tensor(name, shape, dt))

        def sem(name):
            return ctx.enter_context(nc.semaphore(name))

        w_att = sb("w_att", [P, L, 3, D])
        w_hp = sb("w_hp", [P, L, D])
        w_fc = sb("w_fc", [P, L, FC * D])
        w_mp = sb("w_mp", [P, L, FC, D])
        NCOL = 4 + 3 + FC
        LN1W, LN1B, LN2W, LN2B, AB, FB = 0, 1, 2, 3, 4, 7
        cols = sb("cols", [P, NCOL, L])
        rows_b = sb("rows_b", [PARTS * GROUP, 2, L, D], bf16)
        share = sb("share", [PARTS * GROUP, P], bf16)
        w_g0 = sb("w_g0", [P, E0, H0])
        w_u0 = sb("w_u0", [P, E0, H0])
        w_d0 = sb("w_d0", [P, E0, HALF0, D])
        w_r = sb("w_r", [P, E0 + E1])
        w_r0, w_r1 = w_r[:, 0:E0], w_r[:, E0:E0 + E1]
        w_a1 = sb("w_a1", [P, 3 * INNER])
        w_o1 = sb("w_o1", [P, HP, D])
        w_g1 = sb("w_g1", [P, PAIR1 + 1, P])
        w_u1 = sb("w_u1", [P, PAIR1 + 1, P])
        w_d1 = sb("w_d1", [P, PAIR1 + 1, D])
        rbias = sb("rbias", [P, E1])
        ident = sb("ident", [P, P])
        identb = sb("identb", [P, P], bf16)
        cmod = sb("cmod", [P, S])
        cosT = sb("cosT", [P, S])
        sinT = sb("sinT", [P, S])
        maskb = sb("maskb", [P, 6 * WIN], bf16)
        sel0 = sb("sel0", [PARTS * E0, E0, P], bf16)
        sel1 = sb("sel1", [PARTS * E1, PAIR1, P], bf16)
        iota = sb("iota", [P, E1])
        ltri = sb("ltri", [P, GROUPS, GROUPS])
        nhalf = sb("nhalf", [P, NT])
        epsT = sb("epsT", [P, NT])
        roundT = sb("roundT", [P, 1])
        scratch = sb("scratch", [P, 1])
        hpi = sb("hpi", [P, 1])
        x_ld = sb("x_ld", [P, NT, D])
        xn = sb("xn", [P, NT, D])
        xr = sb("xr", [P, NT, D])
        xn_f = sb("xn_f", [P, S])
        gates0 = sb("gates0", [PARTS * E0, S], bf16)
        comps = sb("comps", [P, 3, 4, S])
        acc = sb("acc", [P, 4, S])
        tmp = sb("tmp", [P, 2, S])
        gate_f = sb("gate_f", [P, S])
        z, zc, xf = acc[:, 0, :], acc[:, 1, :], acc[:, 3, :]
        hid = acc
        ln_hat = tmp[:, 0, :].rearrange("p (t d) -> p t d", t=NT)
        xmul = tmp[:, 1, :].rearrange("p (t d) -> p t d", t=NT)
        stA, mvA = sb("stA", [P, NT, 6]), sb("mvA", [P, NT, 2])
        veA, rsA = sb("veA", [P, NT]), sb("rsA", [P, NT])
        r0_lg = sb("r0_lg", [P, NT, E0])
        r0_top = sb("r0_top", [P, NT, 8])
        r0_idx = sb("r0_idx", [P, NT, 8], u32)
        r0_idf = sb("r0_idf", [P, NT, 8])
        r0_sg = sb("r0_sg", [P, NT, K0])
        r0_sum = sb("r0_sum", [P, NT])
        r0_hit = sb("r0_hit", [P, NT, K0, E0])
        r0_g = sb("r0_g", [P, NT, E0])
        r0_parts = sb("r0_parts", [P, NT, PARTS, E0], bf16)
        x1 = sb("x1", [P, NT, D])
        x1n_f = sb("x1n_f", [P, S])
        Q = sb("Q", [P, S])
        Kk = sb("Kk", [P, S])
        raw = sb("raw", [P, 2, S])
        rot = sb("rot", [P, 2, S])
        V = sb("V", [P, NW, 2, DH + 1])
        probs = sb("probs", [P, 2, NW, 2 * WIN])
        probsT = sb("probsT", [P, 2, 4 * WIN])
        O = sb("O", [P, NW, P])
        OT = sb("OT", [P, 2, S])
        y = sb("y", [P, S])
        nmax = sb("nmax", [P, 2, NW])
        rinv = sb("rinv", [P, 2, 2])
        s_h = sb("s_h", [P, S])
        ge = sb("ge", [P, S])
        hu = sb("hu", [P, S])
        gate1_f = sb("gate1_f", [P, S])
        gates1 = sb("gates1", [PARTS * E1, S], bf16)
        x1n = rot[:, 0, :].rearrange("p (t d) -> p t d", t=NT)
        y_out = O
        stB, mvB = sb("stB", [P, NT, 6]), sb("mvB", [P, NT, 2])
        veB, rsB = sb("veB", [P, NT]), sb("rsB", [P, NT])
        r1_s = sb("r1_s", [P, NT, E1])
        r1_c = sb("r1_c", [P, NT, E1])
        r1_m8 = sb("r1_m8", [P, NT, GROUPS, 8])
        r1_gs = sb("r1_gs", [P, NT, GROUPS])
        r1_gt = sb("r1_gt", [P, NT, GROUPS, GROUPS])
        r1_eq = sb("r1_eq", [P, NT, GROUPS, GROUPS])
        r1_top = sb("r1_top", [P, NT, 8])
        r1_idx = sb("r1_idx", [P, NT, 8], u32)
        r1_idf = sb("r1_idf", [P, NT, 8])
        r1_hit = y[:, :].rearrange("p (t k e) -> p t k e", t=NT, k=TOPK1)
        r1_sum = sb("r1_sum", [P, NT])
        r1_parts = sb("r1_parts", [P, NT, PARTS, E1], bf16)

        bA = [ctx.enter_context(nc.psum_tensor(f"bA{h}", [P, S], fp32)) for h in range(2)]
        bT = [ctx.enter_context(nc.psum_tensor(f"bT{i}", [P, S], fp32)) for i in range(TB)]
        bG = ctx.enter_context(nc.psum_tensor("bG", [P, S], fp32))
        bU = ctx.enter_context(nc.psum_tensor("bU", [P, S], fp32))
        bC = ctx.enter_context(nc.psum_tensor("bC", [P, S], fp32))
        banks = bA + bT + [bG, bU]

        st_att = comps[:, 0, 0:3, :].rearrange("p a n -> p (a n)").rearrange("p (l n) -> p l n", l=L)
        st_par = comps[0:L, 0, 3, :]
        st_rows = rot[0:PARTS * GROUP, :, :].rearrange("p n (l d) -> p n l d", l=L)
        st_par2 = comps[0:L, 1, 0:3, :].rearrange("p a n -> p (a n)")
        st_g = probs[:, :, :, :].rearrange("p a b n -> p (a b n)").rearrange("p (j n) -> p j n", n=P)
        st_u = acc[:, :, :].rearrange("p a n -> p (a n)").rearrange("p (j n) -> p j n", n=P)
        st_d = comps[:, 2, :, :].rearrange("p a n -> p (a n)")
        st_sh = comps[:, 1, 3, :].rearrange("p (a n) -> p a n", n=P)
        st_r0, st_r1 = tmp[0:E0, 0, 0:P], tmp[0:E1, 0, P:2 * P]
        st_pw = tmp[:, 1, :].rearrange("p (l n) -> p l n", l=L)
        hart_w = sb("hart_w", [P, D])

        loaded = {n: sem("loaded_" + n) for n in ("small", "rows", "consts", "attn", "gates", "experts0", "wqkv")}
        set_up = sem("set_up")
        prep_T = sem("prep_T")
        prep_c = sem("prep_c")
        w_perm = sem("w_perm")
        row_part = sem("row_part")
        bias_mm = sem("bias_mm")
        folded = sem("folded")
        hp_mm = sem("hp_mm")
        hp_c = sem("hp_c")
        a_full = [sem("a_full%d" % h) for h in range(2)]
        a_done = [sem("a_done%d" % h) for h in range(2)]
        lnA_bn = [sem("lnA_bn%d" % h) for h in range(2)]
        lnA_mv = [sem("lnA_mv%d" % h) for h in range(2)]
        lnA_ve = [sem("lnA_ve%d" % h) for h in range(2)]
        lnA_rs = [sem("lnA_rs%d" % h) for h in range(2)]
        lnA_out = [sem("lnA_out%d" % h) for h in range(2)]
        lnB_bn, lnB_mv, lnB_ve, lnB_rs, lnB_out = (sem("lnB_" + n) for n in ("bn", "mv", "ve", "rs", "out"))
        angled = [sem("angled%d" % h) for h in range(2)]
        ham = [sem("ham%d" % h) for h in range(2)]
        rolled_kv = [sem("rolled_kv%d" % h) for h in range(2)]
        rolled_q = [sem("rolled_q%d" % h) for h in range(2)]
        diffed = [sem("diffed%d" % h) for h in range(2)]
        turned = [sem("turned%d" % h) for h in range(2)]
        folded_ang = [sem("folded_ang%d" % h) for h in range(2)]
        cosined = [sem("cosined%d" % h) for h in range(2)]
        r0_step, r1_step = sem("r0_step"), sem("r1_step")
        r0_sig = sem("r0_sig")
        r0_done, r1_done = sem("r0_done"), sem("r1_done")
        x_in = [sem("x_in%d" % h) for h in range(2)]
        joined = [sem("joined%d" % h) for h in range(2)]
        x1_ready = sem("x1_ready")
        t_full = sem("t_full")
        t_done = [sem(f"t_done{i}") for i in range(TB)]
        swapped = {n: sem("swapped_" + n) for n in "qk"}
        cos_part, sin_part = sem("cos_part"), sem("sin_part")
        roped = sem("roped")
        smax = sem("smax")
        rinved = sem("rinved")
        y_gated = sem("y_gated")
        stored = sem("stored")
        g_full, e_full, u_full = sem("g_full"), sem("e_full"), sem("u_full")
        silu = sem("silu")
        ge_sb = sem("ge_sb")
        weighed = sem("weighed")
        h_ready = sem("h_ready")
        c_full = sem("c_full")
        c_done = sem("c_done")

        block = ctx.enter_context(nc.Block())

        class Round:

            def __init__(self, a, b, unit, gel, wei, mix):
                self.a, self.b, self.unit, self.gel, self.wei, self.mix = a, b, unit, gel, wei, mix

        GEL0, GEL1 = E0, PAIR1
        WEI = UNITS0 + PAIR1
        first = Round(0, None, 0, 0, 0, 0)
        last = Round(None, NB - 1, (NB - 1) * UNITS, (NB - 1) * (GEL0 + GEL1), (NB - 1) * WEI, (NB - 1) * 2)

        def middle(i):
            return Round(i, i - 1, i * UNITS - UNITS1, i * (GEL0 + GEL1) - GEL1, i * WEI - PAIR1, i * 2 - 1)

        def fill_no(r, name):
            return r.a * NFILL + (NPREP + FILL[name])

        def a_ready(eng, r, h, name):
            eng.wait_ge(a_full[h], fill_no(r, name) + 1)

        def a_ended(eng, r, h, name):
            eng.wait_ge(a_done[h], fill_no(r, name) + 1)

        def tokens(h):
            return slice(h * HT, (h + 1) * HT)

        def subtiles(h):
            return slice(h * NT // 2, (h + 1) * NT // 2)

        def t_bank(t):
            return bT[STEP_AT[t] % TB]

        def t_ready(eng, r, t):
            eng.wait_ge(t_full, r.b * len(STEPS) + (STEP_AT[t] + 1))

        def t_sem(t):
            return t_done[STEP_AT[t] % TB]

        def t_ended(eng, r, t):
            n = STEP_AT[t]
            eng.wait_ge(t_done[n % TB], r.b * STEPS_OF[n % TB] + (n // TB + 2))

        def t_begin(eng, r, t, *earlier):
            n = STEP_AT[t]
            eng.wait_ge(t_done[n % TB], r.b * STEPS_OF[n % TB] + (n // TB + 1))
            for i in range(TB):
                other = [STEP_AT[e] for e in earlier if STEP_AT[e] % TB == i]
                if other and i != n % TB:
                    t_ended(eng, r, STEPS[max(other)])

        def ham_no(r, l, n):
            return r.a * (L * HAM_OPS) + (l * HAM_OPS + n)

        def angle_no(r, l, n):
            return r.a * (L * 3) + (l * 3 + n)

        def ln_no(r, name):
            return r.a * LNS + (1 + LN_AT[name])

        def unit_kind(u):
            if u < UNITS0:
                e, half = u // HALF0, u % HALF0
                c = slice(half * P, half * P + P)
                return w_g0[:, e, c], w_u0[:, e, c], w_d0[:, e, half, :], (sel0[:, e, :] if half == 0 else None), e
            j = u - UNITS0
            return w_g1[:, j, :], w_u1[:, j, :], w_d1[:, j, :], (sel1[:, j, :] if j < PAIR1 else None), GEL0 + j

        def has_weight(u):
            return u < UNITS - 1

        def units_of(r):
            return range(0 if r.a is not None else UNITS0, UNITS if r.b is not None else UNITS0)

        def rounds(eng, one):
            one(first)
            with eng.Fori(1, NB) as i:
                one(middle(i))
            one(last)

        def streams(r, a, t, u=None, rt=None):
            units = units_of(r)

            def u_part(name, n):
                if n in units:
                    u(name, n)

            def r_part(name, n):
                if (r.a if name == "r0" else r.b) is not None:
                    rt(name, n)

            def half(h):
                def part(name, l):
                    a(h, name, l)
                return part if r.a is not None else None

            return {"a": half(0), "b": half(1), "t": t if r.b is not None else None, "u": u_part, "r": r_part}

        def gates0_bank(h):
            return bA[h][:, :].bitcast(bf16)[0:PARTS * E0, 0:HT]

        def gates0_no(r):
            return NPREP if r is first else r.a * NFILL + (NPREP - NFILL + FILL[("gates0_T", L - 1)] + 1)

        def prep_sources():
            rows = [st_par[:, n * D:(n + 1) * D] for n in range(4)] + \
                   [st_par2[:, n * D:(n + 1) * D] for n in range(NCOL - 4)]
            out = [rows, [st_r0, st_r1]]
            for st in (st_g, st_u):
                out += [[st[:, 4 * g + k, :] for k in range(4)] for g in range(PAIR1 // 4)]
            out += [[st_d[:, (4 * g + k) * P:(4 * g + k + 1) * P] for k in range(4)] for g in range(PAIR1 // 4)]
            return out + [[st_sh[:, n, :]] for n in range(3)]

        def prep_targets():
            out = [(cols[:, :, :], NCOL * L, NCOL), (w_r[:, :], E0 + E1, None)]
            for w in (w_g1, w_u1, w_d1):
                out += [(w[:, 4 * g:4 * g + 4, :], 4 * P, 4) for g in range(PAIR1 // 4)]
            return out + [(w[:, PAIR1, :], P, None) for w in (w_g1, w_u1, w_d1)]

        @block.sync
        def _(sp):
            def load(dst, src, s, n=1):
                sp.dma_start(dst, src).then_inc(s, 16)

            def load_x(n, h):
                load(x_ld[:, subtiles(h), :], x[n].rearrange("(t p) d -> p t d", p=P)[:, subtiles(h), :], x_in[h])

            for h in range(2):
                load_x(0, h)
            sm = loaded["small"]
            for n, src in enumerate((ln1_w, ln1_b, ln2_w, ln2_b)):
                load(st_par[:, n * D:(n + 1) * D], src, sm)
            for n in range(3):
                load(st_par2[:, n * D:(n + 1) * D].rearrange("l (h d) -> l h d", h=H),
                     attn_b.rearrange("l (h t d) -> l h t d", h=H, t=3)[:, :, n, :], sm)
            load(st_par2[:, 3 * D:3 * D + FC * D], fc_b, sm)
            for n, src in enumerate((aproj_b, mproj_b)):
                load(st_rows[:, n, :, :], src.unsqueeze(0).to_broadcast([PARTS * GROUP, L, D]), loaded["rows"])
            load(ident[:, :], c_ident, sm)
            load(st_r0, router_w, sm)
            load(st_r1, route_w1, sm)
            load(hart_w[:, :], c_hart, sm)
            load(st_pw, aproj_w.rearrange("l k n -> k l n"), sm)
            load(st_att, attn_w.rearrange("l k n -> k l n"), loaded["attn"])
            load(w_fc[:, :, :], fc_w.rearrange("l k n -> k l n"), loaded["attn"])
            load(st_g, gate_w1.rearrange("(j e) i h -> (e i) j h", j=PAIR1), loaded["gates"])
            load(st_u, up_w1.rearrange("(j e) i h -> (e i) j h", j=PAIR1), loaded["gates"])
            load(st_d.rearrange("p (e i) -> p e i", e=E1), down_w1.rearrange("e h i -> h e i"), loaded["gates"])
            for n, src in enumerate((sh_gate, sh_up, sh_down)):
                load(st_sh[:, n, :], src, loaded["gates"])
            load(w_g0[:, :, :], w_gate.rearrange("e k n -> k e n"), loaded["experts0"])
            load(w_u0[:, :, :], w_up.rearrange("e k n -> k e n"), loaded["experts0"])
            load(w_d0[:, :, :, :], w_down.rearrange("e (a p) n -> p e a n", p=P), loaded["experts0"])
            load(w_a1[:, :], w_qkv, loaded["wqkv"])
            cs = loaded["consts"]
            load(identb[:, :], c_identb, cs)
            load(cmod[:, :], c_cmod, cs)
            load(cosT[:, :], c_cos, cs)
            load(sinT[:, :], c_sin, cs)
            load(maskb[:, :], c_mask, cs)
            load(sel0[:, :, :], c_sel0, cs)
            load(sel1[:, :, :], c_sel1, cs)
            load(iota[:, :], c_iota, cs)
            load(ltri[:, :, :], c_ltri, cs)
            load(rbias[:, :], route_b1.unsqueeze(0).to_broadcast([P, E1]), cs)
            load(w_mp[:, :, :, :], mproj_w.rearrange("l (a p) n -> p l a n", p=P), cs)
            load(w_o1[:, :, :], w_out.rearrange("(a p) n -> p a n", p=P), cs)

            def one(r):
                def a_part(h, name, l):
                    if name == "prep_norm":
                        sp.wait_ge(lnA_out[h], ln_no(r, ("prep_stats", l)) + 1)
                        load_x(r.a, h)
                    else:
                        n, done = "qkv".index(name), (rolled_q if name == "q" else rolled_kv)[h]
                        a_ended(sp, r, h, (name, l))
                        sp.dma_start(comps[HD:P, n, 2, tokens(h)], comps[0:P - HD, n, 0, tokens(h)]).then_inc(done, 16)
                        sp.dma_start(comps[0:HD, n, 2, tokens(h)], comps[P - HD:P, n, 0, tokens(h)]).then_inc(done, 16)

                def t_part(*t):
                    t_ended(sp, r, t)
                    if t[0] in "qk":
                        i = "qk".index(t[0])
                        for at in range(0, P, DH // 2):
                            other = at ^ (DH // 2)
                            sp.dma_start(rot[at:at + DH // 2, i, :], raw[other:other + DH // 2, i, :]).then_inc(swapped[t[0]], 16)
                        return
                    sp.dma_start(out[r.b].rearrange("(t p) d -> p t d", p=P), y_out[:, :, :]).then_inc(stored, 16)

                if r.a is not None:
                    for h in range(2):
                        if r is first:
                            sp.wait_ge(lnA_out[h], 1)
                        else:
                            sp.wait_ge(x1_ready, 2 * r.a)
                        load_x((r.a + 1) % NB, h)
                take_turns("sp", streams(r, a_part, t_part))

            rounds(sp, one)
            sp.wait_ge(stored, (NB + 1) * 16)

        @block.gpsimd
        def _(pool):
            nc.gpsimd.memset(nhalf[:, :], -0.5).then_inc(t_done[0], 1)
            nc.gpsimd.memset(epsT[:, :], EPS).then_inc(t_done[1], 1)
            nc.gpsimd.memset(hpi[:, :], math.pi / 2).then_inc(roped, 1)
            nc.gpsimd.memset(roundT[:, :], ROUND).then_inc(h_ready, 1)
            nc.gpsimd.memset(V[:, :, :, DH:], 1.0)
            nc.gpsimd.memset(share[:, 0:DH], 1.0 / GROUP).then_inc(stored, 16)
            nc.gpsimd.memset(share[:, DH:], 1.0 / GROUP).then_inc(t_done[2], 1)
            pool.wait_ge(prep_T, PREP_BANKS)
            pool.wait_ge(w_perm, 1)
            nc.gpsimd.memset(comps[:, 0:2, 1, 0:1], 0.0).then_inc(set_up, 1)
            nc.gpsimd.memset(comps[:, 2, 1, 0:1], 0.0).then_inc(diffed[1], 1)
            pool.wait_ge(set_up, 1)

            def rstd(mv, ve, rs, mv_sem, ve_sem, rs_sem, n):
                pool.wait_ge(mv_sem, n + 1)
                k = ve.shape[1]
                nc.gpsimd.tensor_tensor(ve, mv[:, :, 1], epsT[:, 0:k], ALU.add).then_inc(ve_sem, 1)
                pool.wait_ge(ve_sem, n + 1)
                nc.gpsimd.tensor_tensor(rs, ve, nhalf[:, 0:k], ALU.pow).then_inc(rs_sem, 1)

            def rstd_a(h, n):
                rstd(mvA[:, subtiles(h), :], veA[:, subtiles(h)], rsA[:, subtiles(h)], lnA_mv[h], lnA_ve[h], lnA_rs[h], n)

            for h in range(2):
                rstd_a(h, 0)

            def one(r):
                def a_part(h, name, l):
                    if name in ("stats1", "stats2", "prep_stats"):
                        rstd_a(h, ln_no(r, (name, l)))
                    if name in ("q", "k", "v"):
                        c = comps[:, "qkv".index(name), :, :]
                        at, end = max(h * HT, 1), (h + 1) * HT
                        for k in range(h + 1):
                            a_ended(pool, r, k, (name, l))
                        nc.gpsimd.tensor_tensor(c[:, 1, at:end], c[:, 0, at:end], c[:, 0, at - 1:end - 1],
                                                ALU.subtract).then_inc(diffed[h], 1)

                def t_part(*t):
                    if t[0] == "statsB":
                        rstd(mvB[:, :, :], veB[:, :], rsB[:, :], lnB_mv, lnB_ve, lnB_rs, r.b)
                    if t[0] in "qk":
                        i = "qk".index(t[0])
                        pool.wait_ge(swapped[t[0]], 64 * (r.b * HP + (t[1] + 1)))
                        nc.gpsimd.tensor_tensor(rot[:, i, :], rot[:, i, :], sinT[:, :], ALU.mult).then_inc(sin_part, 1)
                    if t[0] == "rope":
                        if t[1]:
                            t_ready(pool, r, ("S", t[1] - 1, 3))
                        for i, dst in enumerate((Q, Kk)):
                            n = r.b * len(ROPE_ORDER) + (2 * t[1] + i + 1)
                            pool.wait_ge(cos_part, n)
                            pool.wait_ge(sin_part, n)
                            nc.gpsimd.tensor_tensor(dst[:, :], raw[:, i, :], rot[:, i, :], ALU.add).then_inc(roped, 1)

                def u_part(name, u):
                    pool.wait_ge(silu, r.unit + (u + 1))
                    pool.wait_ge(ge_sb, r.gel + (unit_kind(u)[4] + 1))
                    nc.gpsimd.tensor_tensor(s_h[:, :], s_h[:, :], ge[:, :], ALU.mult).then_inc(weighed, 1)

                take_turns("pool", streams(r, a_part, t_part, u_part))

            rounds(pool, one)

        @block.scalar
        def _(act):
            def copy(dst, src):
                return nc.scalar.activation(dst, src, ACT.Copy)

            for n, (dst, width, shape) in enumerate(prep_targets()):
                act.wait_ge(prep_T, n + 1)
                copy(dst, banks[n % len(banks)][:, 0:width] if shape is None else
                     banks[n % len(banks)][:, 0:width].rearrange("p (a n) -> p a n", a=shape)).then_inc(prep_c, 1)
            act.wait_ge(hp_mm, 1)
            copy(w_hp[:, :, :], bC[:, :].rearrange("p (l n) -> p l n", l=L)).then_inc(hp_c, 1)

            def prep_copy(h, ready):
                ready(act, h, "prep_T")
                copy(xn_f[:, tokens(h)], bA[h][:, 0:HT]).then_inc(a_done[h], 1)

            def prep_sig(n):
                act.wait_ge(r0_step, n)
                nc.scalar.activation(r0_sg[:, :, :], r0_top[:, :, 0:K0], ACT.Sigmoid).then_inc(r0_sig, 1)

            def prep_gates(h, ready):
                ready(act, h, "gates0_T")
                copy(gates0[:, tokens(h)], gates0_bank(h)).then_inc(a_done[h], 1)

            def prep_ready(e, h, name):
                e.wait_ge(a_full[h], PREP_FILL[name] + 1)

            for h in range(2):
                prep_copy(h, prep_ready)
            prep_sig(R0_TOP)
            for h in range(2):
                prep_gates(h, prep_ready)

            def one(r):
                def ready(e, h, name):
                    a_ready(e, r, h, (name, L - 1))

                def a_part(h, name, l):
                    m, bank = tokens(h), bA[h][:, 0:HT]
                    n = "qkv".find(name[-1])
                    if name in ("ln1_T", "ln2_T"):
                        a_ready(act, r, h, (name, l))
                        copy(xf[:, m], bank).then_inc(a_done[h], 1)
                    if name in ("q", "k", "v"):
                        if h == 0 and name == "k":
                            act.wait_ge(diffed[1], angle_no(r, l, 0) + 1)
                        a_ready(act, r, h, (name, l))
                        nc.scalar.activation(comps[:, n, 0, m], bank, ACT.Identity,
                                             bias=cols[:, AB + n, l:l + 1]).then_inc(a_done[h], 1)
                    if name in ("turn_q", "turn_k", "turn_v"):
                        a_ended(act, r, h, (name[-1], l))
                        nc.scalar.activation(comps[:, n, 3, m], comps[:, n, 0, m], ACT.Identity, bias=roundT[:, 0:1],
                                             scale=1.0 / TWO_PI).then_inc(turned[h], 1)
                    if name in ("abs_q", "abs_k", "abs_v"):
                        act.wait_ge(angled[h], 2 * angle_no(r, l, ANGLE_ORDER.index(name[-1]) + 1))
                        nc.scalar.activation(comps[:, n, 3, m], comps[:, n, 3, m], ACT.Abs).then_inc(folded_ang[h], 1)
                    if name in ("cos_q", "cos_k", "cos_v"):
                        act.wait_ge(folded_ang[h], angle_no(r, l, ANGLE_ORDER.index(name[-1]) + 1))
                        nc.scalar.activation(comps[:, n, 3, m], comps[:, n, 3, m], ACT.Sin, bias=hpi[:, 0:1],
                                             scale=-1.0).then_inc(cosined[h], 1)
                    if name in ("fc0", "fc1", "fc2", "fc3"):
                        j = int(name[2])
                        a_ready(act, r, h, (name, l))
                        nc.scalar.activation(hid[:, j, m], bank, ACT.Gelu,
                                             bias=cols[:, FB + j, l:l + 1]).then_inc(a_done[h], 1)
                    if name == "gate_T":
                        a_ready(act, r, h, (name, l))
                        copy(gate_f[:, m], bank).then_inc(a_done[h], 1)
                    if name == "prep_T":
                        prep_copy(h, ready)
                    if name == "gates0_T":
                        prep_gates(h, ready)

                def r_part(name, n):
                    prep_sig((r.a + 1) * R0_STEPS + R0_TOP)

                def t_part(*t):
                    b = t_bank(t)
                    if t[0] == "xn1_T":
                        t_ready(act, r, t)
                        copy(x1n_f[:, :], b[:, :]).then_inc(t_sem(t), 1)
                    if t[0] == "route1":
                        t_ready(act, r, t)
                        nc.scalar.activation(r1_s[:, :, :], b[:, 0:NT * E1].rearrange("p (t e) -> p t e", t=NT),
                                             ACT.Sigmoid).then_inc(t_sem(t), 1)
                    if t[0] in "qk":
                        t_ready(act, r, t)
                        act.wait_ge(roped, r.b * len(ROPE_ORDER) + max(ROPE_ORDER.index(t), 1))
                        copy(raw[:, "qk".index(t[0]), :], b[:, :]).then_inc(t_sem(t), 1)
                    if t[0] == "V":
                        t_ready(act, r, t)
                        copy(V[:, :, :, 0:DH], b[:, :].rearrange("p (w h d) -> p w h d", w=NW, h=2)).then_inc(t_sem(t), 1)
                    if t[0] == "S":
                        h = t[2] % 2
                        act.wait_ge(smax, r.b * (NW * HP) + (NW * t[1] + t[2] + 1))
                        for k in range(2):
                            w = t[2] // 2 * 2 + k
                            ins = nc.scalar.activation(probs[:, h, w, :], b[:, k * 2 * WIN:(k + 1) * 2 * WIN], ACT.Exp,
                                                       bias=nmax[:, h, w:w + 1])
                        ins.then_inc(t_sem(t), 1)
                    if t[0] == "PT":
                        t_ready(act, r, t)
                        at = P if t[2] < 2 else 0
                        copy(probsT[:, t[2] % 2, at:], b[:, at:]).then_inc(t_sem(t), 1)
                    if t[0] == "OT":
                        t_ready(act, r, t)
                        copy(OT[:, t[1] % 2, :], b[:, :]).then_inc(t_sem(t), 1)
                    if t[0] == "gates1_T":
                        t_ready(act, r, t)
                        copy(gates1[:, :], b[:, :].bitcast(bf16)[0:PARTS * E1, 0:S]).then_inc(t_sem(t), 1)

                def mixture(n, dst):
                    act.wait_ge(c_full, r.mix + (n + 1))
                    nc.scalar.activation(dst, bC[:, :], ACT.Silu).then_inc(c_done, 1)

                def u_part(name, u):
                    g = unit_kind(u)[4]
                    if name == "gate":
                        act.wait_ge(g_full, r.unit + (u + 1))
                        act.wait_ge(h_ready, r.unit + (u + 1))
                        nc.scalar.activation(s_h[:, :], bG[:, :], ACT.Silu).then_inc(silu, 1)
                    if name == "weight":
                        act.wait_ge(e_full, r.gel + (g + 1))
                        copy(ge[:, :], bU[:, :]).then_inc(ge_sb, 1)
                    if name == "down":
                        if u == UNITS0 - 1:
                            mixture(0, gate_f[:, :])
                        else:
                            mixture(1, gate1_f[:, :])

                take_turns("act", streams(r, a_part, t_part, u_part, r_part))

            rounds(act, one)

        @block.vector
        def _(dve):
            V_ = nc.vector

            def settled():
                V_.memset(scratch[:, :], 0.0)

            def stats(src, st, mv, bn_s, mv_s, n):
                for t in range(src.shape[1]):
                    ins = V_.bn_stats(st[:, t, :], src[:, t, :])
                ins.then_inc(bn_s, 1)
                dve.wait_ge(bn_s, n + 1)
                settled()
                for t in range(src.shape[1]):
                    ins = V_.bn_aggr(mv[:, t, :], st[:, t, :])
                ins.then_inc(mv_s, 1)

            def normalise(src, dst, mv, rs, mv_s, rs_s, out_s, n):
                dve.wait_ge(mv_s, n + 1)
                dve.wait_ge(rs_s, n + 1)
                for t in range(src.shape[1]):
                    ins = V_.tensor_scalar(dst[:, t, :], src[:, t, :], mv[:, t, 0:1], rs[:, t:t + 1],
                                           ALU.subtract, ALU.mult)
                ins.then_inc(out_s, 1)

            def stats_a(h, src, n):
                k = subtiles(h)
                stats(src[:, k, :], stA[:, k, :], mvA[:, k, :], lnA_bn[h], lnA_mv[h], n)

            def normalise_a(h, src, dst, n):
                k = subtiles(h)
                normalise(src[:, k, :], dst[:, k, :], mvA[:, k, :], rsA[:, k], lnA_mv[h], lnA_rs[h], lnA_out[h], n)

            def linker(s, base, start):
                n = [start]

                def link(ins, alone=False, end=False):
                    n[0] += 1
                    ins.then_inc(s, 1)
                    if not end:
                        dve.wait_ge(s, base + n[0])
                        if alone:
                            settled()
                return link

            def split(link, g, parts, done):
                for k in range(PARTS):
                    ins = V_.tensor_copy(parts[:, :, k, :], g)
                    if k == PARTS - 1:
                        ins.then_inc(done, 1)
                    else:
                        link(ins)
                        link(V_.tensor_tensor(g, g, parts[:, :, k, :], ALU.subtract))

            def route0(h, ready):
                ready(dve, h, "route0")
                V_.tensor_copy(r0_lg[:, subtiles(h), :], bA[h][:, 0:NT // 2 * E0].rearrange("p (t e) -> p t e", e=E0)
                               ).then_inc(a_done[h], 1)

            def route0_chunk(k, base, sig_n, copied):
                start = (0, 1, 4, 9)[k]
                link = linker(r0_step, base, start)
                if k == 0:
                    for h in range(2):
                        dve.wait_ge(a_done[h], copied)
                    settled()
                    for t in range(NT):
                        ins = V_.max(r0_top[:, t, :], r0_lg[:, t, :])
                    link(ins, end=True)
                    return
                dve.wait_ge(r0_step, base + start)
                if k == 1:
                    settled()
                    for t in range(NT):
                        ins = V_.max_index(r0_idx[:, t, :], r0_top[:, t, :], r0_lg[:, t, :])
                    link(ins)
                    link(V_.tensor_copy(r0_idf[:, :, :], r0_idx[:, :, :]))
                    link(V_.tensor_tensor(r0_hit[:, :, :, :], iota[:, 0:E0].unsqueeze(1).unsqueeze(1).to_broadcast([P, NT, K0, E0]),
                                          r0_idf[:, :, 0:K0].unsqueeze(3).to_broadcast([P, NT, K0, E0]), ALU.is_equal), end=True)
                if k == 2:
                    dve.wait_ge(r0_sig, sig_n)
                    link(V_.tensor_reduce(r0_sum[:, :], r0_sg[:, :, :], AX.X, ALU.add))
                    link(V_.tensor_scalar(r0_sum[:, :], r0_sum[:, :], 1e-10, None, ALU.add))
                    link(V_.reciprocal(r0_sum[:, :], r0_sum[:, :]))
                    link(V_.tensor_tensor(r0_sg[:, :, :], r0_sg[:, :, :], r0_sum[:, :].unsqueeze(2).to_broadcast([P, NT, K0]), ALU.mult))
                    link(V_.tensor_tensor(r0_hit[:, :, :, :], r0_hit[:, :, :, :],
                                          r0_sg[:, :, :].unsqueeze(3).to_broadcast([P, NT, K0, E0]), ALU.mult), end=True)
                if k == 3:
                    link(V_.tensor_tensor(r0_g[:, :, :], r0_hit[:, :, 0, :], r0_hit[:, :, 1, :], ALU.add))
                    split(link, r0_g[:, :, :], r0_parts, r0_done)

            dve.wait_ge(loaded["rows"], 2 * 16)
            steps = 0
            for k in range(PARTS):
                for at in range(k * GROUP, PARTS * GROUP, GROUP):
                    on = slice(at, at + GROUP)
                    if k:
                        dve.wait_ge(row_part, steps)
                        V_.tensor_tensor(st_rows[on], st_rows[on], rows_b[on], ALU.subtract).then_inc(row_part, 1)
                        steps += 1
                        dve.wait_ge(row_part, steps)
                    V_.tensor_copy(rows_b[on], st_rows[on]).then_inc(row_part, 1)
                    steps += 1
            dve.wait_ge(loaded["attn"], 32)
            for l in range(L):
                ins = V_.tensor_copy(w_att[:, l, :, :].rearrange("p t (h d) -> p t h d", h=H),
                                     st_att[:, l, :].rearrange("p (h t d) -> p t h d", h=H, t=3))
            ins.then_inc(w_perm, 1)
            dve.wait_ge(loaded["wqkv"], 16)
            V_.tensor_scalar(w_a1[:, 0:INNER], w_a1[:, 0:INNER], DH ** -0.5, None, ALU.mult).then_inc(folded, 1)
            dve.wait_ge(prep_c, PREP_BANKS)
            dve.wait_ge(bias_mm, 1)
            nb = L * (3 + FC)
            V_.tensor_tensor(cols[:, AB:AB + 3 + FC, :], cols[:, AB:AB + 3 + FC, :],
                             bC[:, 0:nb].rearrange("p (n l) -> p n l", l=L), ALU.add)
            for l in range(L):
                V_.tensor_scalar(w_att[:, l, :, :], w_att[:, l, :, :], cols[:, LN1W, l:l + 1], None, ALU.mult)
                ins = V_.tensor_scalar(w_fc[:, l, :], w_fc[:, l, :], cols[:, LN2W, l:l + 1], None, ALU.mult)
            ins.then_inc(folded, 1)
            dve.wait_ge(loaded["consts"], 16 * 12)
            for h in range(2):
                dve.wait_ge(x_in[h], 16)
                stats_a(h, x_ld, 0)
            for h in range(2):
                normalise_a(h, x_ld, xn, 0)

            def prep_ready(e, h, name):
                e.wait_ge(a_full[h], PREP_FILL[name] + 1)

            for h in range(2):
                route0(h, prep_ready)
            for k in range(R0_CHUNKS):
                route0_chunk(k, 0, 1, PREP_FILL["route0"] + 1)

            def angle(r, h, l, name):
                m, n, no = tokens(h), "qkv".index(name), angle_no(r, l, ANGLE_ORDER.index(name))
                dve.wait_ge(turned[h], no + 1)
                V_.tensor_scalar(comps[:, n, 3, m], comps[:, n, 3, m], ROUND, TWO_PI, ALU.subtract, ALU.mult).then_inc(angled[h], 1)
                dve.wait_ge(angled[h], 2 * no + 1)
                V_.tensor_tensor(comps[:, n, 3, m], comps[:, n, 0, m], comps[:, n, 3, m], ALU.subtract).then_inc(angled[h], 1)

            def quaternions(r, h, l, k):
                m = tokens(h)
                a, b, c = comps[:, 0, :, m], comps[:, 1, :, m], comps[:, 2, :, m]
                w, e = acc[:, :, m], tmp[:, :, m]

                def many(k, n):
                    return b[:, k:k + 1, :].to_broadcast([P, n, HT])

                def tt(n, dst, i0, i1, op):
                    if n > 1:
                        dve.wait_ge(ham[h], ham_no(r, l, n - 1))
                    V_.tensor_tensor(dst, i0, i1, op).then_inc(ham[h], 1)

                if k == 0:
                    dve.wait_ge(cosined[h], angle_no(r, l, 2))
                    dve.wait_ge(diffed[h], angle_no(r, l, 2) + h)
                    dve.wait_ge(rolled_kv[h], 32 * (r.a * (2 * L) + (2 * l + 2)))
                    tt(1, w, many(0, 4), c, ALU.mult)
                if k == 1:
                    tt(2, e, many(1, 2), c[:, 1::2, :], ALU.mult)
                if k == 2:
                    tt(3, w[:, 0::2, :], w[:, 0::2, :], e, ALU.subtract)
                if k == 3:
                    tt(4, e, many(1, 2), c[:, 0::2, :], ALU.mult)
                if k == 4:
                    tt(5, w[:, 1::2, :], w[:, 1::2, :], e, ALU.add)
                if k == 5:
                    tt(6, e, many(2, 2), c[:, 2:0:-1, :], ALU.mult)
                if k == 6:
                    tt(7, w[:, 0::3, :], w[:, 0::3, :], e, ALU.subtract)
                if k == 7:
                    tt(8, e, many(2, 2), c[:, 3::-3, :], ALU.mult)
                if k == 8:
                    tt(9, w[:, 1:3, :], w[:, 1:3, :], e, ALU.add)
                if k == 9:
                    tt(10, e, many(3, 2), c[:, 3:1:-1, :], ALU.mult)
                if k == 10:
                    tt(11, w[:, 0:2, :], w[:, 0:2, :], e, ALU.subtract)
                if k == 11:
                    tt(12, e, many(3, 2), c[:, 1::-1, :], ALU.mult)
                if k == 12:
                    tt(13, w[:, 2:4, :], w[:, 2:4, :], e, ALU.add)
                if k == 13:
                    dve.wait_ge(cosined[h], angle_no(r, l, 3))
                    dve.wait_ge(diffed[h], angle_no(r, l, 3) + h)
                    dve.wait_ge(rolled_q[h], 32 * (r.a * L + (l + 1)))
                    tt(14, w, a, w, ALU.mult)
                if k == 14:
                    tt(15, e[:, 0, :], w[:, 0, :], w[:, 1, :], ALU.subtract)
                    tt(16, e[:, 1, :], w[:, 2, :], w[:, 3, :], ALU.add)
                    tt(17, z[:, m], e[:, 0, :], e[:, 1, :], ALU.subtract)

            def route1_chunk(k, r):
                start = (0, 2, 9, 12, 17, 23)[k]
                link = linker(r1_step, r.b * R1_STEPS, start)
                if k == 0:
                    t_ended(dve, r, ("route1",))
                    link(V_.tensor_tensor(r1_c[:, :, :], r1_s[:, :, :], rbias[:, :].unsqueeze(1).to_broadcast([P, NT, E1]), ALU.add), True)
                    for t in range(NT):
                        for g in range(GROUPS):
                            ins = V_.max(r1_m8[:, t, g, :], r1_c[:, t, g * EG:(g + 1) * EG])
                    link(ins, end=True)
                    return
                dve.wait_ge(r1_step, r.b * R1_STEPS + start)
                if k == 1:
                    link(V_.tensor_tensor(r1_gs[:, :, :], r1_m8[:, :, :, 0], r1_m8[:, :, :, 1], ALU.add))
                    other = r1_gs[:, :, :].unsqueeze(2).to_broadcast([P, NT, GROUPS, GROUPS])
                    mine = r1_gs[:, :, :].unsqueeze(3).to_broadcast([P, NT, GROUPS, GROUPS])
                    link(V_.tensor_tensor(r1_gt[:, :, :, :], other, mine, ALU.is_gt))
                    link(V_.tensor_tensor(r1_eq[:, :, :, :], other, mine, ALU.is_equal))
                    link(V_.tensor_tensor(r1_eq[:, :, :, :], r1_eq[:, :, :, :],
                                          ltri[:, :, :].unsqueeze(1).to_broadcast([P, NT, GROUPS, GROUPS]), ALU.mult))
                    link(V_.tensor_tensor(r1_gt[:, :, :, :], r1_gt[:, :, :, :], r1_eq[:, :, :, :], ALU.add))
                    link(V_.tensor_reduce(r1_gs[:, :, :], r1_gt[:, :, :, :], AX.X, ALU.add))
                    link(V_.tensor_scalar(r1_gs[:, :, :], r1_gs[:, :, :], float(TOPG), None, ALU.is_lt), end=True)
                if k == 2:
                    by_group = r1_c[:, :, :].rearrange("p t (g e) -> p t g e", g=GROUPS)
                    link(V_.tensor_tensor(by_group, by_group, r1_gs[:, :, :].unsqueeze(3).to_broadcast([P, NT, GROUPS, EG]), ALU.mult))
                    link(V_.tensor_scalar(r1_c[:, :, :], r1_c[:, :, :], 0.0, None, ALU.add), True)
                    for t in range(NT):
                        ins = V_.max(r1_top[:, t, :], r1_c[:, t, :])
                    link(ins, end=True)
                if k == 3:
                    settled()
                    for t in range(NT):
                        ins = V_.max_index(r1_idx[:, t, :], r1_top[:, t, :], r1_c[:, t, :])
                    link(ins)
                    link(V_.tensor_copy(r1_idf[:, :, :], r1_idx[:, :, :]))
                    link(V_.tensor_tensor(r1_hit, iota[:, :].unsqueeze(1).unsqueeze(1).to_broadcast([P, NT, TOPK1, E1]),
                                          r1_idf[:, :, 0:TOPK1].unsqueeze(3).to_broadcast([P, NT, TOPK1, E1]), ALU.is_equal))
                    link(V_.tensor_tensor(r1_hit[:, :, 0:2, :], r1_hit[:, :, 0:2, :], r1_hit[:, :, 2:4, :], ALU.add))
                    link(V_.tensor_tensor(r1_c[:, :, :], r1_hit[:, :, 0, :], r1_hit[:, :, 1, :], ALU.add), end=True)
                if k == 4:
                    link(V_.tensor_tensor(r1_s[:, :, :], r1_s[:, :, :], r1_c[:, :, :], ALU.mult))
                    link(V_.tensor_reduce(r1_sum[:, :], r1_s[:, :, :], AX.X, ALU.add))
                    link(V_.tensor_scalar(r1_sum[:, :], r1_sum[:, :], 1e-20, None, ALU.add))
                    link(V_.reciprocal(r1_sum[:, :], r1_sum[:, :]))
                    link(V_.tensor_scalar(r1_sum[:, :], r1_sum[:, :], SCALE1, None, ALU.mult))
                    link(V_.tensor_tensor(r1_s[:, :, :], r1_s[:, :, :], r1_sum[:, :].unsqueeze(2).to_broadcast([P, NT, E1]), ALU.mult), end=True)
                if k == 5:
                    split(link, r1_s[:, :, :], r1_parts, r1_done)

            def one(r):
                def a_part(h, name, l):
                    m, k = tokens(h), subtiles(h)
                    if name in ("stats1", "stats2", "prep_stats"):
                        if name == "prep_stats":
                            dve.wait_ge(x_in[h], r.a * 32 + 32)
                        src = x_ld if name == "prep_stats" else xn if name == "stats1" and l == 0 else xr
                        if src is xr:
                            a_ended(dve, r, h, ("proj", l) if name == "stats2" else ("mproj", l - 1))
                        stats_a(h, src, ln_no(r, (name, l)))
                    if name in ("norm1", "norm2"):
                        normalise_a(h, xn if name == "norm1" and l == 0 else xr, ln_hat, ln_no(r, ("stats" + name[-1], l)))
                    if name == "prep_norm":
                        normalise_a(h, x_ld, xn, ln_no(r, ("prep_stats", l)))
                    if name == "route0":
                        route0(h, lambda e, h, n: a_ready(e, r, h, (n, L - 1)))
                    if name in ("ang_k", "ang_v", "ang_q"):
                        angle(r, h, l, name[-1])
                    if name in HAM_NAMES:
                        quaternions(r, h, l, int(name[3:]))
                    if name == "hart":
                        a_ready(dve, r, h, (name, l))
                        V_.tensor_tensor(zc[:, m], bA[h][:, 0:HT], cmod[:, m], ALU.mult).then_inc(a_done[h], 1)
                    if name in ("proj", "mproj"):
                        a_ready(dve, r, h, (name, l))
                        src = xn if name == "proj" and l == 0 else xr
                        V_.tensor_tensor(xr[:, k, :], bA[h][:, 0:HT].rearrange("p (t d) -> p t d", d=D), src[:, k, :],
                                         ALU.add).then_inc(a_done[h], 1)
                    if name == "join":
                        a_ended(dve, r, h, ("gate_T", L - 2))
                        a_ended(dve, r, h, ("mproj", L - 1))
                        if r.b is not None:
                            t_ended(dve, r, ("final_T",))
                        V_.tensor_tensor(xmul[:, k, :], gate_f[:, m].rearrange("p (t d) -> p t d", d=D), xr[:, k, :],
                                         ALU.mult).then_inc(joined[h], 1)
                        dve.wait_ge(joined[h], r.a + 1)
                        dve.wait_ge(x_in[h], r.a * 32 + 48)
                        V_.tensor_tensor(x1[:, k, :], xmul[:, k, :], x_ld[:, k, :], ALU.add).then_inc(x1_ready, 1)

                def t_part(*t):
                    if t[0] == "statsB":
                        dve.wait_ge(x1_ready, 2 * (r.b + 1))
                        stats(x1[:, :, :], stB[:, :, :], mvB[:, :, :], lnB_bn, lnB_mv, r.b)
                    if t[0] == "normB":
                        normalise(x1[:, :, :], x1n, mvB[:, :, :], rsB[:, :], lnB_mv, lnB_rs, lnB_out, r.b)
                    b = t_bank(t) if t in STEP_AT else None
                    if t[0] == "rope":
                        for i, name in enumerate("qk"):
                            dve.wait_ge(swapped[name], 64 * (r.b * HP + (t[1] + 1)))
                            V_.tensor_tensor(raw[:, i, :], raw[:, i, :], cosT[:, :], ALU.mult).then_inc(cos_part, 1)
                    if t[0] == "S":
                        t_ready(dve, r, t)
                        w, h = t[2] // 2 * 2, t[2] % 2
                        V_.tensor_reduce(nmax[:, h, w:w + 2], b[:, :].rearrange("p (w n) -> p w n", w=2), AX.X, ALU.max,
                                         negate=True).then_inc(smax, 1)
                    if t[0] == "O":
                        n = 2 * t[1] + t[2] + 1
                        w = range(2 * t[2], 2 * t[2] + 2)
                        if (t[1], t[2]) == (0, 0):
                            dve.wait_ge(stored, r.b * 16 + 16)
                        t_ready(dve, r, t)
                        out4 = b[:, 0:4 * (DH + 1)].rearrange("p (w h d) -> p w h d", w=2, h=2)
                        V_.reciprocal(rinv[:, :, :], out4[:, :, :, DH]).then_inc(rinved, 1)
                        dve.wait_ge(rinved, r.b * (2 * HP) + n)
                        V_.tensor_tensor(O[:, w[0]:w[0] + 2, :].rearrange("p w (h d) -> p w h d", h=2), out4[:, :, :, 0:DH],
                                         rinv[:, :, :].unsqueeze(3).to_broadcast([P, 2, 2, DH]),
                                         ALU.mult).then_inc(t_sem(t), 1)
                    if t[0] == "out":
                        l = t[1]
                        t_ready(dve, r, t)
                        if l == 0:
                            V_.tensor_copy(y[:, :], b[:, :]).then_inc(t_sem(t), 1)
                        else:
                            t_ended(dve, r, ("out", l - 1))
                            V_.tensor_tensor(y[:, :], b[:, :], y[:, :], ALU.add).then_inc(t_sem(t), 1)

                    if t[0] == "gated":
                        dve.wait_ge(c_done, r.mix + 2)
                        t_ended(dve, r, ("out", L - 1))
                        V_.tensor_tensor(y[:, :], y[:, :], gate1_f[:, :], ALU.mult).then_inc(y_gated, 1)
                    if t[0] == "final_T":
                        t_ready(dve, r, t)
                        V_.tensor_tensor(y_out[:, :, :], b[:, :].rearrange("p (t d) -> p t d", t=NT),
                                         x1[:, :, :], ALU.add).then_inc(t_sem(t), 1)

                def u_part(name, u):
                    dve.wait_ge(u_full, r.unit + (u + 1))
                    if has_weight(u):
                        dve.wait_ge(weighed, r.wei + (u + 1))
                    else:
                        dve.wait_ge(silu, r.unit + (u + 1))
                    V_.tensor_tensor(hu[:, :], bU[:, :], s_h[:, :], ALU.mult).then_inc(h_ready, 1)

                def r_part(name, k):
                    if name == "r1":
                        route1_chunk(k, r)
                    else:
                        route0_chunk(k, (r.a + 1) * R0_STEPS, r.a + 2, fill_no(r, ("route0", L - 1)) + 1)

                take_turns("dve", streams(r, a_part, t_part, u_part, r_part))

            rounds(dve, one)

        @block.tensor
        def _(pe):
            mm = nc.tensor.matmul

            def transpose(dst, src):
                k = src.shape[0]
                return nc.tensor.transpose(dst, src, ident[0:k, 0:k])

            def transpose_b(dst, src):
                return nc.tensor.transpose(dst, src, identb[:, :])

            def transposes(bank, tiles):
                for n, src in enumerate(tiles):
                    ins = transpose(bank[:, n * P:(n + 1) * P], src)
                return ins

            def projection(bank, tile_nos, xs, ws, row):
                for n, t in enumerate(tile_nos):
                    dst = bank[:, n * P:(n + 1) * P]
                    for k, w in enumerate(ws):
                        mm(dst, xs[k][:, t * P:(t + 1) * P], w, start=k == 0, stop=False)
                    ins = mm(dst, share[:, :], row, start=False, stop=True)
                return ins

            for n, tiles in enumerate(prep_sources()):
                if n == 0:
                    pe.wait_ge(loaded["small"], 13 * 16)
                if n == 2:
                    pe.wait_ge(loaded["gates"], 6 * 16)
                if n >= len(banks):
                    pe.wait_ge(prep_c, n - len(banks) + 1)
                at = 0
                for src in tiles:
                    k = src.shape[0]
                    ins = transpose(banks[n % len(banks)][:, at:at + k], src)
                    at += k
                ins.then_inc(prep_T, 1)
            pe.wait_ge(w_perm, 1)
            pe.wait_ge(prep_c, 1)
            for n in range(3 + FC):
                for l in range(L):
                    w = w_att[:, l, n, :] if n < 3 else w_fc[:, l, (n - 3) * D:(n - 2) * D]
                    b = LN1B if n < 3 else LN2B
                    ins = mm(bC[:, n * L + l:n * L + l + 1], w, cols[:, b, l:l + 1], start=True, stop=True)
            ins.then_inc(bias_mm, 1)
            pe.wait_ge(folded, 2)
            for l in range(L):
                ins = mm(bC[:, l * D:(l + 1) * D], hart_w[:, :], st_pw[:, l, :], start=True, stop=True)
            ins.then_inc(hp_mm, 1)
            pe.wait_ge(hp_c, 1)
            pe.wait_ge(prep_c, PREP_BANKS)
            pe.wait_ge(loaded["experts0"], 3 * 16)
            pe.wait_ge(row_part, 2 * PARTS + PARTS)
            pe.wait_ge(loaded["consts"], 12 * 16)

            def prep_step(h, name, before, out_n, done_n):
                k = range(NT)[subtiles(h)]
                pe.wait_ge(a_done[h], before)
                if name == "prep_T":
                    pe.wait_ge(lnA_out[h], out_n)
                    return transposes(bA[h], [xn[:, t, :] for t in k])
                if name == "route0":
                    for n, t in enumerate(k):
                        ins = mm(bA[h][:, n * E0:(n + 1) * E0], xn_f[:, t * P:(t + 1) * P], w_r0,
                                 start=True, stop=True)
                    return ins
                pe.wait_ge(r0_done, done_n)
                for n, t in enumerate(k):
                    ins = transpose_b(gates0_bank(h)[:, n * P:(n + 1) * P],
                                      r0_parts[:, t, :, :].rearrange("p k e -> p (k e)"))
                return ins

            for n, name in enumerate(PREP):
                for h in range(2):
                    prep_step(h, name, n, 1, 1).then_inc(a_full[h], 1)

            def one(r):
                def fill(h, name, l):
                    pe.wait_ge(a_done[h], fill_no(r, (name, l)))

                def a_part(h, name, l):
                    m, tile_nos, bank = tokens(h), range(NT)[subtiles(h)], bA[h][:, 0:HT]
                    if name == "prep_T":
                        pe.wait_ge(h_ready, r.unit + (UNITS0 + 1))
                    if name in PREP:
                        ins = prep_step(h, name, fill_no(r, (name, l)), ln_no(r, ("prep_stats", l)) + 1, r.a + 2)
                    else:
                        if name == "hart":
                            pe.wait_ge(ham[h], ham_no(r, l, HAM_OPS))
                        if name in ("ln1_T", "ln2_T"):
                            pe.wait_ge(lnA_out[h], ln_no(r, ("stats" + name[2], l)) + 1)
                        if name == "gate_T":
                            pe.wait_ge(c_done, r.mix + 1)
                        fill(h, name, l)
                    if name in ("ln1_T", "ln2_T"):
                        ins = transposes(bank, [ln_hat[:, t, :] for t in tile_nos])
                    if name in ("q", "k", "v"):
                        ins = mm(bank, w_att[:, l, "qkv".index(name), :], xf[:, m], start=True, stop=True)
                    if name == "hart":
                        ins = mm(bank, hart_w[:, :], z[:, m], start=True, stop=True)
                    if name == "proj":
                        ins = projection(bank, tile_nos, [zc], [w_hp[:, l, :]], rows_b[:, 0, l, :])
                    if name == "gate_T":
                        ins = transposes(bank, [gate_f[:, t * P:(t + 1) * P] for t in tile_nos])
                    if name in ("fc0", "fc1", "fc2", "fc3"):
                        j = int(name[2])
                        ins = mm(bank, w_fc[:, l, j * D:(j + 1) * D], xf[:, m], start=True, stop=True)
                    if name == "mproj":
                        ins = projection(bank, tile_nos, [hid[:, j, :] for j in range(FC)],
                                         [w_mp[:, l, j, :] for j in range(FC)], rows_b[:, 1, l, :])
                    ins.then_inc(a_full[h], 1)

                def t_part(*t):
                    b = t_bank(t)
                    builds_on = {"route1": [("xn1_T",)], "PT": [("S",) + t[1:]],
                                 "O": [("V",) + t[1:2]] + [("PT", t[1], 2 * t[-1] + k) for k in range(2)] if t[0] == "O" else [],
                                 "OT": [("O",) + t[1:] + (k,) for k in range(2)],
                                 "out": [("OT", 2 * t[-1] + k) for k in range(2)] if t[0] == "out" else []}
                    if t == ("q", 0):
                        builds_on["q"] = [("xn1_T",)]
                    t_begin(pe, r, t, *builds_on.get(t[0], []))
                    if t[0] == "xn1_T":
                        pe.wait_ge(lnB_out, r.b + 1)
                        ins = transposes(b, [x1n[:, k, :] for k in range(NT)])
                    if t[0] == "route1":
                        for k in range(NT):
                            ins = mm(b[:, k * E1:(k + 1) * E1], x1n_f[:, k * P:(k + 1) * P], w_r1, start=True, stop=True)
                    if t[0] in "qk":
                        c = t[1] * P + (0 if t[0] == "q" else INNER)
                        ins = mm(b[:, :], w_a1[:, c:c + P], x1n_f[:, :], start=True, stop=True)
                    if t[0] == "V":
                        c = t[1] * P + 2 * INNER
                        for w in range(NW):
                            ins = mm(b[:, w * P:(w + 1) * P], x1n_f[:, w * WIN:(w + 1) * WIN], w_a1[:, c:c + P],
                                     start=True, stop=True)
                    if t[0] == "S":
                        first_w, h = t[2] // 2 * 2, t[2] % 2
                        f = slice(h * DH, (h + 1) * DH)
                        if t[2] == 0:
                            pe.wait_ge(roped, r.b * len(ROPE_ORDER) + (ROPE_ORDER.index(("k", t[1])) + 2))
                        mm(b[:, :], identb[:, :], maskb[:, first_w * WIN:first_w * WIN + S], start=True, stop=False)
                        for k in range(2):
                            w = first_w + k
                            n = min(w, 1) + 1
                            ins = mm(b[:, ((k + 1) * 2 - n) * WIN:(k + 1) * 2 * WIN], Q[f, w * WIN:(w + 1) * WIN],
                                     Kk[f, (w + 1 - n) * WIN:(w + 1) * WIN], start=False, stop=k == 1)
                    if t[0] == "PT":
                        first_w, h = t[2] // 2 * 2, t[2] % 2
                        skip = 0 if first_w else 1
                        tiles = [probs[:, h, first_w + w, k * P:(k + 1) * P] for w in range(2) for k in range(2)]
                        ins = transposes(b[:, skip * P:], tiles[skip:])
                    if t[0] == "O":
                        for w in range(2):
                            for h in range(2):
                                keys = (0, 1) if t[2] or w else (1,)
                                for k in keys:
                                    ins = mm(b[:, (2 * w + h) * (DH + 1):(2 * w + h + 1) * (DH + 1)],
                                             probsT[:, h, (2 * w + k) * P:(2 * w + k + 1) * P],
                                             V[:, 2 * t[2] + w + k - 1, h, :], start=k == keys[0], stop=k == 1)
                    if t[0] == "OT":
                        ins = transposes(b, [O[:, w, :] for w in range(NW)])
                    if t[0] == "gates1_T":
                        pe.wait_ge(r1_done, r.b + 1)
                        bank = b[:, :].bitcast(bf16)
                        for k in range(NT):
                            ins = transpose_b(bank[0:PARTS * E1, k * P:(k + 1) * P],
                                              r1_parts[:, k, :, :].rearrange("p k e -> p (k e)"))
                    if t[0] == "out":
                        for k in range(2):
                            ins = mm(b[:, :], w_o1[:, 2 * t[1] + k, :], OT[:, k, :], start=k == 0, stop=k == 1)
                    if t[0] == "final_T":
                        pe.wait_ge(y_gated, r.b + 1)
                        ins = transposes(b, [y[:, k * P:(k + 1) * P] for k in range(NT)])
                    ins.then_inc(t_full, 1)

                def u_part(name, u):
                    g, up, down, sel, e = unit_kind(u)
                    src, gates = (xn_f, gates0) if u < UNITS0 else (x1n_f, gates1)
                    begins = u == units_of(r)[0]
                    if name == "gate":
                        if u == 0:
                            for h in range(2):
                                pe.wait_ge(a_done[h], gates0_no(r))
                        if u == UNITS0:
                            t_ended(pe, r, ("gates1_T",))
                        if not begins:
                            pe.wait_ge(silu, r.unit + u)
                        mm(bG[:, :], g, src[:, :], start=True, stop=True).then_inc(g_full, 1)
                    if name == "weight":
                        pe.wait_ge(h_ready, r.unit + (u + 1))
                        mm(bU[:, :], sel, gates[:, :], start=True, stop=True).then_inc(e_full, 1)
                    if name == "up":
                        if sel is not None:
                            pe.wait_ge(ge_sb, r.gel + (e + 1))
                        mm(bU[:, :], up, src[:, :], start=True, stop=True).then_inc(u_full, 1)
                    if name == "down":
                        if u == UNITS0:
                            pe.wait_ge(c_done, r.mix + 1)
                        if u == 0 and r is not first:
                            pe.wait_ge(c_done, r.mix)
                        pe.wait_ge(h_ready, r.unit + (u + 2))
                        ins = mm(bC[:, :], down, hu[:, :], start=u in (0, UNITS0), stop=u in (UNITS0 - 1, UNITS - 1))
                        if u in (UNITS0 - 1, UNITS - 1):
                            ins.then_inc(c_full, 1)

                take_turns("pe", streams(r, a_part, t_part, u_part))

            rounds(pe, one)


def hartley():
    h, d = np.divmod(np.arange(D), HD)
    turns = (np.outer(h, h) % H) / H + (np.outer(d, d) % HD) / HD
    return ((np.cos(2 * np.pi * turns) + np.sin(2 * np.pi * turns)) / np.sqrt(D)).astype(np.float32)


def filter_modulation():
    h, d = np.divmod(np.arange(D), HD)
    ks, kh, kd = np.fft.fftfreq(S)[None, :], np.fft.fftfreq(H)[h][:, None], np.fft.fftfreq(HD)[d][:, None]
    km = np.sqrt(ks ** 2 + kh ** 2 + kd ** 2 + 1e-10)
    real = np.cos(np.arctan(np.log(km + 1e-10)))
    lam, t = np.arange(S) / S, np.arange(S) * 0.1
    mod = np.sin(t + lam) * np.cos(t - 2.0 * lam + 0.5 * lam ** 2)
    return (real * (1.0 + 0.1 * mod)[None, :]).astype(np.float32)


def rotary():
    d = np.arange(P) % DH
    ang = (10000.0 ** -(2.0 * (d % (DH // 2)) / DH))[:, None] * np.arange(S)[None, :]
    return np.cos(ang).astype(np.float32), (np.sin(ang) * np.where(d < DH // 2, -1, 1)[:, None]).astype(np.float32)


def masks(dtype):
    i, j = np.arange(WIN)[:, None], np.arange(WIN)[None, :]
    here, before = np.where(j <= i, 0.0, MASKED), np.where(j >= i, 0.0, MASKED)
    return np.concatenate([np.full((WIN, WIN), MASKED), here, before, here, before, here], 1).astype(dtype)


def selectors(dtype):
    e0 = np.arange(PARTS * E0) % E0
    s0 = np.broadcast_to((e0[:, None] == np.arange(E0)[None, :])[:, :, None], (PARTS * E0, E0, P))
    e1 = np.arange(PARTS * E1) % E1
    s1 = e1[:, None, None] == (2 * np.arange(PAIR1)[:, None] + np.arange(P)[None, :] // I1)[None, :, :]
    return s0.astype(dtype), s1.astype(dtype)


_INS = ["L0_attn_x", "L0_attn_ln1_w", "L0_attn_ln1_b", "L0_attn_attn_w", "L0_attn_attn_b", "L0_attn_aproj_w",
        "L0_attn_aproj_b", "L0_attn_ln2_w", "L0_attn_ln2_b", "L0_attn_fc_w", "L0_attn_fc_b", "L0_attn_mproj_w",
        "L0_attn_mproj_b", "L0_ffn_router_w", "L0_ffn_w_gate", "L0_ffn_w_up", "L0_ffn_w_down", "L1_attn_W_qkv",
        "L1_attn_W_out", "L1_ffn_router_weight", "L1_ffn_router_bias", "L1_ffn_gate_w", "L1_ffn_up_w",
        "L1_ffn_down_w", "L1_ffn_shared_gate_w", "L1_ffn_shared_up_w", "L1_ffn_shared_down_w"]


def kernel(**inputs):
    import concourse.bacc as bacc
    from concourse.bass_utils import run_bass_kernel_spmd

    bf = mybir.dt.np(mybir.dt.bfloat16)
    nc = bacc.Bacc("TRN2", target_bir_lowering=False, num_devices=1)
    arrays = {name: np.ascontiguousarray(inputs[name]) for name in _INS}
    cos, sin = rotary()
    sel0, sel1 = selectors(bf)
    consts = {
        "c_ident": np.eye(P, dtype=np.float32), "c_identb": np.eye(P).astype(bf), "c_hart": hartley(),
        "c_cmod": filter_modulation(), "c_cos": cos, "c_sin": sin, "c_mask": masks(bf), "c_sel0": sel0, "c_sel1": sel1,
        "c_iota": np.broadcast_to(np.arange(E1, dtype=np.float32), (P, E1)),
        "c_ltri": np.broadcast_to(np.tril(np.ones((GROUPS, GROUPS), np.float32), -1), (P, GROUPS, GROUPS)),
    }
    arrays.update({n: np.ascontiguousarray(a) for n, a in consts.items()})
    args = [nc.dram_tensor("in_" + n, a.shape, mybir.dt.from_np(a.dtype), kind="ExternalInput").ap()
            for n, a in arrays.items()]
    out = nc.dram_tensor("out", (NB, S, D), mybir.dt.float32, kind="ExternalOutput").ap()
    program(nc, *args, out)
    r = run_bass_kernel_spmd(nc, [{"in_" + n: a for n, a in arrays.items()}], core_ids=[0])
    return r.results[0]["out"]
```
